# Optimizing a Trainium2 kernel written in Bass

```python
import numpy as np
import jax
import jax.numpy as jnp

def _softmax(x, axis=-1):
    return jax.nn.softmax(x, axis=axis)

def _gelu(x):
    return jax.nn.gelu(x, approximate=True)

def _silu(x):
    return jax.nn.silu(x)

def _sigmoid(x):
    return jax.nn.sigmoid(x)

def _layernorm(x, axis=-1, eps=1e-05):
    m = jnp.mean(x, axis=axis, keepdims=True)
    v = jnp.var(x, axis=axis, keepdims=True)
    return (x - m) / jnp.sqrt(v + eps)

def _scatter_add(tgt, idx, src, axis=0):
    return tgt.at[idx].add(src)

def _segment_sum(src, seg, n):
    return jax.ops.segment_sum(src, seg, n)
kernel_name = 'mk_gnn_preln_d4_gnn_r32_31e075'

def setup_inputs(seed: int=0):
    np.random.seed(seed)
    _w = jnp.asarray

    def _rec_inputs():
        import jax
        import jax.numpy as jnp
        _gk = jax.random.key(seed)
        x = -0.0003713 + 1 * jax.random.normal(jax.random.fold_in(_gk, 1), (3125, 128), jnp.float32)
        src = jax.random.randint(jax.random.fold_in(_gk, 2), (50000,), 0, 3125, jnp.int32)
        dst = jax.random.randint(jax.random.fold_in(_gk, 3), (50000,), 0, 3125, jnp.int32)
        _o = jnp.argsort(dst, stable=True)
        src = src[_o]
        dst = dst[_o]
        return (x, src, dst)
    x, src, dst = _rec_inputs()

    def _L0_gnn_setup():
        import jax, jax.numpy as jnp
        import numpy as np
        NUM_NODES = 3125
        NUM_EDGES = 50000
        D = 128
        key = jax.random.key(seed)
        k1, k2, k3, k4 = jax.random.split(key, 4)
        x = jax.random.normal(k1, (NUM_NODES, D), dtype=jnp.float32)
        W_lin = jax.random.normal(k2, (D, D), dtype=jnp.float32) * (1.0 / np.sqrt(D))
        W_agg = jax.random.normal(k3, (D, D), dtype=jnp.float32) * (1.0 / np.sqrt(D))
        edge_index = jax.random.randint(k4, (2, NUM_EDGES), 0, NUM_NODES, dtype=jnp.int64)
        return {'x': x, 'W_lin': W_lin, 'W_agg': W_agg, 'edge_index': edge_index}
    _L0_gnn_all = _L0_gnn_setup()
    _L0_gnn_in = {k: v for k, v in _L0_gnn_all.items() if k in ('W_lin', 'W_agg')}
    del _L0_gnn_all

    def _L1_gnn_setup():
        import jax, jax.numpy as jnp
        import numpy as np
        N, E = (50000, 18750)
        IN, H, M, OUT = (128, 256, 256, 128)

        def _sage(x, src, dst, W_l, b_l, W_r, n):
            agg = jax.ops.segment_sum(x[src], dst, num_segments=n)
            deg = jax.ops.segment_sum(jnp.ones((src.shape[0],), x.dtype), dst, num_segments=n)
            agg = agg / jnp.maximum(deg, 1.0)[:, None]
            return agg @ W_l.T + b_l + x @ W_r.T
        key = jax.random.key(seed)
        ks = jax.random.split(key, 20)

        def lin(k, o, i):
            s = 1.0 / np.sqrt(i)
            return jax.random.normal(k, (o, i), jnp.float32) * s
        inp = {'x': jax.random.normal(ks[0], (N, IN), jnp.float32), 'edge_index': jax.random.randint(ks[1], (2, E), 0, N, jnp.int64), 'W_l1': lin(ks[2], H, IN), 'b_l1': jnp.zeros((H,), jnp.float32), 'W_r1': lin(ks[3], H, IN), 'W_l2': lin(ks[4], H, H), 'b_l2': jnp.zeros((H,), jnp.float32), 'W_r2': lin(ks[5], H, H), 'res1_W': lin(ks[6], H, IN), 'res1_b': jnp.zeros((H,), jnp.float32), 'res2_W': lin(ks[7], H, IN), 'res2_b': jnp.zeros((H,), jnp.float32), 'fc1_W': lin(ks[8], M, H), 'fc1_b': jnp.zeros((M,), jnp.float32), 'fc2_W': lin(ks[9], M, M), 'fc2_b': jnp.zeros((M,), jnp.float32), 'fc3_W': lin(ks[10], OUT, M), 'fc3_b': jnp.zeros((OUT,), jnp.float32)}
        return inp
    _L1_gnn_all = _L1_gnn_setup()
    _L1_gnn_in = {k: v for k, v in _L1_gnn_all.items() if k in ('W_l1', 'b_l1', 'W_r1', 'W_l2', 'b_l2', 'W_r2', 'res1_W', 'res1_b', 'res2_W', 'res2_b', 'fc1_W', 'fc1_b', 'fc2_W', 'fc2_b', 'fc3_W', 'fc3_b')}
    del _L1_gnn_all

    def _L2_gnn_setup():
        import jax, jax.numpy as jnp
        import numpy as np
        N = 10000
        E = 20000
        D_IN = 128
        D_OUT = 128
        key = jax.random.key(seed)
        k1, k2, k3, k4, k5, k6, k7 = jax.random.split(key, 7)
        x = jax.random.normal(k1, (N, D_IN), dtype=jnp.float32)
        edge_index = jax.random.randint(k2, (2, E), 0, N, dtype=jnp.int64)
        s = 1.0 / np.sqrt(D_IN)
        W_self = jax.random.uniform(k3, (D_OUT, D_IN), minval=-s, maxval=s, dtype=jnp.float32)
        b_self = jax.random.uniform(k4, (D_OUT,), minval=-s, maxval=s, dtype=jnp.float32)
        W_nei = jax.random.uniform(k5, (D_OUT, D_IN), minval=-s, maxval=s, dtype=jnp.float32)
        b_nei = jax.random.uniform(k6, (D_OUT,), minval=-s, maxval=s, dtype=jnp.float32)
        return {'x': x, 'edge_index': edge_index, 'W_self': W_self, 'b_self': b_self, 'W_nei': W_nei, 'b_nei': b_nei}
    _L2_gnn_all = _L2_gnn_setup()
    _L2_gnn_in = {k: v for k, v in _L2_gnn_all.items() if k in ('W_self', 'b_self', 'W_nei', 'b_nei')}
    del _L2_gnn_all

    def _L3_gnn_setup():
        import jax, jax.numpy as jnp
        import numpy as np
        N = 3125
        E = 50000
        IN_DIM = 128
        OUT_DIM = 128
        H = 4
        HD = OUT_DIM // H
        NEG_SLOPE = 0.2
        EPS_SOFTMAX = 1e-08
        EPS_LN = 1e-05

        def _attention_aggregate(h_proj, sender, receiver, attn_vec, num_nodes):
            h_sender = h_proj[sender]
            h_receiver = h_proj[receiver]
            e = jnp.einsum('ehd,hd->eh', h_sender, attn_vec[:, :HD]) + jnp.einsum('ehd,hd->eh', h_receiver, attn_vec[:, HD:])
            e = jax.nn.leaky_relu(e, NEG_SLOPE)
            e_max = jax.ops.segment_max(e, receiver, num_segments=num_nodes)
            alpha = jnp.exp(e - e_max[receiver])
            alpha_sum = jax.ops.segment_sum(alpha, receiver, num_segments=num_nodes)
            alpha = alpha / (alpha_sum[receiver] + EPS_SOFTMAX)
            msg = h_sender * alpha[..., None]
            return jax.ops.segment_sum(msg, receiver, num_segments=num_nodes)
        key = jax.random.key(seed)
        ks = jax.random.split(key, 6)
        h = jax.random.normal(ks[0], (N, IN_DIM), dtype=jnp.float32)
        edge_index = jax.random.randint(ks[1], (2, E), 0, N, dtype=jnp.int32)
        W = jax.random.normal(ks[2], (IN_DIM, OUT_DIM), dtype=jnp.float32) / np.sqrt(IN_DIM)
        W_self = jax.random.normal(ks[3], (IN_DIM, OUT_DIM), dtype=jnp.float32) / np.sqrt(IN_DIM)
        a_in = jax.random.normal(ks[4], (H, 2 * HD), dtype=jnp.float32) * 0.01
        a_out = jax.random.normal(ks[5], (H, 2 * HD), dtype=jnp.float32) * 0.01
        bias = jnp.zeros((OUT_DIM,), dtype=jnp.float32)
        ln_gamma = jnp.ones((OUT_DIM,), dtype=jnp.float32)
        ln_beta = jnp.zeros((OUT_DIM,), dtype=jnp.float32)
        return {'h': h, 'edge_index': edge_index, 'W': W, 'W_self': W_self, 'a_in': a_in, 'a_out': a_out, 'bias': bias, 'ln_gamma': ln_gamma, 'ln_beta': ln_beta}
    _L3_gnn_all = _L3_gnn_setup()
    _L3_gnn_in = {k: v for k, v in _L3_gnn_all.items() if k in ('W', 'W_self', 'a_in', 'a_out', 'bias', 'ln_gamma', 'ln_beta')}
    del _L3_gnn_all
    return {'x': x, 'src': src, 'dst': dst, 'L0_gnn_W_lin': _L0_gnn_in['W_lin'], 'L0_gnn_W_agg': _L0_gnn_in['W_agg'], 'L1_gnn_W_l1': _L1_gnn_in['W_l1'], 'L1_gnn_b_l1': _L1_gnn_in['b_l1'], 'L1_gnn_W_r1': _L1_gnn_in['W_r1'], 'L1_gnn_W_l2': _L1_gnn_in['W_l2'], 'L1_gnn_b_l2': _L1_gnn_in['b_l2'], 'L1_gnn_W_r2': _L1_gnn_in['W_r2'], 'L1_gnn_res1_W': _L1_gnn_in['res1_W'], 'L1_gnn_res1_b': _L1_gnn_in['res1_b'], 'L1_gnn_res2_W': _L1_gnn_in['res2_W'], 'L1_gnn_res2_b': _L1_gnn_in['res2_b'], 'L1_gnn_fc1_W': _L1_gnn_in['fc1_W'], 'L1_gnn_fc1_b': _L1_gnn_in['fc1_b'], 'L1_gnn_fc2_W': _L1_gnn_in['fc2_W'], 'L1_gnn_fc2_b': _L1_gnn_in['fc2_b'], 'L1_gnn_fc3_W': _L1_gnn_in['fc3_W'], 'L1_gnn_fc3_b': _L1_gnn_in['fc3_b'], 'L2_gnn_W_self': _L2_gnn_in['W_self'], 'L2_gnn_b_self': _L2_gnn_in['b_self'], 'L2_gnn_W_nei': _L2_gnn_in['W_nei'], 'L2_gnn_b_nei': _L2_gnn_in['b_nei'], 'L3_gnn_W': _L3_gnn_in['W'], 'L3_gnn_W_self': _L3_gnn_in['W_self'], 'L3_gnn_a_in': _L3_gnn_in['a_in'], 'L3_gnn_a_out': _L3_gnn_in['a_out'], 'L3_gnn_bias': _L3_gnn_in['bias'], 'L3_gnn_ln_gamma': _L3_gnn_in['ln_gamma'], 'L3_gnn_ln_beta': _L3_gnn_in['ln_beta']}

def reference(x, src, dst, L0_gnn_W_lin, L0_gnn_W_agg, L1_gnn_W_l1, L1_gnn_b_l1, L1_gnn_W_r1, L1_gnn_W_l2, L1_gnn_b_l2, L1_gnn_W_r2, L1_gnn_res1_W, L1_gnn_res1_b, L1_gnn_res2_W, L1_gnn_res2_b, L1_gnn_fc1_W, L1_gnn_fc1_b, L1_gnn_fc2_W, L1_gnn_fc2_b, L1_gnn_fc3_W, L1_gnn_fc3_b, L2_gnn_W_self, L2_gnn_b_self, L2_gnn_W_nei, L2_gnn_b_nei, L3_gnn_W, L3_gnn_W_self, L3_gnn_a_in, L3_gnn_a_out, L3_gnn_bias, L3_gnn_ln_gamma, L3_gnn_ln_beta):
    import jax
    import jax.numpy as jnp

    def _L0_gnn_ref(x, W_lin, W_agg, edge_index):
        import jax, jax.numpy as jnp
        import numpy as np
        NUM_NODES = 3125
        NUM_EDGES = 50000
        D = 128
        row, col = (edge_index[0], edge_index[1])
        num_nodes = x.shape[0]
        msgs = x[row]
        summed = jax.ops.segment_sum(msgs, col, num_segments=num_nodes)
        count = jax.ops.segment_sum(jnp.ones((row.shape[0],), x.dtype), col, num_segments=num_nodes)[:, None]
        agg = summed / jnp.maximum(count, 1.0)
        out = agg @ W_agg.T + x @ W_lin.T
        norm = jnp.linalg.norm(out, axis=-1, keepdims=True)
        return out / jnp.maximum(norm, 1e-12)

    def _L1_gnn_ref(x, edge_index, W_l1, b_l1, W_r1, W_l2, b_l2, W_r2, res1_W, res1_b, res2_W, res2_b, fc1_W, fc1_b, fc2_W, fc2_b, fc3_W, fc3_b):
        import jax, jax.numpy as jnp
        import numpy as np
        N, E = (50000, 18750)
        IN, H, M, OUT = (128, 256, 256, 128)

        def _sage(x, src, dst, W_l, b_l, W_r, n):
            agg = jax.ops.segment_sum(x[src], dst, num_segments=n)
            deg = jax.ops.segment_sum(jnp.ones((src.shape[0],), x.dtype), dst, num_segments=n)
            agg = agg / jnp.maximum(deg, 1.0)[:, None]
            return agg @ W_l.T + b_l + x @ W_r.T
        src, dst = (edge_index[0], edge_index[1])
        n = x.shape[0]
        res1 = x @ res1_W.T + res1_b
        res2 = x @ res2_W.T + res2_b
        h = jax.nn.elu(_sage(x, src, dst, W_l1, b_l1, W_r1, n))
        h = jax.nn.elu(_sage(h, src, dst, W_l2, b_l2, W_r2, n)) + res1
        h = jax.nn.elu(h @ fc1_W.T + fc1_b)
        h = jax.nn.elu(h @ fc2_W.T + fc2_b) + res2
        return jax.nn.softplus(h @ fc3_W.T + fc3_b)

    def _L2_gnn_ref(x, edge_index, W_self, b_self, W_nei, b_nei):
        import jax, jax.numpy as jnp
        import numpy as np
        N = 10000
        E = 20000
        D_IN = 128
        D_OUT = 128
        row, col = (edge_index[0], edge_index[1])
        n = x.shape[0]
        m = x[col]
        summed = jax.ops.segment_sum(m, row, num_segments=n)
        cnt = jax.ops.segment_sum(jnp.ones((m.shape[0],), m.dtype), row, num_segments=n)
        nei = summed / (cnt[:, None] + 1e-12)
        h = x @ W_self.T + b_self + nei @ W_nei.T + b_nei
        return jax.nn.relu(h)

    def _L3_gnn_ref(h, edge_index, W, W_self, a_in, a_out, bias, ln_gamma, ln_beta):
        import jax, jax.numpy as jnp
        import numpy as np
        N = 3125
        E = 50000
        IN_DIM = 128
        OUT_DIM = 128
        H = 4
        HD = OUT_DIM // H
        NEG_SLOPE = 0.2
        EPS_SOFTMAX = 1e-08
        EPS_LN = 1e-05

        def _attention_aggregate(h_proj, sender, receiver, attn_vec, num_nodes):
            h_sender = h_proj[sender]
            h_receiver = h_proj[receiver]
            e = jnp.einsum('ehd,hd->eh', h_sender, attn_vec[:, :HD]) + jnp.einsum('ehd,hd->eh', h_receiver, attn_vec[:, HD:])
            e = jax.nn.leaky_relu(e, NEG_SLOPE)
            e_max = jax.ops.segment_max(e, receiver, num_segments=num_nodes)
            alpha = jnp.exp(e - e_max[receiver])
            alpha_sum = jax.ops.segment_sum(alpha, receiver, num_segments=num_nodes)
            alpha = alpha / (alpha_sum[receiver] + EPS_SOFTMAX)
            msg = h_sender * alpha[..., None]
            return jax.ops.segment_sum(msg, receiver, num_segments=num_nodes)
        n = h.shape[0]
        h_proj = (h @ W).reshape(n, H, HD)
        h_self = h @ W_self
        src, dst = (edge_index[0], edge_index[1])
        h_in = _attention_aggregate(h_proj, src, dst, a_in, n)
        h_out = _attention_aggregate(h_proj, dst, src, a_out, n)
        combined = h_self + h_in.reshape(n, -1) + h_out.reshape(n, -1) + bias
        mean = combined.mean(axis=-1, keepdims=True)
        var = combined.var(axis=-1, keepdims=True)
        normed = (combined - mean) * jax.lax.rsqrt(var + EPS_LN)
        return normed * ln_gamma + ln_beta
    edge_index = jnp.stack([src, dst])
    h = jnp.maximum(_layernorm(x, axis=-1), 0.0)
    x = x + _L0_gnn_ref(h, L0_gnn_W_lin, L0_gnn_W_agg, edge_index)
    h = jnp.maximum(_layernorm(x, axis=-1), 0.0)
    x = x + _L1_gnn_ref(h, edge_index, L1_gnn_W_l1, L1_gnn_b_l1, L1_gnn_W_r1, L1_gnn_W_l2, L1_gnn_b_l2, L1_gnn_W_r2, L1_gnn_res1_W, L1_gnn_res1_b, L1_gnn_res2_W, L1_gnn_res2_b, L1_gnn_fc1_W, L1_gnn_fc1_b, L1_gnn_fc2_W, L1_gnn_fc2_b, L1_gnn_fc3_W, L1_gnn_fc3_b)
    h = jnp.maximum(_layernorm(x, axis=-1), 0.0)
    x = x + _L2_gnn_ref(h, edge_index, L2_gnn_W_self, L2_gnn_b_self, L2_gnn_W_nei, L2_gnn_b_nei)
    h = jnp.maximum(_layernorm(x, axis=-1), 0.0)
    x = x + _L3_gnn_ref(h, edge_index, L3_gnn_W, L3_gnn_W_self, L3_gnn_a_in, L3_gnn_a_out, L3_gnn_bias, L3_gnn_ln_gamma, L3_gnn_ln_beta)
    return x

_drawn_inputs = setup_inputs


def setup_inputs(seed=0):
    import zlib

    import numpy as np

    out = dict(_drawn_inputs(seed))
    spreads = {'L1_gnn_b_l1': (0.0, 0.272),
     'L1_gnn_b_l2': (0.0, 0.284),
     'L1_gnn_res1_b': (0.0, 0.1),
     'L1_gnn_res2_b': (0.0, 0.1),
     'L1_gnn_fc1_b': (0.0, 0.304),
     'L1_gnn_fc2_b': (0.0, 0.1),
     'L1_gnn_fc3_b': (0.0, 0.1),
     'L3_gnn_bias': (0.0, 0.1),
     'L3_gnn_ln_gamma': (1.0, 0.2),
     'L3_gnn_ln_beta': (0.0, 0.1)}
    factors = {'L3_gnn_a_in': 30.098, 'L3_gnn_a_out': 31.387}
    for name, (base, spread) in spreads.items():
        noise = np.random.default_rng([zlib.crc32(name.encode()), seed]).standard_normal(out[name].shape)
        drawn = base * np.exp(spread * noise) if base else spread * noise
        out[name] = jnp.asarray(drawn.astype(out[name].dtype))
    for name, factor in factors.items():
        out[name] = (out[name] * factor).astype(out[name].dtype)
    return out
```

```python
from contextlib import ExitStack

import numpy as np
import concourse.bass as bass
from concourse import mybir

F32 = mybir.dt.float32
F16 = mybir.dt.float16
BF16 = mybir.dt.bfloat16
I32 = mybir.dt.int32
ALU = mybir.AluOpType
ACT = mybir.ActivationFunctionType
AX_X = mybir.AxisListType.X

P = 128
N_NODES, N_EDGES, D = 3125, 50000, 128
TILES = -(-N_NODES // P)
NP_ = TILES * P
TAIL = N_NODES - (TILES - 1) * P
EP = 125
EC = N_EDGES // EP
GROUP = 8
CHUNKS = -(-(N_EDGES // P + TILES) // (2 * GROUP)) * 2 * GROUP
STEPS = CHUNKS // (2 * GROUP)
SLOTS = 2 * GROUP
BLK = 400
NBLK = NP_ // BLK
HEADS, HD = 4, 32
H1 = 256
SC = 4 * HEADS
SPLIT = 3
NEG_BIG = -float(2.0 ** 100)
BANK = 512
DEG_COL = NP_

C_ID, C_TRI, C_TRII, C_IOTA, C_ONE, C_MASK = 0, 128, 256, 384, 384 + CHUNKS, 384 + CHUNKS + 128
C_PICK = C_MASK + 1
C_ALL = C_PICK + HEADS * P

_W = [("L0_lin", D), ("L0_agg", D), ("l1", H1), ("r1", H1), ("l2", 2 * H1), ("r2", 2 * H1), ("res1", H1),
      ("res2", H1), ("fc1", 2 * H1), ("fc2", 2 * H1), ("fc3", 2 * D), ("L2_self", D), ("L2_nei", D),
      ("L3_W", D), ("L3_self", D), ("L3_WT", D)]
W_AT = {}
_at = 0
for _n, _c in _W:
    W_AT[_n] = _at
    _at += _c
W_ALL = _at
BCOL = {"b_l1": 0, "b_l2": 2, "res1": 4, "res2": 6, "fc1": 8, "fc2": 10}
B_ALL = 12
ROW = {"fc3": 0, "L2_self": 1, "L2_nei": 2, "L3_bias": 3, "gamma": 4, "beta": 5}
ROWS = 6


def linker(eng, sem):
    count = [0]

    def link(ins):
        count[0] += 1
        ins.then_inc(sem, 1)
        eng.wait_ge(sem, count[0])

    return link


def gnn_kernel(nc, edges, x_in, consts, weights, bias_cols, bias_rows, attn, out, dbg=None):
    with ExitStack() as ctx:
        def sb(name, shape, dt=F32):
            return ctx.enter_context(nc.sbuf_tensor(name, shape, dt))

        def sem(name):
            return ctx.enter_context(nc.semaphore(name))

        def dram(name, shape):
            return nc.dram_tensor(name, shape, F32, kind="Internal").ap()

        PS = ctx.enter_context(nc.psum_tensor("PS", [P, 8 * BANK], F32))
        cst = sb("cst", [P, C_ALL])
        ident, tri, tri_incl = cst[:, C_ID:C_ID + P], cst[:, C_TRI:C_TRI + P], cst[:, C_TRII:C_TRII + P]
        iota = cst[:, C_IOTA:C_IOTA + CHUNKS]
        ones = cst[:, C_ONE:C_ONE + P]
        neg_mask = cst[:, C_MASK:C_MASK + 1]
        W = sb("W", [P, W_ALL])
        bcol = sb("bcol", [P, B_ALL])
        brow = sb("brow", [P, ROWS, D])
        x = sb("x", [P, TILES, D])
        h = sb("h", [P, TILES, D])
        hT = sb("hT", [P, NP_])
        big = sb("big", [P, 16000])
        rdeg = sb("rdeg", [P, NP_])
        idx = sb("idx", [P, 2, CHUNKS], I32)
        key = sb("key", [P, 2, CHUNKS])
        tile_off = sb("tile_off", [1, 2, CHUNKS], I32)
        tile_sel = sb("tile_sel", [TILES, 2, CHUNKS])
        G = sb("G", [P, SLOTS, D])
        OH = sb("OH", [P, SLOTS, P])
        aggT = big[:, 12800:16000]
        scr = big[:, 12800:16000].rearrange("p (t f) -> p t f", t=TILES)
        h1T = big[:, 0:6400].rearrange("p (c n) -> p c n", c=2)
        agg2T = big[:, 6400:12800].rearrange("p (c n) -> p c n", c=2)
        h1N = agg2T[:, 0, :].rearrange("p (t f) -> p t f", t=TILES)
        bcol_m1 = sb("bcol_m1", [P, B_ALL])
        chunk_tile = sb("chunk_tile", [P, 2, CHUNKS])
        attn_sb = sb("attn_sb", [P, SC])
        Wx = sb("Wx", [P, SC])
        score = sb("score", [P, TILES, SC])
        parts = sb("parts", [P, 2, TILES, SPLIT * HEADS])
        rT = sb("rT", [TILES, 2, HEADS, P])
        pick = sb("pick", [P, HEADS, P], BF16)
        big_id = sb("big_id", [P, P], BF16)
        sT = sb("sT", [P, SLOTS, P], BF16)
        part_h = sb("part_h", [P, TILES * HEADS], BF16)
        comb = rdeg[:, :].rearrange("p (t f) -> p t f", t=TILES)
        sE = big[:, 0:4992].rearrange("p (k c) -> p k c", c=SPLIT * HEADS)
        cmax = big[:, 4992:6656].rearrange("p (h k) -> p h k", h=HEADS)
        mr = big[:, 6656:9984].rearrange("p (q k) -> p q k", q=2 * HEADS)
        er = big[:, 9984:13312].rearrange("p (q k) -> p q k", q=2 * HEADS)
        ex = big[:, 13312:14976].rearrange("p (h k) -> p h k", h=HEADS)
        sender = hT[:, 0:1664].rearrange("p (h k) -> p h k", h=HEADS)
        reset = hT[:, 1664:1664 + 2 * CHUNKS].rearrange("p (a k) -> p a k", a=2)
        OHb = OH[:, :, :].bitcast(BF16)[:, :, 0:P]
        idxbuf = sb("idxbuf", [P, 2, GROUP], I32)
        zeros = sb("zeros", [P, BANK], BF16)
        st = sb("st", [P, 8, TILES])
        eps = sb("eps", [P, 2])

        masks = big[0:EP, 0:TILES * EC // 2].bitcast(BF16)
        scan = big[0:EP, TILES * EC // 2:TILES * EC // 2 * 3]
        scan_cmp = big[0:TILES, 15000:15000 + 2 * CHUNKS].rearrange("p (a b) -> p a b", a=2)
        cmp_f = big[:, 0:2 * CHUNKS].rearrange("p (a b) -> p a b", a=2)
        cmp_i = big[:, 2 * CHUNKS:4 * CHUNKS].bitcast(I32).rearrange("p (a b) -> p a b", a=2)
        e_i = sb("e_i", [EP, 2, EC], I32)
        ev_i = G[0:EP, 0:12, :].bitcast(I32).rearrange("p a b -> p (a b)")[:, 0:3 * EC] \
            .rearrange("p (a b) -> p a b", a=3)
        ev_f = OH[0:EP, 0:16, :].rearrange("p a b -> p (a b)")[:, 0:5 * EC].rearrange("p (a b) -> p a b", a=5)
        cnt = sb("cnt", [P, 6, TILES])
        cnt_i = sb("cnt_i", [P, 2, TILES], I32)
        col = sb("col", [TILES, 4])
        col_i = sb("col_i", [TILES, 2], I32)
        iota_h = sb("iota_h", [P, CHUNKS], F16)
        U = 4
        work = sb("work", [P, 2 * U * CHUNKS + U * P])
        A = work[0:EP, 0:2 * U * CHUNKS].bitcast(F16).rearrange("p (g j k c) -> p g j k c", g=2, j=U, k=2)
        B = work[0:EP, 2 * U * CHUNKS:].bitcast(F16).rearrange("p (g j c) -> p g j c", g=2, j=U)
        blk = work[:, 0:8 * BLK].rearrange("p (x o c n) -> p x o c n", x=2, o=2, c=2)

        T = {n: dram(f"T_{n}", [NP_, D]) for n in ("h0", "h1", "g0", "g1", "h2", "proj")}
        T_sc = [dram(f"T_sc{d}", [NP_, SPLIT * HEADS]) for d in range(2)]

        loaded_edges = sem("loaded_edges")
        loaded_consts = sem("loaded_consts")
        loaded_x = sem("loaded_x")
        loaded_w = sem("loaded_w")
        loaded_b = sem("loaded_b")
        dve_step = sem("dve_step")
        act_step = sem("act_step")
        zeros_ready = sem("zeros_ready")
        x_cleared = sem("x_cleared")
        counts_ready = sem("counts_ready")
        counts_summed = sem("counts_summed")
        chunks_ready = sem("chunks_ready")
        chunks_summed = sem("chunks_summed")
        bounds_ready = sem("bounds_ready")
        tiles_summed = sem("tiles_summed")
        where_ready = sem("where_ready")
        perm_used = sem("perm_used")
        perm_done = sem("perm_done")
        sorted_ready = sem("sorted_ready")
        table_ready = sem("table_ready")
        table_stored = sem("table_stored")
        idx_ready = sem("idx_ready")
        landed = [sem(f"landed{i}") for i in range(SLOTS)]
        oh_ready = sem("oh_ready")
        used = [sem(f"used{i}") for i in range(2)]
        round_done = sem("round_done")
        gathers_begun = sem("gathers_begun")
        var_ready = sem("var_ready")
        std_ready = sem("std_ready")
        h_ready = sem("h_ready")
        hT_summed = sem("hT_summed")
        hT_ready = sem("hT_ready")
        diag_ready = sem("diag_ready")
        rdeg_summed = sem("rdeg_summed")
        agg_ready = sem("agg_ready")
        wx_summed = sem("wx_summed")
        wx_ready = sem("wx_ready")
        out0_summed = sem("out0_summed")
        square_ready = sem("square_ready")
        sumsq_ready = sem("sumsq_ready")
        len_ready = sem("len_ready")
        lin_ready = sem("lin_ready")
        exp_ready = sem("exp_ready")
        act_done = sem("act_done")
        h1_transposed = sem("h1_transposed")
        h1_ready = sem("h1_ready")
        fc3_summed = sem("fc3_summed")
        z_ready = sem("z_ready")
        log_ready = sem("log_ready")
        out2_summed = sem("out2_summed")
        proj_summed = sem("proj_summed")
        proj_ready = sem("proj_ready")
        score_summed = sem("score_summed")
        self_summed = sem("self_summed")
        self_ready = sem("self_ready")
        parts_ready = sem("parts_ready")
        rT_summed = sem("rT_summed")
        rT_ready = sem("rT_ready")
        sT_summed = sem("sT_summed")
        sT_ready = sem("sT_ready")
        masked_ready = sem("masked_ready")
        reduced = sem("reduced")
        recv_summed = sem("recv_summed")
        mr_ready = sem("mr_ready")
        oh_again = sem("oh_again")
        ohT_summed = sem("ohT_summed")
        ohT_ready = sem("ohT_ready")
        er_summed = sem("er_summed")
        er_ready = sem("er_ready")
        arg_ready = sem("arg_ready")
        ex_ready = sem("ex_ready")
        scaled_ready = sem("scaled_ready")
        den_ready = sem("den_ready")
        x_final = sem("x_final")
        stored = sem("stored")

        dve_link = linker(nc.vector, dve_step)
        act_link = linker(nc.scalar, act_step)
        block = ctx.enter_context(nc.Block())

        def sort_dve(v, d):
            k_i, o_i = e_i[:, 1 - d, :], e_i[:, d, :]
            a, b, lo, hi, tl = (ev_f[:, i, :] for i in range(5))
            dve_link(v.tensor_scalar(ev_i[:, 0, :], k_i, 7, None, ALU.arith_shift_right))
            dve_link(v.tensor_copy(tl, ev_i[:, 0, :]))
            dve_link(v.tensor_scalar(ev_i[:, 1, :], k_i, P - 1, None, ALU.bitwise_and))
            dve_link(v.tensor_scalar(ev_i[:, 2, :], o_i, 256.0, 1.0, ALU.mult, ALU.add))
            dve_link(v.tensor_tensor(ev_i[:, 0, :], ev_i[:, 1, :], ev_i[:, 2, :], ALU.add))
            dve_link(v.tensor_scalar(ev_i[:, 1, :], ev_i[:, 0, :], 1023, None, ALU.bitwise_and))
            dve_link(v.tensor_scalar(ev_i[:, 2, :], ev_i[:, 0, :], 10, None, ALU.arith_shift_right))
            if d == 1:
                v.wait_ge(perm_done, 1)
            v.tensor_copy(lo, ev_i[:, 1, :])
            dve_link(v.tensor_copy(hi, ev_i[:, 2, :]))
            m3 = masks.rearrange("p (t j) -> p t j", t=TILES)
            s3 = scan.rearrange("p (t j) -> p t j", t=TILES)
            dve_link(v.tensor_tensor(m3, iota[0:EP, 0:TILES].unsqueeze(2).to_broadcast([EP, TILES, EC]),
                                     tl.unsqueeze(1).to_broadcast([EP, TILES, EC]), ALU.is_equal))
            dve_link(v.tensor_tensor_scan(scan, masks, masks, 0.0, ALU.add, ALU.max))
            end, n, before, first, tot = (cnt[0:EP, i, :] for i in range(5))
            dve_link(v.tensor_copy(end, s3[:, :, EC - 1]))
            v.tensor_copy(before[:, 1:TILES], end[:, 0:TILES - 1])
            dve_link(v.memset(before[:, 0:1], 0.0))
            v.tensor_tensor(n, end, before, ALU.subtract).then_inc(counts_ready, 1)
            v.wait_ge(counts_summed, d + 1)
            totb = cnt[:, 5, :]
            dve_link(v.tensor_scalar(cnt_i[:, 0, :], PS[:, 0:TILES], float(P - 1), None, ALU.add))
            dve_link(v.tensor_scalar(cnt_i[:, 1, :], cnt_i[:, 0, :], 7, None, ALU.arith_shift_right))
            dve_link(v.tensor_copy(totb, cnt_i[:, 1, :]))
            dve_link(v.tensor_scalar(col_i[:, 0:1], PS[0:TILES, BANK:BANK + 1], float(P - 1), None, ALU.add))
            dve_link(v.tensor_scalar(col_i[:, 1:2], col_i[:, 0:1], 7, None, ALU.arith_shift_right))
            v.tensor_copy(col[:, 0:1], col_i[:, 1:2]).then_inc(chunks_ready, 1)
            dve_link(v.tensor_tensor_scan(cnt[:, 4, :], totb, totb, 0.0, ALU.add, ALU.max))
            dve_link(v.tensor_tensor(cnt[:, 3, :], cnt[:, 4, :], totb, ALU.subtract))
            dve_link(v.tensor_scalar(first, first, float(P), -1.0, ALU.mult, ALU.add))
            dve_link(v.tensor_tensor(first, first, PS[0:EP, TILES:2 * TILES], ALU.add))
            dve_link(v.tensor_tensor(first, first, before, ALU.subtract))
            dve_link(v.tensor_tensor(s3, s3, first.unsqueeze(2).to_broadcast([EP, TILES, EC]), ALU.add))
            dve_link(v.tensor_tensor(s3, s3, m3, ALU.mult))
            dve_link(v.tensor_reduce(tl, scan.rearrange("p (t j) -> p j t", t=TILES), AX_X, ALU.add))
            dve_link(v.tensor_copy(ev_i[:, 0, :], tl))
            dve_link(v.tensor_scalar(ev_i[:, 1, :], ev_i[:, 0, :], 7, None, ALU.arith_shift_right))
            dve_link(v.tensor_scalar(ev_i[:, 2, :], ev_i[:, 0, :], P - 1, None, ALU.bitwise_and))
            dve_link(v.tensor_copy(a, ev_i[:, 1, :]))
            dve_link(v.tensor_copy(b, ev_i[:, 2, :]))
            v.wait_ge(chunks_summed, d + 1)
            dve_link(v.tensor_copy(col[:, 1:2], PS[0:TILES, 2 * BANK:2 * BANK + 1]))
            dve_link(v.tensor_tensor(col[:, 2:3], col[:, 1:2], col[:, 0:1], ALU.subtract))
            past, since = scan_cmp[:, 0, :], scan_cmp[:, 1, :]
            v.tensor_scalar(past, iota[0:TILES, :], col[:, 1:2], None, ALU.is_ge).then_inc(bounds_ready, 1)
            v.wait_ge(bounds_ready, d + 1)
            dve_link(v.tensor_scalar(since, iota[0:TILES, :], col[:, 2:3], None, ALU.is_ge))
            dve_link(v.scalar_tensor_tensor(tile_sel[:, d, :], past, neg_mask[0:TILES, :], since, ALU.mult, ALU.add))
            v.wait_ge(tiles_summed, d + 1)
            v.tensor_copy(chunk_tile[:, d, :], PS[:, 3 * BANK:3 * BANK + CHUNKS])
            dve_link(v.tensor_copy(tile_off[0:1, d, :], PS[0:1, 3 * BANK:3 * BANK + CHUNKS]))

            def where_group(i, g, wait):
                if wait is not None:
                    v.wait_ge(perm_used, wait)
                for j in range(U):
                    c = bass.ds(i * (2 * U) + g * U + j, 1)
                    v.tensor_scalar(A[:, g, j, 0, :], iota_h[0:EP, :], a[:, c], lo[:, c], ALU.is_equal, ALU.mult)
                    v.tensor_scalar(A[:, g, j, 1, :], iota_h[0:EP, :], a[:, c], hi[:, c], ALU.is_equal, ALU.mult)
                    last = v.tensor_scalar(B[:, g, j, :], iota_h[0:EP, 0:P], b[:, c], None, ALU.is_equal)
                last.then_inc(where_ready, 1)

            NG = EC // (2 * U)
            for g in range(2):
                where_group(0, g, 2 * NG * d if d else None)
            with v.Fori(1, NG) as i:
                for g in range(2):
                    where_group(i, g, 2 * NG * d + 2 * i + g - 1)
            v.wait_ge(perm_done, d + 1)
            lo_f, sum_f, p_i = cmp_f[:, 0, :], cmp_f[:, 1, :], cmp_i
            dve_link(v.tensor_copy(lo_f, PS[:, 4 * BANK:4 * BANK + CHUNKS]))
            dve_link(v.scalar_tensor_tensor(p_i[:, 0, :], PS[:, 5 * BANK:5 * BANK + CHUNKS], 1024.0, lo_f,
                                            ALU.mult, ALU.add))
            dve_link(v.tensor_scalar(idx[:, d, :], p_i[:, 0, :], 8, None, ALU.arith_shift_right))
            dve_link(v.tensor_scalar(p_i[:, 1, :], p_i[:, 0, :], 255, None, ALU.bitwise_and))
            v.tensor_scalar(key[:, d, :], p_i[:, 1, :], -1.0, None, ALU.add).then_inc(sorted_ready, 1)
            v.wait_ge(sorted_ready, d + 1)


        def sort_pe(t, d):
            t.wait_ge(counts_ready, d + 1)
            n = cnt[0:EP, 1, :]
            t.matmul(PS[:, 0:TILES], ones[0:EP, :], n, start=True, stop=True)
            t.matmul(PS[0:EP, TILES:2 * TILES], tri[0:EP, 0:EP], n, start=True, stop=True)
            t.matmul(PS[0:TILES, BANK:BANK + 1], n, ones[0:EP, 0:1], start=True, stop=True).then_inc(counts_summed, 1)
            t.wait_ge(chunks_ready, d + 1)
            t.matmul(PS[0:TILES, 2 * BANK:2 * BANK + 1], tri_incl[0:TILES, 0:TILES], col[:, 0:1],
                     start=True, stop=True).then_inc(chunks_summed, 1)
            t.wait_ge(bounds_ready, d + 1)
            t.matmul(PS[:, 3 * BANK:3 * BANK + CHUNKS], ones[0:TILES - 1, :], scan_cmp[0:TILES - 1, 0, :],
                     start=True, stop=True).then_inc(tiles_summed, 1)
            for k in (4, 5):
                t.matmul(PS[:, k * BANK:k * BANK + CHUNKS], zeros[:, 0:P], zeros[:, 0:CHUNKS], start=True, stop=False,
                         skip_group_check=True)
            NG = EC // (2 * U)

            def perm_group(i, g):
                t.wait_ge(where_ready, 2 * NG * d + 2 * i + g + 1)
                for j in range(U):
                    for k in range(2):
                        last = t.matmul(PS[:, (4 + k) * BANK:(4 + k) * BANK + CHUNKS], B[:, g, j, :], A[:, g, j, k, :],
                                        start=False, stop=True, skip_group_check=True)
                last.then_inc(perm_used, 1)
                return last

            with t.Fori(0, NG) as i:
                for g in range(2):
                    perm_group(i, g)
            t.wait_ge(perm_used, 2 * NG * (d + 1))
            t.nop().then_inc(perm_done, 1)

        def base(r):
            return r * STEPS

        def round_act(a, r, d):
            def step(i, half, first):
                if r or not first:
                    a.wait_ge(used[half], base(r) + i)
                c = bass.ds(i * SLOTS + half * GROUP, GROUP)
                a.copy(idxbuf[:, half, :], idx[:, d, c]).then_inc(idx_ready, 1)

            for half in range(2):
                step(0, half, True)
            with a.Fori(1, STEPS) as i:
                for half in range(2):
                    step(i, half, False)

        def round_pool(p, r, table, width=D):
            def step(i):
                for half in range(2):
                    p.wait_ge(idx_ready, 2 * (base(r) + i) + half + 1)
                    p.sem_inc(gathers_begun)
                    for j in range(GROUP):
                        s = half * GROUP + j
                        p.indirect_dma_start(out=G[:, s, 0:width], out_offset=None, in_=table[:, :],
                                             in_offset=bass.IndirectOffsetOnAxis(ap=idxbuf[:, half, j:j + 1], axis=0)) \
                            .then_inc(landed[s], 16)

            with p.Fori(0, STEPS) as i:
                step(i)

        def round_dve(v, r, d, op=ALU.is_equal):
            def step(i, half, first):
                if r or not first:
                    v.wait_ge(used[half], base(r) + i)
                c = bass.ds(i * SLOTS + half * GROUP, GROUP)
                v.tensor_tensor(OH[:, half * GROUP:(half + 1) * GROUP, :],
                                iota[:, 0:P].unsqueeze(1).to_broadcast([P, GROUP, P]),
                                key[:, d, c].unsqueeze(2).to_broadcast([P, GROUP, P]), op).then_inc(oh_ready, 1)

            for half in range(2):
                step(0, half, True)
            with v.Fori(1, STEPS) as i:
                for half in range(2):
                    step(i, half, False)

        def load_tiles(t, d, i, half):
            c = bass.ds(i * SLOTS + half * GROUP, GROUP)
            regs = [t.alloc_register(f"off{half}_{j}_{nc.next_id()}") for j in range(GROUP)]
            t.load(regs, tile_off[0:1, d, c])
            return [t.snap(g, min_val=0, max_val=TILES - 1) for g in regs]

        def clear_psum(t):
            for k in range(7):
                t.matmul(PS[:, k * BANK:(k + 1) * BANK], zeros[:, 0:P], zeros[:, 0:BANK], start=True, stop=False,
                         skip_group_check=True)

        def add_to(t, where, lhsT, rhs):
            return t.matmul(where, lhsT, rhs, start=False, stop=True, skip_group_check=True)

        def round_pe(t, r, d, degrees):
            clear_psum(t)
            with t.Fori(0, STEPS) as i:
                for half in range(2):
                    tiles = load_tiles(t, d, i, half)
                    t.wait_ge(oh_ready, 2 * (base(r) + i) + half + 1)
                    for j in range(GROUP):
                        s = half * GROUP + j
                        t.wait_ge(landed[s], 16 * (base(r) + i + 1))
                        last = add_to(t, PS[:, bass.ds(tiles[j] * P, P)], G[:, s, :], OH[:, s, :])
                        if degrees:
                            last = add_to(t, PS[:, bass.ds(tiles[j] + DEG_COL, 1)], OH[:, s, :], ones[:, 0:1])
                    last.then_inc(used[half], 1)
            for half in range(2):
                t.wait_ge(used[half], base(r + 1))
            t.drain().then_inc(round_done, 1)

        def bc(a, n):
            return a.unsqueeze(2).to_broadcast([P, a.shape[1], n])

        def norm_dve(v, n, relu):
            src = x if relu else h
            dve_link(v.tensor_reduce(st[:, 0, :], src[:, :, :], AX_X, ALU.add))
            dve_link(v.tensor_scalar(st[:, 0, :], st[:, 0, :], 1.0 / D, None, ALU.mult))
            dve_link(v.tensor_tensor(h[:, :, :], src[:, :, :], bc(st[:, 0, :], D), ALU.subtract))
            dve_link(v.tensor_tensor(scr, h[:, :, :], h[:, :, :], ALU.mult))
            v.tensor_reduce(st[:, 1, :], scr, AX_X, ALU.add).then_inc(var_ready, 1)
            v.wait_ge(std_ready, n + 1)
            dve_link(v.reciprocal(st[:, 3, :], st[:, 2, :]))
            if relu:
                v.scalar_tensor_tensor(h[:, :, :], h[:, :, :], 0.0, bc(st[:, 3, :], D), ALU.max, ALU.mult) \
                    .then_inc(h_ready, 1)
            else:
                dve_link(v.tensor_tensor(h[:, :, :], h[:, :, :], bc(st[:, 3, :], D), ALU.mult))

        def norm_act(a, n):
            a.wait_ge(var_ready, n + 1)
            a.activation(st[:, 2, :], st[:, 1, :], ACT.Sqrt, bias=eps[:, 0:1], scale=1.0 / D).then_inc(std_ready, 1)

        def transposes_pe(t, src_of, sem_):
            for k in range(TILES):
                last = t.transpose(PS[:, k * P:(k + 1) * P], src_of(k), ident)
            last.then_inc(sem_, 1)

        def node_major(t, pairs, sem_):
            for k in range(TILES):
                for n, (act_T, w) in enumerate(pairs):
                    last = t.matmul(PS[:, k * P:(k + 1) * P], act_T[:, k * P:(k + 1) * P], w,
                                    start=(n == 0), stop=(n == len(pairs) - 1))
            last.then_inc(sem_, 1)

        def wt(name, c=0, width=P):
            at = W_AT[name] + c
            return W[:, at:at + width]

        def agg_dve(v, r, dst, degrees, exact_one):
            v.wait_ge(round_done, r + 1)
            if degrees:
                n = degrees - 1
                deg = PS[:, DEG_COL:DEG_COL + TILES]
                if exact_one:
                    dve_link(v.tensor_scalar(st[:, 4, :], deg, 1.0, None, ALU.max))
                else:
                    dve_link(v.tensor_scalar(st[:, 4, :], deg, 1e-12, None, ALU.add))
                dve_link(v.reciprocal(st[:, 5, :], st[:, 4, :]))
                dve_link(v.tensor_copy(dst, PS[:, 0:NP_]))
                v.tensor_tensor(h[:, :, :], ident.unsqueeze(1).to_broadcast([P, TILES, P]), bc(st[:, 5, :], P),
                                ALU.mult).then_inc(diag_ready, 1)
                v.wait_ge(rdeg_summed, n + 1)
                dve_link(v.tensor_copy(rdeg[:, :], PS[:, 0:NP_]))
                v.tensor_tensor(dst, dst, rdeg[:, :], ALU.mult).then_inc(agg_ready, 1)
            else:
                v.tensor_tensor(dst, PS[:, 0:NP_], rdeg[:, :], ALU.mult).then_inc(agg_ready, 1)

        def rdeg_pe(t, n):
            t.wait_ge(diag_ready, n)
            hf = h[:, :, :].rearrange("p t f -> p (t f)")
            for a0 in range(0, NP_, BANK):
                a1 = min(a0 + BANK, NP_)
                last = t.matmul(PS[:, a0:a1], ones, hf[:, a0:a1], start=True, stop=True)
            last.then_inc(rdeg_summed, 1)

        def ps2(bank):
            return PS[:, bank * BANK:(bank + 2) * BANK].rearrange("p (c n) -> p c n", c=2)[:, :, 0:BLK]

        def lin_pe(t, bank, terms, sem_=None):
            for ob in range(2):
                o = PS[:, (bank + ob) * BANK:(bank + ob) * BANK + BLK]
                for n, (name, c, rhs) in enumerate(terms):
                    last = t.matmul(o, wt(name, c * H1 + ob * P), rhs, start=(n == 0), stop=(n == len(terms) - 1))
            if sem_ is not None:
                last.then_inc(sem_, 1)

        def elu_act(a, n, X, bname):
            a.wait_ge(lin_ready, n)
            for ob in range(2):
                last = a.activation(blk[:, X, 0, ob, :], PS[:, (2 * X + ob) * BANK:(2 * X + ob) * BANK + BLK], ACT.Exp,
                                    bias=bcol[:, BCOL[bname] + ob:BCOL[bname] + ob + 1])
            last.then_inc(exp_ready, 1)

        def elu_dve(v, n, X, bname, dest, res=None):
            v.wait_ge(exp_ready, n)
            e, o = blk[:, X, 0, :, :], blk[:, X, 1, :, :]
            for ob in range(2):
                last = v.tensor_scalar(o[:, ob, :], PS[:, (2 * X + ob) * BANK:(2 * X + ob) * BANK + BLK],
                                bcol_m1[:, BCOL[bname] + ob:BCOL[bname] + ob + 1], -1.0, ALU.add, ALU.max)
            last.then_inc(clipped, 1)
            v.wait_ge(clipped, n)
            if res is None:
                v.scalar_tensor_tensor(dest, e, 1.0, o, ALU.min, ALU.add).then_inc(act_done, 1)
                return
            v.scalar_tensor_tensor(e, e, 1.0, o, ALU.min, ALU.add).then_inc(elu_done, 1)
            v.wait_ge(elu_done, res[1])
            for ob in range(2):
                at = (4 + 2 * X + ob) * BANK
                c = BCOL[res[0]] + ob
                last = v.scalar_tensor_tensor(dest[:, ob, :], PS[:, at:at + BLK], bcol[:, c:c + 1], e[:, ob, :],
                                              ALU.add, ALU.add)
            last.then_inc(act_done, 1)

        PAIRS = NBLK // 2

        def cols(i, X):
            return bass.ds(i * (2 * BLK) + X * BLK, BLK)

        def sage1_pe(t):
            with t.Fori(0, PAIRS) as i:
                for X in range(2):
                    t.wait_ge(act_done, 2 * i + 1 + X)
                    lin_pe(t, 2 * X, [("l1", 0, aggT[:, cols(i, X)]), ("r1", 0, hT[:, cols(i, X)])], lin_ready)

        def chain_pe(t):
            with t.Fori(0, PAIRS) as i:
                for X in range(2):
                    c = cols(i, X)
                    t.wait_ge(act_done, 10 + 6 * i - 1 + X)
                    lin_pe(t, 4 + 2 * X, [("res1", 0, hT[:, c])])
                    lin_pe(t, 2 * X, [("l2", k, agg2T[:, k, c]) for k in range(2)]
                           + [("r2", k, h1T[:, k, c]) for k in range(2)], lin_ready)
                for X in range(2):
                    t.wait_ge(act_done, 10 + 6 * i + 1 + X)
                    lin_pe(t, 2 * X, [("fc1", k, blk[:, X, 1, k, :]) for k in range(2)], lin_ready)
                for X in range(2):
                    t.wait_ge(act_done, 10 + 6 * i + 3 + X)
                    lin_pe(t, 4 + 2 * X, [("res2", 0, hT[:, cols(i, X)])])
                    lin_pe(t, 2 * X, [("fc2", k, blk[:, X, 1, k, :]) for k in range(2)], lin_ready)

        def sage1_act(a):
            with a.Fori(0, PAIRS) as i:
                for X in range(2):
                    elu_act(a, 2 * i + 1 + X, X, "b_l1")

        def chain_act(a):
            with a.Fori(0, PAIRS) as i:
                for n, name in enumerate(("b_l2", "fc1", "fc2")):
                    for X in range(2):
                        elu_act(a, 8 + 6 * i + 2 * n + X + 1, X, name)

        def sage1_dve(v):
            with v.Fori(0, PAIRS) as i:
                for X in range(2):
                    elu_dve(v, 2 * i + 1 + X, X, "b_l1", h1T[:, :, cols(i, X)])

        def chain_dve(v):
            with v.Fori(0, PAIRS) as i:
                for X in range(2):
                    elu_dve(v, 8 + 6 * i + X + 1, X, "b_l2", blk[:, X, 1, :, :], ("res1", 4 * i + X + 1))
                for X in range(2):
                    elu_dve(v, 8 + 6 * i + 2 + X + 1, X, "fc1", blk[:, X, 1, :, :])
                for X in range(2):
                    elu_dve(v, 8 + 6 * i + 4 + X + 1, X, "fc2", agg2T[:, :, cols(i, X)], ("res2", 4 * i + 2 + X + 1))

        def top_act(a, r, d):
            def indices(i, half):
                c = bass.ds(i * SLOTS + half * GROUP, GROUP)
                a.wait_ge(used[half], base(r) + i)
                a.copy(idxbuf[:, half, :], idx[:, d, c]).then_inc(idx_ready, 1)

            def step(i, more):
                for half in range(2):
                    a.wait_ge(sT_summed, 2 * (STEPS * d + i) + half + 1)
                    c = bass.ds(i * SLOTS + half * GROUP, GROUP)
                    a.copy(sE[:, c, :], G[:, half * GROUP:(half + 1) * GROUP, 0:SPLIT * HEADS])
                    at = (4 + 2 * half) * BANK
                    a.copy(sT[0:SPLIT * HEADS, half * GROUP:(half + 1) * GROUP, :],
                           PS[0:SPLIT * HEADS, at:at + GROUP * P].rearrange("p (j e) -> p j e", j=GROUP)) \
                        .then_inc(sT_ready, 1)
                    if more:
                        indices(i + 1, half)

            for half in range(2):
                indices(0, half)
            with a.Fori(0, STEPS - 1) as i:
                step(i, True)
            step(STEPS - 1, False)

        def top_pe(t, r, d):
            with t.Fori(0, STEPS) as i:
                for half in range(2):
                    n = 2 * (STEPS * d + i) + half
                    for j in range(GROUP):
                        s = half * GROUP + j
                        t.wait_ge(landed[s], 16 * (base(r) + i + 1))
                        at = (4 + 2 * half) * BANK + j * P
                        last = t.transpose(PS[0:SPLIT * HEADS, at:at + P], G[:, s, 0:SPLIT * HEADS], ident)
                    last.then_inc(sT_summed, 1)
                    t.wait_ge(oh_ready, 2 * (base(r) + i) + half + 1)
                    t.wait_ge(sT_ready, n + 1)
                    for j in range(GROUP):
                        s = half * GROUP + j
                        bank = (j % 4) * BANK
                        t.wait_ge(reduced, n * GROUP + j + 1)
                        t.matmul(PS[:, bank:bank + BANK], OHb[:, s, :],
                                 big_id[:, :].unsqueeze(1).to_broadcast([P, HEADS, P]), start=True, stop=False,
                                 skip_group_check=True)
                        for hd in range(HEADS):
                            last = t.matmul(PS[:, bank + hd * P:bank + (hd + 1) * P], pick[:, hd, :], sT[:, s, :],
                                            start=False, stop=True, skip_group_check=True)
                        last.then_inc(masked_ready, 1)
                    t.nop().then_inc(used[half], 1)
            for half in range(2):
                t.wait_ge(used[half], base(r + 1))
            t.drain().then_inc(round_done, 1)

        def top_dve(v, r, d):
            with v.Fori(0, STEPS) as i:
                for half in range(2):
                    n = 2 * (STEPS * d + i) + half
                    v.wait_ge(used[half], base(r) + i)
                    c = bass.ds(i * SLOTS + half * GROUP, GROUP)
                    v.tensor_tensor(OHb[:, half * GROUP:(half + 1) * GROUP, :],
                                    iota[:, 0:P].unsqueeze(1).to_broadcast([P, GROUP, P]),
                                    key[:, d, c].unsqueeze(2).to_broadcast([P, GROUP, P]), ALU.not_equal) \
                        .then_inc(oh_ready, 1)
                    for j in range(GROUP):
                        v.wait_ge(masked_ready, n * GROUP + j + 1)
                        bank = (j % 4) * BANK
                        v.tensor_reduce(cmax[:, :, bass.ds(i * SLOTS + half * GROUP + j, 1)].rearrange("p h k -> p (h k)"),
                                        PS[:, bank:bank + BANK].rearrange("p (h e) -> p h e", h=HEADS), AX_X, ALU.max) \
                            .then_inc(reduced, 1)

        def flat(a):
            return a.rearrange("p h k -> p (h k)")

        def guard_dve(v, d):
            ct = chunk_tile[:, d, :]
            v.memset(reset[:, 0, 0:1], 0.0)
            v.memset(reset[:, 1, CHUNKS - 1:CHUNKS], 0.0)
            v.tensor_tensor(reset[:, 0, 1:CHUNKS], ct[:, 1:CHUNKS], ct[:, 0:CHUNKS - 1], ALU.not_equal)
            dve_link(v.tensor_tensor(reset[:, 1, 0:CHUNKS - 1], ct[:, 1:CHUNKS], ct[:, 0:CHUNKS - 1], ALU.not_equal))
            dve_link(v.tensor_scalar(reset, reset, NEG_BIG, None, ALU.mult))
            for hd in range(HEADS):
                v.tensor_tensor_scan(mr[:, hd, :], reset[:, 0, :], cmax[:, hd, :], NEG_BIG, ALU.add, ALU.max)
                last = v.tensor_tensor_scan(mr[:, HEADS + hd, ::-1], reset[:, 1, ::-1], cmax[:, hd, ::-1], NEG_BIG,
                                            ALU.add, ALU.max)
            dve_link(last)
            dve_link(v.tensor_tensor(cmax, mr[:, 0:HEADS, :], mr[:, HEADS:, :], ALU.max))
            v.wait_ge(recv_summed, d + 1)
            recv = PS[:, 0:4 * BANK].rearrange("p (h k) -> p h k", h=HEADS)[:, :, 0:CHUNKS]
            v.tensor_copy(mr[:, HEADS:, :], recv)
            dve_link(v.tensor_tensor(mr[:, 0:HEADS, :], recv, cmax, ALU.add))
            v.scalar_tensor_tensor(mr[:, 0:HEADS, :], mr[:, 0:HEADS, :], 0.2, mr[:, 0:HEADS, :], ALU.mult, ALU.max) \
                .then_inc(mr_ready, 1)
            v.tensor_tensor(sender, sE[:, :, 0:HEADS].rearrange("p k h -> p h k"),
                            sE[:, :, HEADS:2 * HEADS].rearrange("p k h -> p h k"), ALU.add).then_inc(mr_ready, 1)
            v.wait_ge(mr_ready, 2 * d + 2)
            dve_link(v.tensor_tensor(sender, sender, sE[:, :, 2 * HEADS:].rearrange("p k h -> p h k"), ALU.add))
            with v.Fori(0, STEPS) as i:
                for half in range(2):
                    n = 2 * (STEPS * d + i) + half
                    v.wait_ge(er_ready, n + 1)
                    c = bass.ds(i * SLOTS + half * GROUP, GROUP)
                    v.tensor_tensor(OH[:, half * GROUP:(half + 1) * GROUP, :],
                                    iota[:, 0:P].unsqueeze(1).to_broadcast([P, GROUP, P]),
                                    key[:, d, c].unsqueeze(2).to_broadcast([P, GROUP, P]), ALU.is_equal) \
                        .then_inc(oh_again, 1)
                    v.wait_ge(er_summed, n + 1)
                    at = (4 + half) * BANK
                    v.tensor_copy(er[:, :, c], PS[:, at:at + 8 * GROUP].rearrange("p (k q) -> p q k", q=8)) \
                        .then_inc(er_ready, 1)
            v.wait_ge(er_ready, 1 + 2 * STEPS * (d + 1))
            dve_link(v.tensor_tensor(ex, sender, er[:, HEADS:, :], ALU.add))
            dve_link(v.scalar_tensor_tensor(ex, ex, 0.2, ex, ALU.mult, ALU.max))
            dve_link(v.tensor_tensor(ex, ex, er[:, 0:HEADS, :], ALU.subtract))
            v.tensor_scalar(ex, ex, 0.0, None, ALU.min).then_inc(arg_ready, 1)

        def guard_pe(t, d):
            t.wait_ge(reduced, 4 + CHUNKS * (d + 1))
            for hd in range(HEADS):
                last = t.matmul(PS[:, hd * BANK:hd * BANK + CHUNKS], rT[:, d, hd, :], tile_sel[:, d, :],
                                start=True, stop=True)
            last.then_inc(recv_summed, 1)
            t.wait_ge(mr_ready, 2 * d + 2)
            with t.Fori(0, STEPS) as i:
                for half in range(2):
                    n = 2 * (STEPS * d + i) + half
                    t.wait_ge(oh_again, n + 1)
                    for j in range(GROUP):
                        at = 2 * half * BANK + j * P
                        last = t.transpose(PS[:, at:at + P], OH[:, half * GROUP + j, :], ident)
                    last.then_inc(ohT_summed, 1)
                    t.wait_ge(ohT_ready, n + 1)
                    for j in range(GROUP):
                        at = (4 + half) * BANK + 8 * j
                        k = bass.ds(i * SLOTS + half * GROUP + j, 1)
                        last = t.matmul(PS[:, at:at + 8], G[:, half * GROUP + j, :],
                                        mr[:, :, k].rearrange("p q k -> p (q k)"), start=True, stop=True)
                    last.then_inc(er_summed, 1)

        def guard_act(a, d):
            with a.Fori(0, STEPS) as i:
                for half in range(2):
                    n = 2 * (STEPS * d + i) + half
                    a.wait_ge(ohT_summed, n + 1)
                    at = 2 * half * BANK
                    a.copy(G[:, half * GROUP:(half + 1) * GROUP, :],
                           PS[:, at:at + GROUP * P].rearrange("p (j e) -> p j e", j=GROUP)).then_inc(ohT_ready, 1)
            a.wait_ge(arg_ready, d + 1)
            a.activation(ex, ex, ACT.Exp).then_inc(ex_ready, 1)

        def weighted_dve(v, r, d):
            v.wait_ge(ex_ready, d + 1)
            with v.Fori(0, STEPS) as i:
                for half in range(2):
                    v.wait_ge(used[half], base(r) + i)
                    c = bass.ds(i * SLOTS + half * GROUP, GROUP)
                    v.tensor_tensor(OH[:, half * GROUP:(half + 1) * GROUP, :],
                                    iota[:, 0:P].unsqueeze(1).to_broadcast([P, GROUP, P]),
                                    key[:, d, c].unsqueeze(2).to_broadcast([P, GROUP, P]), ALU.is_equal) \
                        .then_inc(oh_ready, 1)
                    for j in range(GROUP):
                        v.wait_ge(landed[half * GROUP + j], 16 * (base(r) + i + 1))
                    g = G[:, half * GROUP:(half + 1) * GROUP, :].rearrange("p j (h f) -> p j h f", h=HEADS)
                    v.tensor_tensor(g, g, ex[:, :, c].rearrange("p h k -> p k h").unsqueeze(3)
                                    .to_broadcast([P, GROUP, HEADS, HD]), ALU.mult).then_inc(scaled_ready, 1)

        def weighted_pe(t, r, d):
            clear_psum(t)
            with t.Fori(0, STEPS) as i:
                for half in range(2):
                    tiles = load_tiles(t, d, i, half)
                    t.wait_ge(scaled_ready, 2 * (STEPS * d + i) + half + 1)
                    for j in range(GROUP):
                        s = half * GROUP + j
                        add_to(t, PS[:, bass.ds(tiles[j] * P, P)], OH[:, s, :], G[:, s, :])
                        k = bass.ds(i * SLOTS + s, 1)
                        last = add_to(t, PS[:, bass.ds(tiles[j] * HEADS + DEG_COL, HEADS)], OH[:, s, :],
                                      ex[:, :, k].rearrange("p h k -> p (h k)"))
                    last.then_inc(used[half], 1)
            for half in range(2):
                t.wait_ge(used[half], base(r + 1))
            t.drain().then_inc(round_done, 1)

        def weighted_out_dve(v, r, d):
            v.wait_ge(round_done, r + 1)
            n = TILES * HEADS
            den = rden[:, 0, :]
            dve_link(v.tensor_scalar(den, PS[:, DEG_COL:DEG_COL + n], 1e-8, None, ALU.add))
            dve_link(v.reciprocal(rden[:, 1, :], den))
            hv = h[:, :, :].rearrange("p t (h f) -> p (t h) f", h=HEADS)
            dve_link(v.tensor_tensor(hv, PS[:, 0:NP_].rearrange("p (n f) -> p n f", f=HD),
                                     rden[:, 1, :].unsqueeze(2).to_broadcast([P, n, HD]), ALU.mult))
            dve_link(v.tensor_tensor(comb, comb, h[:, :, :], ALU.add))
            v.nop().then_inc(den_ready, 1)

        elu_done = sem("elu_done")
        table = {n: sem(f"table_{n}") for n in ("h0", "h1", "g0", "g1", "h2", "proj", "sc")}
        clipped = sem("clipped")
        rden = sb("rden", [P, 2, TILES * HEADS])
        rowsum = sb("rowsum", [P, D])

        def table_rows(name):
            return T[name].rearrange("(t p) f -> p t f", p=P)

        @block.sync
        def _(sp):
            sp.dma_start(e_i[:, :, :], edges.rearrange("k (p j) -> p k j", p=EP)).then_inc(loaded_edges, 16)
            sp.dma_start(cst[:, :], consts).then_inc(loaded_consts, 16)
            sp.wait_ge(x_cleared, 1)
            with sp.Fori(0, TILES - 1) as i:
                sp.dma_start(x[:, bass.ds(i, 1), :].rearrange("p t f -> p (t f)"), x_in[bass.ds(i * P, P), :]) \
                    .then_inc(loaded_x, 16)
            sp.dma_start(x[0:TAIL, TILES - 1, :], x_in[(TILES - 1) * P:N_NODES, :]).then_inc(loaded_x, 16)
            sp.dma_start(W[:, :], weights).then_inc(loaded_w, 16)
            sp.dma_start(bcol[:, :], bias_cols).then_inc(loaded_b, 16)
            sp.dma_start(brow[:, :, :], bias_rows.unsqueeze(0).to_broadcast([P, ROWS, D])).then_inc(loaded_b, 16)
            sp.dma_start(attn_sb[:, :], attn).then_inc(loaded_b, 16)
            sp.wait_ge(h_ready, 1)
            sp.dma_start(table_rows("h0"), h[:, :, :]).then_inc(table["h0"], 16)
            sp.wait_ge(h_ready, 2)
            sp.dma_start(table_rows("h1"), h[:, :, :]).then_inc(table["h1"], 16)
            sp.wait_ge(h1_ready, 1)
            sp.dma_start(table_rows("g0"), h[:, :, :]).then_inc(table["g0"], 16)
            sp.wait_ge(h1_ready, 2)
            sp.dma_start(table_rows("g1"), h1N).then_inc(table["g1"], 16)
            sp.wait_ge(h_ready, 3)
            sp.dma_start(table_rows("h2"), h[:, :, :]).then_inc(table["h2"], 16)
            sp.wait_ge(proj_ready, 1)
            sp.dma_start(table_rows("proj"), h[:, :, :]).then_inc(table["proj"], 16)
            sp.wait_ge(parts_ready, 1)
            for d in range(2):
                sp.dma_start(T_sc[d].rearrange("(t p) f -> p t f", p=P), parts[:, d, :, :]).then_inc(table["sc"], 16)
            sp.wait_ge(x_final, 1)
            sp.dma_start(out[0:(TILES - 1) * P, :].rearrange("(t p) f -> p t f", p=P), x[:, 0:TILES - 1, :]) \
                .then_inc(stored, 16)
            sp.dma_start(out[(TILES - 1) * P:N_NODES, :], x[0:TAIL, TILES - 1, :]).then_inc(stored, 16)
            sp.wait_ge(stored, 32)

        @block.gpsimd
        def _(p):
            p.memset(x[:, TILES - 1, :], 0.0).then_inc(x_cleared, 1)
            p.memset(zeros[:, :], 0.0)
            p.memset(sT[:, :, :], 0.0)
            p.memset(eps[:, :], 1e-5).then_inc(zeros_ready, 1)
            for r, name in enumerate(("h0", "h1", "g0", "g1", "h2")):
                p.wait_ge(table[name], 16)
                round_pool(p, r, T[name])
            p.wait_ge(table["proj"], 16)
            p.wait_ge(table["sc"], 32)
            for d in range(2):
                round_pool(p, 5 + 2 * d, T_sc[d], SPLIT * HEADS)
                round_pool(p, 6 + 2 * d, T["proj"])

        @block.vector
        def _(v):
            v.wait_ge(loaded_edges, 16)
            v.wait_ge(loaded_consts, 16)
            dve_link(v.tensor_copy(iota_h[:, :], iota))
            dve_link(v.tensor_scalar(big_id[:, :], ident, NEG_BIG, None, ALU.mult))
            dve_link(v.tensor_copy(pick[:, :, :], cst[:, C_PICK:C_ALL].rearrange("p (h m) -> p h m", h=HEADS)))
            v.wait_ge(loaded_x, 16 * TILES)
            v.wait_ge(zeros_ready, 1)
            norm_dve(v, 0, True)
            v.wait_ge(hT_ready, 1)
            for d in range(2):
                sort_dve(v, d)
            v.wait_ge(loaded_b, 48)
            dve_link(v.tensor_scalar(bcol_m1[:, :], bcol[:, :], -1.0, None, ALU.add))
            dve_link(v.tensor_tensor(rowsum[:, :], brow[:, ROW["L2_self"], :], brow[:, ROW["L2_nei"], :], ALU.add))

            def row(a):
                return a.unsqueeze(1).to_broadcast([P, TILES, D])

            ps3 = PS[:, 0:NP_].rearrange("p (t f) -> p t f", t=TILES)
            round_dve(v, 0, 0)
            agg_dve(v, 0, aggT, 1, True)
            v.wait_ge(square_ready, 1)
            dve_link(v.tensor_reduce(st[:, 6, :], h[:, :, :], AX_X, ALU.add))
            v.nop().then_inc(sumsq_ready, 1)
            v.wait_ge(len_ready, 1)
            dve_link(v.tensor_scalar(st[:, 7, :], st[:, 7, :], 1e-12, None, ALU.max))
            dve_link(v.reciprocal(st[:, 6, :], st[:, 7, :]))
            dve_link(v.tensor_tensor(h[:, :, :], ps3, bc(st[:, 6, :], D), ALU.mult))
            dve_link(v.tensor_tensor(x[:, :, :], x[:, :, :], h[:, :, :], ALU.add))
            norm_dve(v, 1, True)
            v.wait_ge(hT_ready, 2)
            round_dve(v, 1, 0)
            agg_dve(v, 1, aggT, 0, True)
            v.sem_inc(act_done, 2)
            sage1_dve(v)
            v.wait_ge(h1_ready, 2)
            for k in range(2):
                round_dve(v, 2 + k, 0)
                v.wait_ge(table["g1"], 16)
                agg_dve(v, 2 + k, agg2T[:, k, :], 0, True)
            chain_dve(v)
            v.wait_ge(fc3_summed, 1)
            v.tensor_tensor(h[:, :, :], ps3, row(brow[:, ROW["fc3"], :]), ALU.add).then_inc(z_ready, 1)
            v.wait_ge(log_ready, 1)
            dve_link(v.scalar_tensor_tensor(h[:, :, :], h[:, :, :], 0.0, scr, ALU.max, ALU.add))
            dve_link(v.tensor_tensor(x[:, :, :], x[:, :, :], h[:, :, :], ALU.add))
            norm_dve(v, 2, True)
            v.wait_ge(hT_ready, 3)
            round_dve(v, 4, 1)
            agg_dve(v, 4, aggT, 2, False)
            v.wait_ge(out2_summed, 1)
            dve_link(v.tensor_tensor(h[:, :, :], ps3, row(rowsum[:, :]), ALU.add))
            dve_link(v.scalar_tensor_tensor(x[:, :, :], h[:, :, :], 0.0, x[:, :, :], ALU.max, ALU.add))
            norm_dve(v, 3, True)
            v.wait_ge(hT_ready, 4)
            v.wait_ge(score_summed, 1)
            dve_link(v.tensor_copy(score[:, :, :], PS[:, 7 * BANK:7 * BANK + TILES * SC]
                                   .rearrange("p (t c) -> p t c", t=TILES)))
            for d in range(2):
                rest = score[:, :, 8 * d:8 * d + HEADS]
                left = rden[:, 0, :].rearrange("p (t h) -> p t h", h=HEADS)
                ph = part_h[:, :].rearrange("p (t h) -> p t h", h=HEADS)
                for k in range(SPLIT):
                    part = parts[:, d, :, k * HEADS:(k + 1) * HEADS]
                    dve_link(v.tensor_copy(ph, rest))
                    dve_link(v.tensor_copy(part, ph))
                    if k < SPLIT - 1:
                        dve_link(v.tensor_tensor(left, rest, part, ALU.subtract))
                        rest = left
            v.nop().then_inc(parts_ready, 1)
            v.wait_ge(proj_summed, 1)
            v.tensor_copy(h[:, :, :], ps3).then_inc(proj_ready, 1)
            v.wait_ge(self_summed, 1)
            dve_link(v.tensor_tensor(comb, ps3, row(brow[:, ROW["L3_bias"], :]), ALU.add))
            v.nop().then_inc(self_ready, 1)
            v.wait_ge(rT_summed, 1)
            v.tensor_copy(rT[:, :, :, :], PS[0:TILES, 0:2 * HEADS * P].rearrange("p (d h e) -> p d h e", d=2, h=HEADS)) \
                .then_inc(rT_ready, 1)
            v.sem_inc(reduced, 4)
            v.sem_inc(er_ready, 1)
            for d in range(2):
                top_dve(v, 5 + 2 * d, d)
                v.wait_ge(round_done, 6 + 2 * d)
                guard_dve(v, d)
                weighted_dve(v, 6 + 2 * d, d)
                weighted_out_dve(v, 6 + 2 * d, d)
            dve_link(v.tensor_copy(h[:, :, :], comb))
            norm_dve(v, 4, False)
            dve_link(v.tensor_tensor(h[:, :, :], h[:, :, :], row(brow[:, ROW["gamma"], :]), ALU.mult))
            dve_link(v.tensor_tensor(h[:, :, :], h[:, :, :], row(brow[:, ROW["beta"], :]), ALU.add))
            v.tensor_tensor(x[:, :, :], x[:, :, :], h[:, :, :], ALU.add).then_inc(x_final, 1)

        @block.tensor
        def _(t):
            t.wait_ge(loaded_consts, 16)
            t.wait_ge(zeros_ready, 1)
            t.wait_ge(loaded_w, 16)
            t.wait_ge(loaded_b, 48)
            t.matmul(PS[:, 7 * BANK:7 * BANK + SC], wt("L3_WT"), attn_sb[:, :], start=True, stop=True) \
                .then_inc(wx_summed, 1)

            def h_tile(k):
                return h[:, k, :]

            t.wait_ge(h_ready, 1)
            transposes_pe(t, h_tile, hT_summed)
            t.wait_ge(hT_ready, 1)
            for d in range(2):
                sort_pe(t, d)
            t.wait_ge(sorted_ready, 2)
            round_pe(t, 0, 0, True)
            rdeg_pe(t, 1)
            t.wait_ge(agg_ready, 1)
            node_major(t, [(hT, wt("L0_lin")), (aggT, wt("L0_agg"))], out0_summed)
            t.wait_ge(h_ready, 2)
            transposes_pe(t, h_tile, hT_summed)
            t.wait_ge(hT_ready, 2)
            round_pe(t, 1, 0, False)
            t.wait_ge(agg_ready, 2)
            sage1_pe(t)
            for k in range(2):
                t.wait_ge(act_done, 10)
                if k:
                    t.wait_ge(h1_ready, k)
                transposes_pe(t, lambda n: h1T[:, k, n * P:(n + 1) * P], h1_transposed)
            t.wait_ge(h1_ready, 2)
            for k in range(2):
                round_pe(t, 2 + k, 0, False)
                t.wait_ge(agg_ready, 3 + k)
            chain_pe(t)
            t.wait_ge(act_done, 10 + 6 * PAIRS)
            node_major(t, [(agg2T[:, 0, :], wt("fc3", 0)), (agg2T[:, 1, :], wt("fc3", D))], fc3_summed)
            t.wait_ge(h_ready, 3)
            transposes_pe(t, h_tile, hT_summed)
            t.wait_ge(hT_ready, 3)
            round_pe(t, 4, 1, True)
            rdeg_pe(t, 2)
            t.wait_ge(agg_ready, 5)
            node_major(t, [(hT, wt("L2_self")), (aggT, wt("L2_nei"))], out2_summed)
            t.wait_ge(h_ready, 4)
            transposes_pe(t, h_tile, hT_summed)
            t.wait_ge(hT_ready, 4)
            t.wait_ge(wx_ready, 1)
            for k in range(TILES):
                last = t.matmul(PS[:, 7 * BANK + k * SC:7 * BANK + (k + 1) * SC], hT[:, k * P:(k + 1) * P], Wx[:, :],
                                start=True, stop=True)
            last.then_inc(score_summed, 1)
            node_major(t, [(hT, wt("L3_W"))], proj_summed)
            t.wait_ge(proj_ready, 1)
            node_major(t, [(hT, wt("L3_self"))], self_summed)
            t.wait_ge(self_ready, 1)
            for d in range(2):
                for hd in range(HEADS):
                    at = (d * HEADS + hd) * P
                    last = t.transpose(PS[0:TILES, at:at + P], score[:, :, 8 * d + HEADS + hd], ident)
            last.then_inc(rT_summed, 1)
            t.wait_ge(rT_ready, 1)
            for d in range(2):
                top_pe(t, 5 + 2 * d, d)
                guard_pe(t, d)
                t.wait_ge(ex_ready, d + 1)
                weighted_pe(t, 6 + 2 * d, d)
                t.wait_ge(den_ready, d + 1)

        @block.scalar
        def _(a):
            def copy_hT(n):
                a.wait_ge(hT_summed, n)
                a.copy(hT[:, :], PS[:, 0:NP_]).then_inc(hT_ready, 1)

            a.wait_ge(wx_summed, 1)
            a.copy(Wx[:, :], PS[:, 7 * BANK:7 * BANK + SC]).then_inc(wx_ready, 1)
            norm_act(a, 0)
            copy_hT(1)
            a.wait_ge(sorted_ready, 2)
            round_act(a, 0, 0)
            a.wait_ge(out0_summed, 1)
            a.activation(h[:, :, :], PS[:, 0:NP_].rearrange("p (t f) -> p t f", t=TILES), ACT.Square) \
                .then_inc(square_ready, 1)
            a.wait_ge(sumsq_ready, 1)
            a.activation(st[:, 7, :], st[:, 6, :], ACT.Sqrt).then_inc(len_ready, 1)
            norm_act(a, 1)
            copy_hT(2)
            round_act(a, 1, 0)
            sage1_act(a)
            for k in range(2):
                a.wait_ge(h1_transposed, k + 1)
                a.copy(h[:, :, :] if k == 0 else h1N, PS[:, 0:NP_].rearrange("p (t f) -> p t f", t=TILES)) \
                    .then_inc(h1_ready, 1)
            for k in range(2):
                round_act(a, 2 + k, 0)
            chain_act(a)
            a.wait_ge(z_ready, 1)
            act_link(a.activation(scr, h[:, :, :], ACT.Abs))
            act_link(a.activation(scr, scr, ACT.Exp, scale=-1.0))
            a.activation(scr, scr, ACT.Ln, bias=1.0).then_inc(log_ready, 1)
            norm_act(a, 2)
            copy_hT(3)
            round_act(a, 4, 1)
            norm_act(a, 3)
            copy_hT(4)
            a.wait_ge(rT_ready, 1)
            for d in range(2):
                top_act(a, 5 + 2 * d, d)
                guard_act(a, d)
                round_act(a, 6 + 2 * d, d)
            norm_act(a, 4)


def pack_consts():
    c = np.zeros((P, C_ALL), np.float32)
    c[:, C_ID:C_ID + P] = np.eye(P)
    c[:, C_TRI:C_TRI + P] = np.triu(np.ones((P, P)), 1)
    c[:, C_TRII:C_TRII + P] = np.triu(np.ones((P, P)), 0)
    c[:, C_IOTA:C_IOTA + CHUNKS] = np.arange(CHUNKS)
    c[:, C_ONE:C_ONE + P] = 1.0
    c[:TILES - 1, C_MASK] = -1.0
    for part in range(SPLIT):
        for hd in range(HEADS):
            c[part * HEADS + hd, C_PICK + hd * P:C_PICK + (hd + 1) * P] = 1.0
    return c


def pack_weights(g):
    def tr(w):
        wt = np.asarray(w).T
        return [wt[k:k + P] for k in range(0, wt.shape[0], P)]

    blocks = {"L0_lin": tr(g("L0_gnn_W_lin")), "L0_agg": tr(g("L0_gnn_W_agg")), "l1": tr(g("L1_gnn_W_l1")),
              "r1": tr(g("L1_gnn_W_r1")), "l2": tr(g("L1_gnn_W_l2")), "r2": tr(g("L1_gnn_W_r2")),
              "res1": tr(g("L1_gnn_res1_W")), "res2": tr(g("L1_gnn_res2_W")), "fc1": tr(g("L1_gnn_fc1_W")),
              "fc2": tr(g("L1_gnn_fc2_W")), "fc3": tr(g("L1_gnn_fc3_W")), "L2_self": tr(g("L2_gnn_W_self")),
              "L2_nei": tr(g("L2_gnn_W_nei")), "L3_W": [g("L3_gnn_W")], "L3_self": [g("L3_gnn_W_self")],
              "L3_WT": [g("L3_gnn_W").T]}
    return np.concatenate([b for n, _ in _W for b in blocks[n]], axis=1)


def pack_bias_cols(g):
    names = {"b_l1": "b_l1", "b_l2": "b_l2", "res1": "res1_b", "res2": "res2_b", "fc1": "fc1_b", "fc2": "fc2_b"}
    c = np.zeros((P, B_ALL), np.float32)
    for n, at in BCOL.items():
        c[:, at:at + 2] = g("L1_gnn_" + names[n]).reshape(2, P).T
    return c


def pack_attn(g):
    c = np.zeros((P, SC), np.float32)
    for d, name in enumerate(("L3_gnn_a_in", "L3_gnn_a_out")):
        for role in range(2):
            for hd in range(HEADS):
                c[hd * HD:(hd + 1) * HD, d * 8 + role * HEADS + hd] = g(name)[hd, role * HD:(role + 1) * HD]
    return c


def kernel(**inp):
    import concourse.bacc as bacc
    from concourse.bass_utils import run_bass_kernel_spmd

    def g(name):
        return np.asarray(inp[name])

    nc = bacc.Bacc("TRN2", target_bir_lowering=False, num_devices=1)
    rows = ["L1_gnn_fc3_b", "L2_gnn_b_self", "L2_gnn_b_nei", "L3_gnn_bias", "L3_gnn_ln_gamma", "L3_gnn_ln_beta"]
    arrays = {"edges": np.stack([g("src"), g("dst")]), "x_in": g("x"), "consts": pack_consts(),
              "weights": pack_weights(g), "bias_cols": pack_bias_cols(g), "bias_rows": np.stack([g(n) for n in rows]),
              "attn": pack_attn(g)}
    ap = {n: nc.dram_tensor(n, a.shape, mybir.dt.from_np(a.dtype), kind="ExternalInput").ap()
          for n, a in arrays.items()}
    out = nc.dram_tensor("out", [N_NODES, D], F32, kind="ExternalOutput").ap()
    gnn_kernel(nc, *ap.values(), out)
    r = run_bass_kernel_spmd(nc, [arrays], core_ids=[0])
    return r.results[0]["out"]
```

```python
from contextlib import ExitStack

import numpy as np
import concourse.bass as bass
from concourse import mybir

F32 = mybir.dt.float32
F16 = mybir.dt.float16
BF16 = mybir.dt.bfloat16
I32 = mybir.dt.int32
ALU = mybir.AluOpType
ACT = mybir.ActivationFunctionType
AX_X = mybir.AxisListType.X

P = 128
N_NODES, N_EDGES, D = 3125, 50000, 128
TILES = -(-N_NODES // P)
NP_ = TILES * P
TAIL = N_NODES - (TILES - 1) * P
EP = 125
EC = N_EDGES // EP
GROUP = 8
CHUNKS = -(-(N_EDGES // P + TILES) // (2 * GROUP)) * 2 * GROUP
STEPS = CHUNKS // (2 * GROUP)
SLOTS = 2 * GROUP
QUAD = 4
GROUPS = 2 * STEPS
LAP = 4
LAPS = GROUPS // LAP
AHEAD_OH, AHEAD_T = 3, 2
BLK = 400
NBLK = NP_ // BLK
HEADS, HD = 4, 32
H1 = 256
SC = 4 * HEADS
SPLIT = 3
ROW_ATT = D + SPLIT * HEADS
RING1 = 3
NEG_BIG = -float(2.0 ** 100)
BANK = 512
DEG_COL = NP_

C_ID, C_TRI, C_TRII, C_IOTA, C_ONE, C_MASK = 0, 128, 256, 384, 384 + CHUNKS, 384 + CHUNKS + 128
C_PICK = C_MASK + 1
C_ALL = C_PICK + HEADS * P

_W = [("L0_lin", D), ("L0_agg", D), ("l1", H1), ("r1", H1), ("l2", 2 * H1), ("r2", 2 * H1), ("res1", H1),
      ("res2", H1), ("fc1", 2 * H1), ("fc2", 2 * H1), ("fc3", 2 * D), ("L2_self", D), ("L2_nei", D),
      ("L3_W", D), ("L3_self", D), ("L3_WT", D)]
W_AT = {}
_at = 0
for _n, _c in _W:
    W_AT[_n] = _at
    _at += _c
W_ALL = _at
BCOL = {"b_l1": 0, "b_l2": 2, "res1": 4, "res2": 6, "fc1": 8, "fc2": 10}
B_ALL = 12
ROW = {"fc3": 0, "L2_self": 1, "L2_nei": 2, "L3_bias": 3, "gamma": 4, "beta": 5}
ROWS = 6


def linker(eng, sem):
    count = [0]

    def link(ins):
        count[0] += 1
        ins.then_inc(sem, 1)
        eng.wait_ge(sem, count[0])

    return link


def gnn_kernel(nc, edges, x_in, consts, weights, bias_cols, bias_rows, attn, out, dbg=None):
    with ExitStack() as ctx:
        def sb(name, shape, dt=F32):
            return ctx.enter_context(nc.sbuf_tensor(name, shape, dt))

        def sem(name):
            return ctx.enter_context(nc.semaphore(name))

        def dram(name, shape):
            return nc.dram_tensor(name, shape, F32, kind="Internal").ap()

        PS = ctx.enter_context(nc.psum_tensor("PS", [P, 8 * BANK], F32))
        cst = sb("cst", [P, C_ALL])
        ident, tri, tri_incl = cst[:, C_ID:C_ID + P], cst[:, C_TRI:C_TRI + P], cst[:, C_TRII:C_TRII + P]
        iota = cst[:, C_IOTA:C_IOTA + CHUNKS]
        ones = cst[:, C_ONE:C_ONE + P]
        neg_mask = cst[:, C_MASK:C_MASK + 1]
        W = sb("W", [P, W_ALL])
        bcol = sb("bcol", [P, B_ALL])
        brow = sb("brow", [P, ROWS, D])
        x = sb("x", [P, TILES, D])
        h = sb("h", [P, TILES, D])
        hT = sb("hT", [P, NP_])
        big = sb("big", [P, 16000])
        rdeg = sb("rdeg", [P, NP_])
        idx = sb("idx", [P, 2, CHUNKS], I32)
        key = sb("key", [P, 2, CHUNKS])
        tile_off = sb("tile_off", [1, 2, CHUNKS], I32)
        tile_sel = sb("tile_sel", [TILES, 2, CHUNKS])
        G = sb("G", [P, SLOTS, D + SPLIT * HEADS])
        OH = sb("OH", [P, SLOTS, P])
        G_flat = G[:, :, :].rearrange("p s f -> p (s f)")
        narrow = [G[:, s, 0:D] for s in range(SLOTS)]
        aggT = big[:, 12800:16000]
        scr = big[:, 12800:16000].rearrange("p (t f) -> p t f", t=TILES)
        h1T = big[:, 0:6400].rearrange("p (c n) -> p c n", c=2)
        agg2T = big[:, 6400:12800].rearrange("p (c n) -> p c n", c=2)
        h1N = agg2T[:, 0, :].rearrange("p (t f) -> p t f", t=TILES)
        bcol_m1 = sb("bcol_m1", [P, B_ALL])
        chunk_tile = sb("chunk_tile", [P, 2, CHUNKS])
        attn_sb = sb("attn_sb", [P, SC])
        Wx = sb("Wx", [P, SC])
        score = sb("score", [P, TILES, SC])
        parts = sb("parts", [P, 2, TILES, SPLIT * HEADS])
        rT = sb("rT", [TILES, 2, HEADS, P])
        pick = sb("pick", [P, HEADS, P], BF16)
        big_id = sb("big_id", [P, P], BF16)
        sT = sb("sT", [P, SLOTS, P], BF16)
        part_h = sb("part_h", [P, TILES * HEADS], BF16)
        comb = rdeg[:, :].rearrange("p (t f) -> p t f", t=TILES)
        mrb = big[:, 0:4992].bitcast(BF16).rearrange("p (s q k) -> p s q k", s=SPLIT, q=2 * HEADS)
        ohT = G[:, :, :].rearrange("p s f -> p (s f)")[:, 0:LAP * GROUP * P // 2].bitcast(BF16) \
            .rearrange("p (g j e) -> p g j e", g=LAP, j=GROUP)
        RING2 = LAP
        ring2 = big[:, 0:RING2 * GROUP * D].rearrange("p (b j f) -> p b j f", b=RING2, j=GROUP)
        cmax = big[:, 4992:6656].rearrange("p (h k) -> p h k", h=HEADS)
        mr = big[:, 6656:9984].rearrange("p (q k) -> p q k", q=2 * HEADS)
        er = big[:, 9984:13312].rearrange("p (q k) -> p q k", q=2 * HEADS)
        ex = big[:, 13312:14976].rearrange("p (h k) -> p h k", h=HEADS)
        exb = big[:, 9984:12480].bitcast(BF16).rearrange("p (s h k) -> p s h k", s=SPLIT, h=HEADS)
        ex_rest = big[:, 6656:6656 + HEADS * CHUNKS].rearrange("p (h k) -> p h k", h=HEADS)
        sender = hT[:, 0:1664].rearrange("p (h k) -> p h k", h=HEADS)
        reset = hT[:, 1664:1664 + 2 * CHUNKS].rearrange("p (a k) -> p a k", a=2)
        eq = OH[:, :, :].rearrange("p s e -> p (s e)").bitcast(BF16).rearrange("p (g j e) -> p g j e", g=LAP, j=GROUP)
        OHb = OH[:, :, :].bitcast(BF16)[:, :, 0:P]
        idxbuf = sb("idxbuf", [P, 2, GROUP], I32)
        score_buf = sb("score_buf", [P, 2, GROUP, SPLIT * HEADS], BF16)
        exs = sb("exs", [P, 2, GROUP, SPLIT * HEADS], BF16)
        idxbuf1 = sb("idxbuf1", [P, RING1, GROUP], I32)
        zeros = sb("zeros", [P, BANK], BF16)
        st = sb("st", [P, 8, TILES])
        eps = sb("eps", [P, 2])

        masks = big[0:EP, 0:TILES * EC // 2].bitcast(BF16)
        scan = big[0:EP, TILES * EC // 2:TILES * EC // 2 * 3]
        scan_cmp = big[0:TILES, 15000:15000 + 2 * CHUNKS].rearrange("p (a b) -> p a b", a=2)
        cmp_i = big[:, 2048:2048 + 2 * CHUNKS].bitcast(I32).rearrange("p (a b) -> p a b", a=2)
        e_i = sb("e_i", [EP, 2, EC], I32)
        h_cols = h[0:EP, :, :].rearrange("p t f -> p (t f)")
        ev_i = h_cols[:, 0:3 * EC].bitcast(I32).rearrange("p (a b) -> p a b", a=3)
        tl = h_cols[:, 3 * EC:4 * EC]
        sort_v = big[0:EP, 0:4 * EC].rearrange("p (a b) -> p a b", a=4)
        lo_keep = big[:, 4 * EC:4 * EC + CHUNKS]
        cnt = sb("cnt", [P, 6, TILES])
        cnt_i = sb("cnt_i", [P, 2, TILES], I32)
        col = sb("col", [TILES, 4])
        col_i = sb("col_i", [TILES, 2], I32)
        iota_h = sb("iota_h", [P, CHUNKS], F16)
        U = 5
        work = sb("work", [P, max(U * (CHUNKS + 2 * P), 8 * BLK)])
        W_flat = W[:, 0:CHUNKS * SPLIT * HEADS // 2]
        sE = [a.bitcast(BF16).rearrange("p (k c) -> p k c", c=SPLIT * HEADS)
              for a in (h[:, :, :].rearrange("p t f -> p (t f)")[:, 0:CHUNKS * SPLIT * HEADS // 2], W_flat)]
        ring1 = work[:, 0:RING1 * GROUP * ROW_ATT].rearrange("p (b j f) -> p b j f", b=RING1, j=GROUP)
        OHw = G_flat[:, 0:GROUP * P].bitcast(BF16).rearrange("p (g j e) -> p g j e", g=2, j=GROUP)
        A = work[0:EP, 0:U * CHUNKS].bitcast(F16).rearrange("p (g j c) -> p g j c", g=2, j=U)
        B = work[0:EP, U * CHUNKS:U * (CHUNKS + 2 * P)].bitcast(F16).rearrange("p (g j k c) -> p g j k c", g=2, j=U, k=2)
        wide = [(G_flat if s < GROUP else work)[:, s % GROUP * H1:(s % GROUP + 1) * H1] for s in range(SLOTS)]
        blk = work[:, 0:8 * BLK].rearrange("p (x o c n) -> p x o c n", x=2, o=2, c=2)

        T = {n: dram(f"T_{n}", [NP_, w]) for n, w in (("h0", D), ("h1", D), ("g", H1), ("h2", D))}
        T_att = [dram(f"T_att{d}", [NP_, D + SPLIT * HEADS]) for d in range(2)]
        spill = [dram(f"spill{d}", [P, CHUNKS * D]) for d in range(2)]

        loaded_edges = sem("loaded_edges")
        loaded_consts = sem("loaded_consts")
        loaded_x = sem("loaded_x")
        loaded_w = sem("loaded_w")
        loaded_b = sem("loaded_b")
        dve_step = sem("dve_step")
        act_step = sem("act_step")
        zeros_ready = sem("zeros_ready")
        x_cleared = sem("x_cleared")
        counts_ready = sem("counts_ready")
        counts_summed = sem("counts_summed")
        chunks_ready = sem("chunks_ready")
        chunks_summed = sem("chunks_summed")
        bounds_ready = sem("bounds_ready")
        tiles_summed = sem("tiles_summed")
        where_ready = sem("where_ready")
        perm_used = sem("perm_used")
        perm_done = sem("perm_done")
        sorted_ready = sem("sorted_ready")
        table_ready = sem("table_ready")
        table_stored = sem("table_stored")
        idx_ready = sem("idx_ready")
        landed = [sem(f"landed{i}") for i in range(SLOTS)]
        oh_ready = sem("oh_ready")
        used = [sem(f"used{i}") for i in range(2)]
        round_done = sem("round_done")
        gathers_begun = sem("gathers_begun")
        var_ready = sem("var_ready")
        std_ready = sem("std_ready")
        h_ready = sem("h_ready")
        hT_summed = sem("hT_summed")
        hT_ready = sem("hT_ready")
        diag_ready = sem("diag_ready")
        rdeg_summed = sem("rdeg_summed")
        agg_ready = sem("agg_ready")
        wx_summed = sem("wx_summed")
        wx_ready = sem("wx_ready")
        out0_summed = sem("out0_summed")
        square_ready = sem("square_ready")
        sumsq_ready = sem("sumsq_ready")
        len_ready = sem("len_ready")
        lin_ready = sem("lin_ready")
        exp_ready = sem("exp_ready")
        act_done = sem("act_done")
        h1_transposed = sem("h1_transposed")
        h1_ready = sem("h1_ready")
        fc3_summed = sem("fc3_summed")
        z_ready = sem("z_ready")
        log_ready = sem("log_ready")
        out2_summed = sem("out2_summed")
        proj_summed = sem("proj_summed")
        proj_ready = sem("proj_ready")
        score_summed = sem("score_summed")
        self_summed = sem("self_summed")
        self_ready = sem("self_ready")
        parts_ready = sem("parts_ready")
        rT_summed = sem("rT_summed")
        rT_ready = sem("rT_ready")
        sT_summed = sem("sT_summed")
        sT_ready = sem("sT_ready")
        masked_ready = sem("masked_ready")
        reduced = sem("reduced")
        recv_summed = sem("recv_summed")
        mr_ready = sem("mr_ready")
        oh_again = sem("oh_again")
        turned = sem("turned")
        ohT_ready = sem("ohT_ready")
        er_summed = sem("er_summed")
        er_ready = sem("er_ready")
        arg_ready = sem("arg_ready")
        ex_ready = sem("ex_ready")
        scaled_ready = sem("scaled_ready")
        den_ready = sem("den_ready")
        x_final = sem("x_final")
        stored = sem("stored")

        dve_link = linker(nc.vector, dve_step)
        act_link = linker(nc.scalar, act_step)
        block = ctx.enter_context(nc.Block())

        COUNT, EARLIER, TOTAL, UPTO, TILE_AT = 7 * BANK, 7 * BANK + TILES, 7 * BANK + 50, 7 * BANK + 51, 7 * BANK + 96
        PASS_GROUPS = EC // U

        def place_dve(v, d, pause):
            k_i, o_i = e_i[:, 1 - d, :], e_i[:, d, :]
            a, b, lo, hi = (sort_v[:, i, :] for i in range(4))
            dve_link(v.tensor_scalar(ev_i[:, 0, :], k_i, 7, None, ALU.arith_shift_right))
            dve_link(v.tensor_copy(tl, ev_i[:, 0, :]))
            m3 = masks.rearrange("p (t j) -> p t j", t=TILES)
            s3 = scan.rearrange("p (t j) -> p t j", t=TILES)
            dve_link(v.tensor_tensor(m3, iota[0:EP, 0:TILES].unsqueeze(2).to_broadcast([EP, TILES, EC]),
                                     tl.unsqueeze(1).to_broadcast([EP, TILES, EC]), ALU.is_equal))
            pause(1)
            dve_link(v.tensor_tensor_scan(scan, masks, masks, 0.0, ALU.add, ALU.max))
            pause(2)
            end, n, before, first = (cnt[0:EP, i, :] for i in range(4))
            dve_link(v.tensor_copy(end, s3[:, :, EC - 1]))
            v.tensor_copy(before[:, 1:TILES], end[:, 0:TILES - 1])
            dve_link(v.memset(before[:, 0:1], 0.0))
            v.tensor_tensor(n, end, before, ALU.subtract).then_inc(counts_ready, 1)
            v.wait_ge(counts_summed, d + 1)
            totb = cnt[:, 5, :]
            dve_link(v.tensor_scalar(cnt_i[:, 0, :], PS[:, COUNT:COUNT + TILES], float(P - 1), None, ALU.add))
            dve_link(v.tensor_scalar(cnt_i[:, 1, :], cnt_i[:, 0, :], 7, None, ALU.arith_shift_right))
            dve_link(v.tensor_copy(totb, cnt_i[:, 1, :]))
            dve_link(v.tensor_tensor(before, PS[0:EP, EARLIER:EARLIER + TILES], before, ALU.subtract))
            dve_link(v.tensor_scalar(col_i[:, 0:1], PS[0:TILES, TOTAL:TOTAL + 1], float(P - 1), None, ALU.add))
            dve_link(v.tensor_scalar(col_i[:, 1:2], col_i[:, 0:1], 7, None, ALU.arith_shift_right))
            v.tensor_copy(col[:, 0:1], col_i[:, 1:2]).then_inc(chunks_ready, 1)
            v.wait_ge(chunks_summed, d + 1)
            dve_link(v.tensor_copy(col[:, 1:2], PS[0:TILES, UPTO:UPTO + 1]))
            dve_link(v.tensor_tensor(col[:, 2:3], col[:, 1:2], col[:, 0:1], ALU.subtract))
            past, since = scan_cmp[:, 0, :], scan_cmp[:, 1, :]
            v.tensor_scalar(past, iota[0:TILES, :], col[:, 1:2], None, ALU.is_ge).then_inc(bounds_ready, 1)
            v.wait_ge(bounds_ready, d + 1)
            dve_link(v.tensor_scalar(since, iota[0:TILES, :], col[:, 2:3], None, ALU.is_ge))
            dve_link(v.scalar_tensor_tensor(tile_sel[:, d, :], past, neg_mask[0:TILES, :], since, ALU.mult, ALU.add))
            v.wait_ge(tiles_summed, d + 1)
            v.tensor_copy(chunk_tile[:, d, :], PS[:, TILE_AT:TILE_AT + CHUNKS])
            dve_link(v.tensor_copy(tile_off[0:1, d, :], PS[0:1, TILE_AT:TILE_AT + CHUNKS]))
            dve_link(v.tensor_tensor_scan(cnt[:, 4, :], totb, totb, 0.0, ALU.add, ALU.max))
            dve_link(v.tensor_tensor(cnt[:, 3, :], cnt[:, 4, :], totb, ALU.subtract))
            dve_link(v.tensor_scalar(first, first, float(P), -1.0, ALU.mult, ALU.add))
            dve_link(v.tensor_tensor(first, first, before, ALU.add))
            dve_link(v.tensor_tensor(s3, s3, first.unsqueeze(2).to_broadcast([EP, TILES, EC]), ALU.add))
            pause(3)
            dve_link(v.tensor_tensor(s3, s3, m3, ALU.mult))
            pause(4)
            dve_link(v.tensor_reduce(tl, scan.rearrange("p (t j) -> p j t", t=TILES), AX_X, ALU.add))
            pause(5)
            dve_link(v.tensor_copy(ev_i[:, 0, :], tl))
            dve_link(v.tensor_scalar(ev_i[:, 1, :], ev_i[:, 0, :], 7, None, ALU.arith_shift_right))
            dve_link(v.tensor_scalar(ev_i[:, 2, :], ev_i[:, 0, :], P - 1, None, ALU.bitwise_and))
            dve_link(v.tensor_copy(a, ev_i[:, 1, :]))
            dve_link(v.tensor_copy(b, ev_i[:, 2, :]))
            dve_link(v.tensor_scalar(ev_i[:, 1, :], k_i, P - 1, None, ALU.bitwise_and))
            dve_link(v.tensor_scalar(ev_i[:, 2, :], o_i, 256.0, 1.0, ALU.mult, ALU.add))
            dve_link(v.tensor_tensor(ev_i[:, 0, :], ev_i[:, 1, :], ev_i[:, 2, :], ALU.add))
            dve_link(v.tensor_scalar(ev_i[:, 1, :], ev_i[:, 0, :], 1023, None, ALU.bitwise_and))
            dve_link(v.tensor_scalar(ev_i[:, 2, :], ev_i[:, 0, :], 10, None, ALU.arith_shift_right))
            dve_link(v.tensor_copy(lo, ev_i[:, 1, :]))
            dve_link(v.tensor_copy(hi, ev_i[:, 2, :]))

        def where_group(v, n, g, at, payloads, first=False):
            if not first:
                v.wait_ge(perm_used, n - 1)
            for j in range(U):
                c = bass.ds(at + j, 1)
                v.tensor_scalar(A[:, g, j, :], iota_h[0:EP, :], sort_v[:, 0, c], None, ALU.is_equal)
                for k in payloads:
                    last = v.tensor_scalar(B[:, g, j, k, :], iota_h[0:EP, 0:P], sort_v[:, 1, c], sort_v[:, 2 + k, c],
                                           ALU.is_equal, ALU.mult)
            last.then_inc(where_ready, 1)

        def perm_group(t, n, g, payloads, bank):
            t.wait_ge(where_ready, n + 1)
            for j in range(U):
                for k in payloads:
                    at = (bank + k) * BANK
                    last = t.matmul(PS[:, at:at + CHUNKS], B[:, g, j, k, :], A[:, g, j, :], start=False, stop=True,
                                    skip_group_check=True)
            last.then_inc(perm_used, 1)

        def clear_bank(t, k):
            t.matmul(PS[:, k * BANK:k * BANK + CHUNKS], zeros[:, 0:P], zeros[:, 0:CHUNKS], start=True, stop=False,
                     skip_group_check=True)

        def decode_dve(v, d, lo, hi):
            dve_link(v.scalar_tensor_tensor(cmp_i[:, 0, :], hi, 1024.0, lo, ALU.mult, ALU.add))
            dve_link(v.tensor_scalar(idx[:, d, :], cmp_i[:, 0, :], 8, None, ALU.arith_shift_right))
            dve_link(v.tensor_scalar(cmp_i[:, 1, :], cmp_i[:, 0, :], 255, None, ALU.bitwise_and))
            v.tensor_scalar(key[:, d, :], cmp_i[:, 1, :], -1.0, None, ALU.add).then_inc(sorted_ready, 1)

        def permute_dve(v):
            for g in range(2):
                where_group(v, g, g, g * U, (0, 1), first=True)
            with v.Fori(1, PASS_GROUPS // 2) as i:
                for g in range(2):
                    where_group(v, 2 * i + g, g, (2 * i + g) * U, (0, 1))
            v.wait_ge(perm_used, PASS_GROUPS)
            dve_link(v.tensor_copy(lo_keep, PS[:, 4 * BANK:4 * BANK + CHUNKS]))
            decode_dve(v, 0, lo_keep, PS[:, 5 * BANK:5 * BANK + CHUNKS])

        def permute_pe(t):
            for k in (4, 5):
                clear_bank(t, k)
            with t.Fori(0, PASS_GROUPS // 2) as i:
                for g in range(2):
                    perm_group(t, 2 * i + g, g, (0, 1), 4)

        def place_pe(t, d):
            t.wait_ge(counts_ready, d + 1)
            n = cnt[0:EP, 1, :]
            t.matmul(PS[:, COUNT:COUNT + TILES], ones[0:EP, :], n, start=True, stop=True)
            t.matmul(PS[0:EP, EARLIER:EARLIER + TILES], tri[0:EP, 0:EP], n, start=True, stop=True)
            t.matmul(PS[0:TILES, TOTAL:TOTAL + 1], n, ones[0:EP, 0:1], start=True, stop=True).then_inc(counts_summed, 1)
            t.wait_ge(chunks_ready, d + 1)
            t.matmul(PS[0:TILES, UPTO:UPTO + 1], tri_incl[0:TILES, 0:TILES], col[:, 0:1],
                     start=True, stop=True).then_inc(chunks_summed, 1)
            t.wait_ge(bounds_ready, d + 1)
            t.matmul(PS[:, TILE_AT:TILE_AT + CHUNKS], ones[0:TILES - 1, :], scan_cmp[0:TILES - 1, 0, :],
                     start=True, stop=True).then_inc(tiles_summed, 1)

        STEP_GROUPS = 4
        BEHIND = (STEPS - PASS_GROUPS // STEP_GROUPS, 1)

        def base(r):
            return r * STEPS

        def round_act(a, r, d):
            def step(i, half, first):
                if r or not first:
                    a.wait_ge(used[half], base(r) + i)
                c = bass.ds(i * SLOTS + half * GROUP, GROUP)
                a.copy(idxbuf[:, half, :], idx[:, d, c]).then_inc(idx_ready, 1)

            for half in range(2):
                step(0, half, True)
            with a.Fori(1, STEPS) as i:
                for half in range(2):
                    step(i, half, False)

        def round_pool(p, r, table, slots):
            def step(i):
                for half in range(2):
                    p.wait_ge(idx_ready, 2 * (base(r) + i) + half + 1)
                    p.sem_inc(gathers_begun)
                    for j in range(GROUP):
                        s = half * GROUP + j
                        p.indirect_dma_start(out=slots[s], out_offset=None, in_=table[:, :],
                                             in_offset=bass.IndirectOffsetOnAxis(ap=idxbuf[:, half, j:j + 1], axis=0)) \
                            .then_inc(landed[s], 16)

            with p.Fori(0, STEPS) as i:
                step(i)

        def one_hots(v, r, d, i, half, first=False):
            if r or not first:
                v.wait_ge(used[half], base(r) + i)
            c = bass.ds(i * SLOTS + half * GROUP, GROUP)
            v.tensor_tensor(OH[:, half * GROUP:(half + 1) * GROUP, :],
                            iota[:, 0:P].unsqueeze(1).to_broadcast([P, GROUP, P]),
                            key[:, d, c].unsqueeze(2).to_broadcast([P, GROUP, P]), ALU.is_equal).then_inc(oh_ready, 1)

        def round_dve(v, r, d, begin=1):
            if begin == 1:
                for half in range(2):
                    one_hots(v, r, d, 0, half, True)
            last = STEPS
            if r < 2:
                last = BEHIND[r] + PASS_GROUPS // STEP_GROUPS
                with v.Fori(BEHIND[r], last) as i:
                    for half in range(2):
                        one_hots(v, r, d, i, half)
                        for g in range(2):
                            n = (i - BEHIND[r]) * STEP_GROUPS + 2 * half + g
                            where_group(v, PASS_GROUPS * (r + 1) + n, g, n * U, (r,))
                begin = last
            if begin < STEPS:
                with v.Fori(begin, STEPS) as i:
                    for half in range(2):
                        one_hots(v, r, d, i, half)
            if r < 2:
                v.wait_ge(perm_used, PASS_GROUPS * (r + 2))
                payload = PS[:, 7 * BANK:7 * BANK + CHUNKS]
                if r == 0:
                    dve_link(v.tensor_copy(lo_keep, payload))
                else:
                    decode_dve(v, 1, lo_keep, payload)

        def load_tiles(t, d, c):
            regs = [t.alloc_register(f"off{j}_{nc.next_id()}") for j in range(GROUP)]
            t.load(regs, tile_off[0:1, d, c])
            return [t.snap(g, min_val=0, max_val=TILES - 1) for g in regs]

        def clear_psum(t):
            for k in range(7):
                t.matmul(PS[:, k * BANK:(k + 1) * BANK], zeros[:, 0:P], zeros[:, 0:BANK], start=True, stop=False,
                         skip_group_check=True)

        def add_to(t, where, lhsT, rhs):
            return t.matmul(where, lhsT, rhs, start=False, stop=True, skip_group_check=True)

        def round_pe(t, r, d, degrees):
            clear_psum(t)

            def step(i, behind):
                for half in range(2):
                    tiles = load_tiles(t, d, bass.ds(i * SLOTS + half * GROUP, GROUP))
                    t.wait_ge(oh_ready, 2 * (base(r) + i) + half + 1)
                    for j in range(GROUP):
                        s = half * GROUP + j
                        t.wait_ge(landed[s], 16 * (base(r) + i + 1))
                        last = add_to(t, PS[:, bass.ds(tiles[j] * P, P)], G[:, s, 0:D], OH[:, s, :])
                        if degrees:
                            last = add_to(t, PS[:, bass.ds(tiles[j] + DEG_COL, 1)], OH[:, s, :], ones[:, 0:1])
                    last.then_inc(used[half], 1)
                    if behind:
                        for g in range(2):
                            n = (i - BEHIND[r]) * STEP_GROUPS + 2 * half + g
                            perm_group(t, PASS_GROUPS * (r + 1) + n, g, (r,), 7 - r)

            begin = 0
            if r == 0:
                with t.Fori(0, 2) as i:
                    step(i, False)
                place_pe(t, 1)
                begin = 2
            if r < 2:
                with t.Fori(begin, BEHIND[r]) as i:
                    step(i, False)
                t.wait_ge(where_ready, PASS_GROUPS * (r + 1) + 1)
                clear_bank(t, 7)
                begin = BEHIND[r] + PASS_GROUPS // STEP_GROUPS
                with t.Fori(BEHIND[r], begin) as i:
                    step(i, True)
            if begin < STEPS:
                with t.Fori(begin, STEPS) as i:
                    step(i, False)
            for half in range(2):
                t.wait_ge(used[half], base(r + 1))
            t.drain().then_inc(round_done, 1)

        def wide_pe(t, r, d):
            clear_psum(t)
            with t.Fori(0, STEPS) as i:
                for half in range(2):
                    tiles = load_tiles(t, d, bass.ds(i * SLOTS + half * GROUP, GROUP))
                    t.wait_ge(oh_ready, 2 * (base(r) + i) + half + 1)
                    for q in range(2):
                        t.wait_ge(added, i * SLOTS + half * GROUP + q * QUAD + 1)
                        for j in range(q * QUAD, (q + 1) * QUAD):
                            s = half * GROUP + j
                            t.wait_ge(landed[s], 16 * (base(r) + i + 1))
                            at = 7 * BANK + (j % QUAD) * P
                            last = t.matmul(PS[:, at:at + P], wide[s][:, D:], OH[:, s, :], start=True, stop=True)
                        last.then_inc(chunks_here, 1)
                        for j in range(q * QUAD, (q + 1) * QUAD):
                            s = half * GROUP + j
                            last = add_to(t, PS[:, bass.ds(tiles[j] * P, P)], wide[s][:, 0:D], OH[:, s, :])
                    last.then_inc(used[half], 1)
            for half in range(2):
                t.wait_ge(used[half], base(r + 1))
            t.drain().then_inc(round_done, 1)

        def wide_dve(v, r, d):
            acc = agg2T[:, 1, :]
            v.memset(acc, 0.0).then_inc(added, 1)

            def add(i, half):
                tiles = load_tiles(v, d, bass.ds(i * SLOTS + half * GROUP, GROUP))
                for q in range(2):
                    v.wait_ge(chunks_here, 4 * i + 2 * half + q + 1)
                    for j in range(q * QUAD, (q + 1) * QUAD):
                        v.wait_ge(added, i * SLOTS + half * GROUP + j + 1)
                        where = acc[:, bass.ds(tiles[j] * P, P)]
                        at = 7 * BANK + (j % QUAD) * P
                        v.tensor_tensor(where, where, PS[:, at:at + P], ALU.add).then_inc(added, 1)
        
            for half in range(2):
                one_hots(v, r, d, 0, half)
            with v.Fori(0, STEPS - 1) as i:
                for half in range(2):
                    add(i, half)
                    one_hots(v, r, d, i + 1, half)
            for half in range(2):
                add(STEPS - 1, half)
            v.wait_ge(added, CHUNKS + 1)
            dve_link(v.tensor_tensor(acc, acc, rdeg[:, :], ALU.mult))

        def bc(a, n):
            return a.unsqueeze(2).to_broadcast([P, a.shape[1], n])

        def norm_dve(v, n, relu):
            src = x if relu else h
            dve_link(v.tensor_reduce(st[:, 0, :], src[:, :, :], AX_X, ALU.add))
            dve_link(v.tensor_scalar(st[:, 0, :], st[:, 0, :], 1.0 / D, None, ALU.mult))
            dve_link(v.tensor_tensor(h[:, :, :], src[:, :, :], bc(st[:, 0, :], D), ALU.subtract))
            dve_link(v.tensor_tensor(scr, h[:, :, :], h[:, :, :], ALU.mult))
            v.tensor_reduce(st[:, 1, :], scr, AX_X, ALU.add).then_inc(var_ready, 1)
            v.wait_ge(std_ready, n + 1)
            dve_link(v.reciprocal(st[:, 3, :], st[:, 2, :]))
            if relu:
                v.scalar_tensor_tensor(h[:, :, :], h[:, :, :], 0.0, bc(st[:, 3, :], D), ALU.max, ALU.mult) \
                    .then_inc(h_ready, 1)
            else:
                dve_link(v.tensor_tensor(h[:, :, :], h[:, :, :], bc(st[:, 3, :], D), ALU.mult))

        def norm_act(a, n):
            a.wait_ge(var_ready, n + 1)
            a.activation(st[:, 2, :], st[:, 1, :], ACT.Sqrt, bias=eps[:, 0:1], scale=1.0 / D).then_inc(std_ready, 1)

        def transposes_pe(t, src_of, sem_):
            for k in range(TILES):
                last = t.transpose(PS[:, k * P:(k + 1) * P], src_of(k), ident)
            last.then_inc(sem_, 1)

        def node_major(t, pairs, sem_):
            for k in range(TILES):
                for n, (act_T, w) in enumerate(pairs):
                    last = t.matmul(PS[:, k * P:(k + 1) * P], act_T[:, k * P:(k + 1) * P], w,
                                    start=(n == 0), stop=(n == len(pairs) - 1))
            last.then_inc(sem_, 1)

        def wt(name, c=0, width=P):
            at = W_AT[name] + c
            return W[:, at:at + width]

        def agg_dve(v, r, dst, degrees, exact_one):
            v.wait_ge(round_done, r + 1)
            if degrees:
                n = degrees - 1
                deg = PS[:, DEG_COL:DEG_COL + TILES]
                if exact_one:
                    dve_link(v.tensor_scalar(st[:, 4, :], deg, 1.0, None, ALU.max))
                else:
                    dve_link(v.tensor_scalar(st[:, 4, :], deg, 1e-12, None, ALU.add))
                dve_link(v.reciprocal(st[:, 5, :], st[:, 4, :]))
                dve_link(v.tensor_copy(dst, PS[:, 0:NP_]))
                v.tensor_tensor(h[:, :, :], ident.unsqueeze(1).to_broadcast([P, TILES, P]), bc(st[:, 5, :], P),
                                ALU.mult).then_inc(diag_ready, 1)
                v.wait_ge(rdeg_summed, n + 1)
                dve_link(v.tensor_copy(rdeg[:, :], PS[:, 0:NP_]))
                v.tensor_tensor(dst, dst, rdeg[:, :], ALU.mult).then_inc(agg_ready, 1)
            else:
                v.tensor_tensor(dst, PS[:, 0:NP_], rdeg[:, :], ALU.mult).then_inc(agg_ready, 1)

        def rdeg_pe(t, n):
            t.wait_ge(diag_ready, n)
            hf = h[:, :, :].rearrange("p t f -> p (t f)")
            for a0 in range(0, NP_, BANK):
                a1 = min(a0 + BANK, NP_)
                last = t.matmul(PS[:, a0:a1], ones, hf[:, a0:a1], start=True, stop=True)
            last.then_inc(rdeg_summed, 1)

        def ps2(bank):
            return PS[:, bank * BANK:(bank + 2) * BANK].rearrange("p (c n) -> p c n", c=2)[:, :, 0:BLK]

        def lin_pe(t, bank, terms, sem_=None):
            for ob in range(2):
                o = PS[:, (bank + ob) * BANK:(bank + ob) * BANK + BLK]
                for n, (name, c, rhs) in enumerate(terms):
                    last = t.matmul(o, wt(name, c * H1 + ob * P), rhs, start=(n == 0), stop=(n == len(terms) - 1))
            if sem_ is not None:
                last.then_inc(sem_, 1)

        def elu_act(a, n, X, bname):
            a.wait_ge(lin_ready, n)
            for ob in range(2):
                last = a.activation(blk[:, X, 0, ob, :], PS[:, (2 * X + ob) * BANK:(2 * X + ob) * BANK + BLK], ACT.Exp,
                                    bias=bcol[:, BCOL[bname] + ob:BCOL[bname] + ob + 1])
            last.then_inc(exp_ready, 1)

        def elu_dve(v, n, X, bname, dest, res=None):
            v.wait_ge(exp_ready, n)
            e, o = blk[:, X, 0, :, :], blk[:, X, 1, :, :]
            for ob in range(2):
                last = v.tensor_scalar(o[:, ob, :], PS[:, (2 * X + ob) * BANK:(2 * X + ob) * BANK + BLK],
                                bcol_m1[:, BCOL[bname] + ob:BCOL[bname] + ob + 1], -1.0, ALU.add, ALU.max)
            last.then_inc(clipped, 1)
            v.wait_ge(clipped, n)
            if res is None:
                v.scalar_tensor_tensor(dest, e, 1.0, o, ALU.min, ALU.add).then_inc(act_done, 1)
                return
            v.scalar_tensor_tensor(e, e, 1.0, o, ALU.min, ALU.add).then_inc(elu_done, 1)
            v.wait_ge(elu_done, res[1])
            for ob in range(2):
                at = (4 + 2 * X + ob) * BANK
                c = BCOL[res[0]] + ob
                last = v.scalar_tensor_tensor(dest[:, ob, :], PS[:, at:at + BLK], bcol[:, c:c + 1], e[:, ob, :],
                                              ALU.add, ALU.add)
            last.then_inc(act_done, 1)

        PAIRS = NBLK // 2

        def cols(i, X):
            return bass.ds(i * (2 * BLK) + X * BLK, BLK)

        def sage1_pe(t):
            with t.Fori(0, PAIRS) as i:
                for X in range(2):
                    t.wait_ge(act_done, 2 * i + 1 + X)
                    lin_pe(t, 2 * X, [("l1", 0, aggT[:, cols(i, X)]), ("r1", 0, hT[:, cols(i, X)])], lin_ready)

        def chain_pe(t):
            with t.Fori(0, PAIRS) as i:
                for X in range(2):
                    c = cols(i, X)
                    t.wait_ge(act_done, 10 + 6 * i - 1 + X)
                    lin_pe(t, 4 + 2 * X, [("res1", 0, hT[:, c])])
                    lin_pe(t, 2 * X, [("l2", k, agg2T[:, k, c]) for k in range(2)]
                           + [("r2", k, h1T[:, k, c]) for k in range(2)], lin_ready)
                for X in range(2):
                    t.wait_ge(act_done, 10 + 6 * i + 1 + X)
                    lin_pe(t, 2 * X, [("fc1", k, blk[:, X, 1, k, :]) for k in range(2)], lin_ready)
                for X in range(2):
                    t.wait_ge(act_done, 10 + 6 * i + 3 + X)
                    lin_pe(t, 4 + 2 * X, [("res2", 0, hT[:, cols(i, X)])])
                    lin_pe(t, 2 * X, [("fc2", k, blk[:, X, 1, k, :]) for k in range(2)], lin_ready)

        def sage1_act(a):
            with a.Fori(0, PAIRS) as i:
                for X in range(2):
                    elu_act(a, 2 * i + 1 + X, X, "b_l1")

        def chain_act(a):
            with a.Fori(0, PAIRS) as i:
                for n, name in enumerate(("b_l2", "fc1", "fc2")):
                    for X in range(2):
                        elu_act(a, 8 + 6 * i + 2 * n + X + 1, X, name)

        def sage1_dve(v):
            with v.Fori(0, PAIRS) as i:
                for X in range(2):
                    elu_dve(v, 2 * i + 1 + X, X, "b_l1", h1T[:, :, cols(i, X)])

        def chain_dve(v):
            with v.Fori(0, PAIRS) as i:
                for X in range(2):
                    elu_dve(v, 8 + 6 * i + X + 1, X, "b_l2", blk[:, X, 1, :, :], ("res1", 4 * i + X + 1))
                for X in range(2):
                    elu_dve(v, 8 + 6 * i + 2 + X + 1, X, "fc1", blk[:, X, 1, :, :])
                for X in range(2):
                    elu_dve(v, 8 + 6 * i + 4 + X + 1, X, "fc2", agg2T[:, :, cols(i, X)], ("res2", 4 * i + 2 + X + 1))

        def top_act(a, r, d):
            def indices(i, half, spills=None):
                c = bass.ds(i * SLOTS + half * GROUP, GROUP)
                a.wait_ge(used[half], base(r) + i)
                if spills is not None:
                    a.wait_ge(spilled[half], spills)
                a.copy(idxbuf[:, half, :], idx[:, d, c]).then_inc(idx_ready, 1)

            def step(i, more):
                for half in range(2):
                    a.wait_ge(sT_summed, 2 * (STEPS * d + i) + half + 1)
                    c = bass.ds(i * SLOTS + half * GROUP, GROUP)
                    a.copy(sE[0][:, c, :], G[:, half * GROUP:(half + 1) * GROUP, D:])
                    at = (4 + 2 * half) * BANK
                    a.copy(sT[0:SPLIT * HEADS, half * GROUP:(half + 1) * GROUP, :],
                           PS[0:SPLIT * HEADS, at:at + GROUP * P].rearrange("p (j e) -> p j e", j=GROUP)) \
                        .then_inc(sT_ready, 1)
                    if more:
                        indices(i + 1, half, 16 * (STEPS * d + i + 1))

            for half in range(2):
                indices(0, half)
            with a.Fori(0, STEPS - 1) as i:
                step(i, True)
            step(STEPS - 1, False)

        def late_top_act(a, r, d):
            def bring(i, half):
                n = 2 * i + half
                a.wait_ge(scores_here, n + 1)
                a.wait_ge(sT_summed, 2 * STEPS * d + n - 1)
                a.copy(score_buf[:, half, :, :], sE[d][:, bass.ds(i * SLOTS + half * GROUP, GROUP), :]) \
                    .then_inc(scores_brought, 1)

            def take(i, half):
                a.wait_ge(sT_summed, 2 * (STEPS * d + i) + half + 1)
                bank = PS[0:SPLIT * HEADS, (4 + 2 * half) * BANK:(5 + 2 * half) * BANK].bitcast(BF16)
                a.copy(sT[0:SPLIT * HEADS, half * GROUP:(half + 1) * GROUP, :],
                       bank.rearrange("p (j e) -> p j e", j=GROUP)).then_inc(sT_ready, 1)

            bring(0, 0)
            with a.Fori(0, STEPS - 1) as i:
                bring(i, 1)
                take(i, 0)
                bring(i + 1, 0)
                take(i, 1)
            bring(STEPS - 1, 1)
            take(STEPS - 1, 0)
            take(STEPS - 1, 1)

        def top_pe(t, r, d):
            with t.Fori(0, STEPS) as i:
                for half in range(2):
                    n = 2 * (STEPS * d + i) + half
                    at = (4 + 2 * half) * BANK
                    if d == 1:
                        t.wait_ge(scores_brought, 2 * i + half + 1)
                        bank = PS[0:SPLIT * HEADS, at:at + BANK].bitcast(BF16)
                    for j in range(GROUP):
                        s = half * GROUP + j
                        if d == 0:
                            t.wait_ge(landed[s], 16 * (base(r) + i + 1))
                            last = t.transpose(PS[0:SPLIT * HEADS, at + j * P:at + (j + 1) * P], G[:, s, D:], ident)
                        else:
                            last = t.transpose(bank[:, j * P:(j + 1) * P], score_buf[:, half, j, :], ident_b[:, :])
                    last.then_inc(sT_summed, 1)
                    t.wait_ge(oh_ready, 2 * (base(r) + i) + half + 1)
                    t.wait_ge(sT_ready, n + 1)
                    for j in range(GROUP):
                        s = half * GROUP + j
                        bank = (j % 4) * BANK
                        t.wait_ge(reduced, n * GROUP + j + 1)
                        t.matmul(PS[:, bank:bank + BANK], OHb[:, s, :],
                                 big_id[:, :].unsqueeze(1).to_broadcast([P, HEADS, P]), start=True, stop=False,
                                 skip_group_check=True)
                        for hd in range(HEADS):
                            last = t.matmul(PS[:, bank + hd * P:bank + (hd + 1) * P], pick[:, hd, :], sT[:, s, :],
                                            start=False, stop=True, skip_group_check=True)
                        last.then_inc(masked_ready, 1)
                    t.nop().then_inc(used[half], 1)
            for half in range(2):
                t.wait_ge(used[half], base(r + 1))
            t.drain().then_inc(round_done, 1)

        def top_dve(v, r, d):
            with v.Fori(0, STEPS) as i:
                for half in range(2):
                    n = 2 * (STEPS * d + i) + half
                    v.wait_ge(used[half], base(r) + i)
                    c = bass.ds(i * SLOTS + half * GROUP, GROUP)
                    v.tensor_tensor(OHb[:, half * GROUP:(half + 1) * GROUP, :],
                                    iota[:, 0:P].unsqueeze(1).to_broadcast([P, GROUP, P]),
                                    key[:, d, c].unsqueeze(2).to_broadcast([P, GROUP, P]), ALU.not_equal) \
                        .then_inc(oh_ready, 1)
                    for j in range(GROUP):
                        v.wait_ge(masked_ready, n * GROUP + j + 1)
                        bank = (j % 4) * BANK
                        v.tensor_reduce(cmax[:, :, bass.ds(i * SLOTS + half * GROUP + j, 1)].rearrange("p h k -> p (h k)"),
                                        PS[:, bank:bank + BANK].rearrange("p (h e) -> p h e", h=HEADS), AX_X, ALU.max) \
                            .then_inc(reduced, 1)

        def flat(a):
            return a.rearrange("p h k -> p (h k)")

        def guard_dve(v, d):
            ct = chunk_tile[:, d, :]
            v.memset(reset[:, 0, 0:1], 0.0)
            v.memset(reset[:, 1, CHUNKS - 1:CHUNKS], 0.0)
            v.tensor_tensor(reset[:, 0, 1:CHUNKS], ct[:, 1:CHUNKS], ct[:, 0:CHUNKS - 1], ALU.not_equal)
            dve_link(v.tensor_tensor(reset[:, 1, 0:CHUNKS - 1], ct[:, 1:CHUNKS], ct[:, 0:CHUNKS - 1], ALU.not_equal))
            dve_link(v.tensor_scalar(reset, reset, NEG_BIG, None, ALU.mult))
            for hd in range(HEADS):
                v.tensor_tensor_scan(mr[:, hd, :], reset[:, 0, :], cmax[:, hd, :], NEG_BIG, ALU.add, ALU.max)
                last = v.tensor_tensor_scan(mr[:, HEADS + hd, ::-1], reset[:, 1, ::-1], cmax[:, hd, ::-1], NEG_BIG,
                                            ALU.add, ALU.max)
            dve_link(last)
            dve_link(v.tensor_tensor(cmax, mr[:, 0:HEADS, :], mr[:, HEADS:, :], ALU.max))
            v.wait_ge(recv_summed, d + 1)
            recv = PS[:, 0:4 * BANK].rearrange("p (h k) -> p h k", h=HEADS)[:, :, 0:CHUNKS]
            v.tensor_copy(mr[:, HEADS:, :], recv)
            dve_link(v.tensor_tensor(mr[:, 0:HEADS, :], recv, cmax, ALU.add))
            v.scalar_tensor_tensor(mr[:, 0:HEADS, :], mr[:, 0:HEADS, :], 0.2, mr[:, 0:HEADS, :], ALU.mult, ALU.max) \
                .then_inc(mr_ready, 1)
            v.tensor_tensor(sender, sE[d][:, :, 0:HEADS].rearrange("p k h -> p h k"),
                            sE[d][:, :, HEADS:2 * HEADS].rearrange("p k h -> p h k"), ALU.add).then_inc(mr_ready, 1)
            v.wait_ge(mr_ready, 2 * d + 2)
            dve_link(v.tensor_tensor(sender, sender, sE[d][:, :, 2 * HEADS:].rearrange("p k h -> p h k"), ALU.add))
            for k in range(SPLIT):
                dve_link(v.tensor_copy(mrb[:, k, :, :], mr))
                if k < SPLIT - 1:
                    dve_link(v.tensor_tensor(mr, mr, mrb[:, k, :, :], ALU.subtract))
            v.nop().then_inc(mrb_ready, 1)

            n0 = GROUPS * d

            def one_hot(i, b):
                n = n0 + LAP * i + b
                v.wait_ge(turned, n + 1)
                c = bass.ds((i * LAP + b) * GROUP, GROUP)
                v.tensor_tensor(eq[:, b % LAP, :, :], iota[:, 0:P].unsqueeze(1).to_broadcast([P, GROUP, P]),
                                key[:, d, c].unsqueeze(2).to_broadcast([P, GROUP, P]), ALU.is_equal) \
                    .then_inc(oh_again, 1)

            def take(i, b):
                n = n0 + LAP * i + b
                v.wait_ge(er_summed, LAP + n + 1)
                c = bass.ds((i * LAP + b) * GROUP, GROUP)
                at = (4 + b % 2) * BANK
                v.tensor_reduce(er[:, :, c].rearrange("p q k -> p k q"),
                                PS[:, at:at + 24 * GROUP].rearrange("p (k s q) -> p k q s", s=SPLIT, q=8), AX_X,
                                ALU.add).then_inc(er_ready, 1)

            for b in range(AHEAD_OH):
                one_hot(0, b)
            with v.Fori(0, LAPS - 1) as i:
                for b in range(LAP):
                    one_hot(i, b + AHEAD_OH)
                    take(i, b)
            for b in range(LAP):
                if b + AHEAD_OH < LAP:
                    one_hot(LAPS - 1, b + AHEAD_OH)
                take(LAPS - 1, b)
            v.wait_ge(er_ready, 2 + GROUPS * (d + 1))
            dve_link(v.tensor_tensor(ex, sender, er[:, HEADS:, :], ALU.add))
            dve_link(v.scalar_tensor_tensor(ex, ex, 0.2, ex, ALU.mult, ALU.max))
            dve_link(v.tensor_tensor(ex, ex, er[:, 0:HEADS, :], ALU.subtract))
            v.tensor_scalar(ex, ex, 0.0, None, ALU.min).then_inc(arg_ready, 1)

        def guard_pe(t, d):
            t.wait_ge(reduced, 4 + CHUNKS * (d + 1))
            for hd in range(HEADS):
                last = t.matmul(PS[:, hd * BANK:hd * BANK + CHUNKS], rT[:, d, hd, :], tile_sel[:, d, :],
                                start=True, stop=True)
            last.then_inc(recv_summed, 1)
            t.wait_ge(mrb_ready, d + 1)
            n0 = GROUPS * d

            def turn(i, b):
                n = n0 + LAP * i + b
                t.wait_ge(oh_again, n + 1)
                t.wait_ge(ohT_ready, n + 1)
                bank = PS[:, (b % LAP) * BANK:(b % LAP + 1) * BANK].bitcast(BF16)
                for j in range(GROUP):
                    last = t.transpose(bank[:, j * P:(j + 1) * P], eq[:, b % LAP, j, :], ident_b[:, :])
                last.then_inc(turned, 1)

            def take(i, b):
                n = n0 + LAP * i + b
                t.wait_ge(ohT_ready, LAP + n + 1)
                t.wait_ge(er_ready, n + 1)
                for j in range(GROUP):
                    at = (4 + b % 2) * BANK + 24 * j
                    k = bass.ds((i * LAP + b) * GROUP + j, 1)
                    last = t.matmul(PS[:, at:at + 24].rearrange("p (s q) -> p s q", s=SPLIT), ohT[:, b, j, :],
                                    mrb[:, :, :, k].rearrange("p s q k -> p s (q k)"), start=True, stop=True)
                last.then_inc(er_summed, 1)

            for b in range(AHEAD_T):
                turn(0, b)
            with t.Fori(0, LAPS - 1) as i:
                for b in range(LAP):
                    turn(i, b + AHEAD_T)
                    take(i, b)
            for b in range(LAP):
                if b + AHEAD_T < LAP:
                    turn(LAPS - 1, b + AHEAD_T)
                take(LAPS - 1, b)

        def guard_act(a, d):
            for half in range(2):
                a.wait_ge(spilled[half], 16 * STEPS)
            with a.Fori(0, LAPS) as i:
                for b in range(LAP):
                    n = GROUPS * d + LAP * i + b
                    a.wait_ge(turned, LAP + n + 1)
                    a.wait_ge(er_summed, n + 1)
                    bank = PS[:, b * BANK:(b + 1) * BANK].bitcast(BF16)
                    a.copy(ohT[:, b, :, :], bank.rearrange("p (j e) -> p j e", j=GROUP)).then_inc(ohT_ready, 1)
            a.wait_ge(arg_ready, d + 1)
            a.activation(ex, ex, ACT.Exp).then_inc(ex_ready, 1)


        def spill_sp(sp, r, d):
            with sp.Fori(0, STEPS) as i:
                for half in range(2):
                    for j in range(GROUP):
                        sp.wait_ge(landed[half * GROUP + j], 16 * (base(r) + i + 1))
                    c = bass.ds((i * SLOTS + half * GROUP) * D, GROUP * D)
                    sp.dma_start(spill[d][:, c].rearrange("p (j f) -> p j f", j=GROUP),
                                 G[:, half * GROUP:(half + 1) * GROUP, 0:D]).then_inc(spilled[half], 16)
            for half in range(2):
                sp.wait_ge(spilled[half], 16 * STEPS)

        def ahead_pool(p, r, d):
            p.wait_ge(self_summed, 1)

            def gather(i, b, first=False):
                if not first:
                    p.wait_ge(spilled1[b], 16 * i)
                c = bass.ds((i * RING1 + b) * GROUP, GROUP)
                p.tensor_copy(idxbuf1[:, b, :], idx[:, d, c]).then_inc(idx_copied, 1)
                p.wait_ge(idx_copied, i * RING1 + b + 1)
                p.sem_inc(gathers_begun)
                for j in range(GROUP):
                    p.indirect_dma_start(out=ring1[:, b, j, :], out_offset=None, in_=T_att[d][:, :],
                                         in_offset=bass.IndirectOffsetOnAxis(ap=idxbuf1[:, b, j:j + 1], axis=0)) \
                        .then_inc(landed1[b], 16)

            def send(i, b):
                p.wait_ge(landed1[b], 16 * GROUP * (i + 1))
                g = i * RING1 + b
                p.tensor_copy(sE[d][:, bass.ds(g * GROUP, GROUP), :], ring1[:, b, :, D:]).then_inc(scores_here, 1)
                p.wait_ge(scores_here, g + 1)
                p.sem_inc(spills_begun)
                p.dma_start(spill[d][:, bass.ds(g * (GROUP * D), GROUP * D)].rearrange("p (j f) -> p j f", j=GROUP),
                            ring1[:, b, :, 0:D]).then_inc(spilled1[b], 16)

            turns, odd = GROUPS // RING1, GROUPS % RING1
            assert odd == 1
            for b in range(RING1):
                gather(0, b, True)
                if b:
                    send(0, b - 1)
            with p.Fori(1, turns) as i:
                for b in range(RING1):
                    gather(i, b)
                    send(i if b else i - 1, (b - 1) % RING1)
            gather(turns, 0)
            send(turns - 1, RING1 - 1)
            send(turns, 0)
            for b in range(RING1):
                p.wait_ge(spilled1[b], 16 * (turns + (b < odd)))

        def back_sp(sp, d):
            if d == 1:
                for b in range(RING1):
                    sp.wait_ge(spilled1[b], 16 * (GROUPS // RING1 + (b < GROUPS % RING1)))
            sp.wait_ge(ex_ready, d + 1)
            with sp.Fori(0, LAPS) as i:
                for b in range(RING2):
                    sp.wait_ge(weighed, 2 * STEPS * d + RING2 * i + b + 1)
                    c = bass.ds((i * RING2 + b) * (GROUP * D), GROUP * D)
                    sp.dma_start(ring2[:, b, :, :].rearrange("p j f -> p (j f)"), spill[d][:, c]) \
                        .then_inc(back[b], 16)

        def weighted_dve(v, d):
            v.wait_ge(ex_ready, d + 1)
            rest = ex
            for k in range(SPLIT):
                dve_link(v.tensor_copy(exb[:, k, :, :], rest))
                if k < SPLIT - 1:
                    dve_link(v.tensor_tensor(ex_rest, rest, exb[:, k, :, :], ALU.subtract))
                    rest = ex_rest
            v.nop().then_inc(exb_ready, 1)
            with v.Fori(0, LAPS) as i:
                for b in range(RING2):
                    half = b % 2
                    n = 2 * STEPS * d + RING2 * i + b
                    v.wait_ge(weighed, n + RING2 - 1)
                    c = bass.ds((i * RING2 + b) * GROUP, GROUP)
                    v.tensor_tensor(OH[:, half * GROUP:(half + 1) * GROUP, :],
                                    iota[:, 0:P].unsqueeze(1).to_broadcast([P, GROUP, P]),
                                    key[:, d, c].unsqueeze(2).to_broadcast([P, GROUP, P]), ALU.is_equal) \
                        .then_inc(oh_third, 1)
                    v.wait_ge(back[b], 16 * (LAPS * d + i + 1))
                    g = ring2[:, b, :, :].rearrange("p j (h f) -> p j h f", h=HEADS)
                    v.tensor_tensor(g, g, ex[:, :, c].rearrange("p h k -> p k h").unsqueeze(3)
                                    .to_broadcast([P, GROUP, HEADS, HD]), ALU.mult).then_inc(scaled_ready, 1)

        def weighted_act(a, d):
            with a.Fori(0, LAPS) as i:
                for b in range(RING2):
                    a.wait_ge(oh_third, GROUPS * d + RING2 * i + b + 1)
                    half = b % 2
                    c = bass.ds((i * RING2 + b) * GROUP, GROUP)
                    a.copy(exs[:, half, :, :].rearrange("p j (s h) -> p s h j", s=SPLIT), exb[:, :, :, c])
                    a.copy(OHw[:, half, :, :], OH[:, half * GROUP:(half + 1) * GROUP, :]).then_inc(oh_cast, 1)

        def weighted_pe(t, d):
            clear_psum(t)
            with t.Fori(0, LAPS) as i:
                for b in range(RING2):
                    c = bass.ds((i * RING2 + b) * GROUP, GROUP)
                    tiles = load_tiles(t, d, c)
                    n = GROUPS * d + RING2 * i + b
                    t.wait_ge(scaled_ready, n + 1)
                    for j in range(GROUP):
                        s = (b % 2) * GROUP + j
                        add_to(t, PS[:, bass.ds(tiles[j] * P, P)], OH[:, s, :], ring2[:, b, j, :])
                    t.wait_ge(oh_cast, n + 1)
                    for j in range(GROUP):
                        at = bass.ds(tiles[j] * (SPLIT * HEADS) + DEG_COL, SPLIT * HEADS)
                        last = add_to(t, PS[:, at], OHw[:, b % 2, j, :], exs[:, b % 2, j, :])
                    last.then_inc(weighed, 1)
            t.wait_ge(weighed, RING2 + 2 * STEPS * (d + 1))
            t.drain().then_inc(weighted_done, 1)

        def weighted_out_dve(v, d):
            v.wait_ge(weighted_done, d + 1)
            n = TILES * HEADS
            den = rden[:, 0, :]
            dve_link(v.tensor_reduce(den.rearrange("p (t h) -> p t h", h=HEADS), PS[:, DEG_COL:DEG_COL + SPLIT * n]
                                     .rearrange("p (t s h) -> p t h s", s=SPLIT, h=HEADS), AX_X, ALU.add))
            dve_link(v.tensor_scalar(den, den, 1e-8, None, ALU.add))
            dve_link(v.reciprocal(rden[:, 1, :], den))
            hv = h[:, :, :].rearrange("p t (h f) -> p (t h) f", h=HEADS)
            dve_link(v.tensor_tensor(hv, PS[:, 0:NP_].rearrange("p (n f) -> p n f", f=HD),
                                     rden[:, 1, :].unsqueeze(2).to_broadcast([P, n, HD]), ALU.mult))
            dve_link(v.tensor_tensor(comb, comb, h[:, :, :], ALU.add))
            v.nop().then_inc(den_ready, 1)

        elu_done = sem("elu_done")
        mrb_ready = sem("mrb_ready")
        oh_third = sem("oh_third")
        weighed = sem("weighed")
        scores_here = sem("scores_here")
        scores_brought = sem("scores_brought")
        landed1 = [sem(f"landed1_{b}") for b in range(RING1)]
        spilled1 = [sem(f"spilled1_{b}") for b in range(RING1)]
        idx_copied = sem("idx_copied")
        spills_begun = sem("spills_begun")
        exb_ready = sem("exb_ready")
        oh_cast = sem("oh_cast")
        weighted_done = sem("weighted_done")
        spilled = [sem(f"spilled{i}") for i in range(2)]
        back = [sem(f"back{i}") for i in range(RING2)]
        ident_b = sb("ident_b", [P, P], BF16)
        table = {n: sem(f"table_{n}") for n in ("h0", "h1", "g", "h2", "att")}
        chunks_here = sem("chunks_here")
        added = sem("added")
        clipped = sem("clipped")
        rden = sb("rden", [P, 2, TILES * HEADS])
        rowsum = sb("rowsum", [P, D])

        def table_rows(name):
            return T[name].rearrange("(t p) f -> p t f", p=P)

        @block.sync
        def _(sp):
            sp.dma_start(e_i[:, :, :], edges.rearrange("k (p j) -> p k j", p=EP)).then_inc(loaded_edges, 16)
            sp.dma_start(cst[:, :], consts).then_inc(loaded_consts, 16)
            sp.wait_ge(x_cleared, 1)
            with sp.Fori(0, TILES - 1) as i:
                sp.dma_start(x[:, bass.ds(i, 1), :].rearrange("p t f -> p (t f)"), x_in[bass.ds(i * P, P), :]) \
                    .then_inc(loaded_x, 16)
            sp.dma_start(x[0:TAIL, TILES - 1, :], x_in[(TILES - 1) * P:N_NODES, :]).then_inc(loaded_x, 16)
            sp.dma_start(W[:, :], weights).then_inc(loaded_w, 16)
            sp.dma_start(bcol[:, :], bias_cols).then_inc(loaded_b, 16)
            sp.dma_start(brow[:, :, :], bias_rows.unsqueeze(0).to_broadcast([P, ROWS, D])).then_inc(loaded_b, 16)
            sp.dma_start(attn_sb[:, :], attn).then_inc(loaded_b, 16)
            sp.wait_ge(h_ready, 1)
            sp.dma_start(table_rows("h0"), h[:, :, :]).then_inc(table["h0"], 16)
            sp.wait_ge(h_ready, 2)
            sp.dma_start(table_rows("h1"), h[:, :, :]).then_inc(table["h1"], 16)
            sp.wait_ge(h1_ready, 1)
            sp.dma_start(table_rows("g")[:, :, 0:D], h[:, :, :]).then_inc(table["g"], 16)
            sp.wait_ge(h1_ready, 2)
            sp.dma_start(table_rows("g")[:, :, D:], h1N).then_inc(table["g"], 16)
            sp.wait_ge(h_ready, 3)
            sp.dma_start(table_rows("h2"), h[:, :, :]).then_inc(table["h2"], 16)
            sp.wait_ge(proj_ready, 1)
            sp.wait_ge(parts_ready, 1)
            for d in range(2):
                rows = T_att[d].rearrange("(t p) f -> p t f", p=P)
                sp.dma_start(rows[:, :, 0:D], h[:, :, :]).then_inc(table["att"], 16)
                sp.dma_start(rows[:, :, D:], parts[:, d, :, :]).then_inc(table["att"], 16)
            spill_sp(sp, 4, 0)
            for d in range(2):
                back_sp(sp, d)
            sp.wait_ge(x_final, 1)
            sp.dma_start(out[0:(TILES - 1) * P, :].rearrange("(t p) f -> p t f", p=P), x[:, 0:TILES - 1, :]) \
                .then_inc(stored, 16)
            sp.dma_start(out[(TILES - 1) * P:N_NODES, :], x[0:TAIL, TILES - 1, :]).then_inc(stored, 16)
            sp.wait_ge(stored, 32)

        @block.gpsimd
        def _(p):
            p.memset(x[:, TILES - 1, :], 0.0).then_inc(x_cleared, 1)
            p.memset(zeros[:, :], 0.0)
            p.memset(sT[:, :, :], 0.0)
            p.memset(eps[:, :], 1e-5).then_inc(zeros_ready, 1)
            for r, name in enumerate(("h0", "h1", "g", "h2")):
                p.wait_ge(table[name], 32 if name == "g" else 16)
                round_pool(p, r, T[name], wide if name == "g" else narrow)
            p.wait_ge(table["att"], 64)
            round_pool(p, 4, T_att[0], [G[:, s, :] for s in range(SLOTS)])
            ahead_pool(p, 5, 1)

        @block.vector
        def _(v):
            v.wait_ge(loaded_edges, 16)
            v.wait_ge(loaded_consts, 16)
            dve_link(v.tensor_copy(iota_h[:, :], iota))
            dve_link(v.tensor_copy(ident_b[:, :], ident))
            dve_link(v.tensor_scalar(big_id[:, :], ident, NEG_BIG, None, ALU.mult))
            dve_link(v.tensor_copy(pick[:, :, :], cst[:, C_PICK:C_ALL].rearrange("p (h m) -> p h m", h=HEADS)))
            v.wait_ge(loaded_x, 16 * TILES)
            v.wait_ge(zeros_ready, 1)
            norm_dve(v, 0, True)
            v.wait_ge(hT_ready, 1)
            v.wait_ge(table["h0"], 16)
            place_dve(v, 0, lambda k: None)
            permute_dve(v)
            v.wait_ge(sorted_ready, 1)
            v.wait_ge(loaded_b, 48)
            dve_link(v.tensor_scalar(bcol_m1[:, :], bcol[:, :], -1.0, None, ALU.add))
            dve_link(v.tensor_tensor(rowsum[:, :], brow[:, ROW["L2_self"], :], brow[:, ROW["L2_nei"], :], ALU.add))

            def row(a):
                return a.unsqueeze(1).to_broadcast([P, TILES, D])

            ps3 = PS[:, 0:NP_].rearrange("p (t f) -> p t f", t=TILES)
            for half in range(2):
                one_hots(v, 0, 0, 0, half, True)

            def between(k):
                for half in range(2):
                    one_hots(v, 0, 0, k, half)

            place_dve(v, 1, between)
            round_dve(v, 0, 0, BEHIND[0])
            agg_dve(v, 0, aggT, 1, True)
            v.wait_ge(square_ready, 1)
            dve_link(v.tensor_reduce(st[:, 6, :], h[:, :, :], AX_X, ALU.add))
            v.nop().then_inc(sumsq_ready, 1)
            v.wait_ge(len_ready, 1)
            dve_link(v.tensor_scalar(st[:, 7, :], st[:, 7, :], 1e-12, None, ALU.max))
            dve_link(v.reciprocal(st[:, 6, :], st[:, 7, :]))
            dve_link(v.tensor_tensor(h[:, :, :], ps3, bc(st[:, 6, :], D), ALU.mult))
            dve_link(v.tensor_tensor(x[:, :, :], x[:, :, :], h[:, :, :], ALU.add))
            norm_dve(v, 1, True)
            v.wait_ge(hT_ready, 2)
            round_dve(v, 1, 0)
            agg_dve(v, 1, aggT, 0, True)
            v.sem_inc(act_done, 2)
            sage1_dve(v)
            v.wait_ge(h1_ready, 2)
            wide_dve(v, 2, 0)
            agg_dve(v, 2, agg2T[:, 0, :], 0, True)
            chain_dve(v)
            v.wait_ge(fc3_summed, 1)
            v.tensor_tensor(h[:, :, :], ps3, row(brow[:, ROW["fc3"], :]), ALU.add).then_inc(z_ready, 1)
            v.wait_ge(log_ready, 1)
            dve_link(v.scalar_tensor_tensor(h[:, :, :], h[:, :, :], 0.0, scr, ALU.max, ALU.add))
            dve_link(v.tensor_tensor(x[:, :, :], x[:, :, :], h[:, :, :], ALU.add))
            norm_dve(v, 2, True)
            v.wait_ge(hT_ready, 3)
            round_dve(v, 3, 1)
            agg_dve(v, 3, aggT, 2, False)
            v.wait_ge(out2_summed, 1)
            dve_link(v.tensor_tensor(h[:, :, :], ps3, row(rowsum[:, :]), ALU.add))
            dve_link(v.scalar_tensor_tensor(x[:, :, :], h[:, :, :], 0.0, x[:, :, :], ALU.max, ALU.add))
            norm_dve(v, 3, True)
            v.wait_ge(hT_ready, 4)
            v.wait_ge(score_summed, 1)
            dve_link(v.tensor_copy(score[:, :, :], PS[:, 7 * BANK:7 * BANK + TILES * SC]
                                   .rearrange("p (t c) -> p t c", t=TILES)))
            for d in range(2):
                rest = score[:, :, 8 * d:8 * d + HEADS]
                left = rden[:, 0, :].rearrange("p (t h) -> p t h", h=HEADS)
                ph = part_h[:, :].rearrange("p (t h) -> p t h", h=HEADS)
                for k in range(SPLIT):
                    part = parts[:, d, :, k * HEADS:(k + 1) * HEADS]
                    dve_link(v.tensor_copy(ph, rest))
                    dve_link(v.tensor_copy(part, ph))
                    if k < SPLIT - 1:
                        dve_link(v.tensor_tensor(left, rest, part, ALU.subtract))
                        rest = left
            v.nop().then_inc(parts_ready, 1)
            v.wait_ge(proj_summed, 1)
            v.tensor_copy(h[:, :, :], ps3).then_inc(proj_ready, 1)
            v.wait_ge(self_summed, 1)
            dve_link(v.tensor_tensor(comb, ps3, row(brow[:, ROW["L3_bias"], :]), ALU.add))
            v.nop().then_inc(self_ready, 1)
            v.wait_ge(rT_summed, 1)
            v.tensor_copy(rT[:, :, :, :], PS[0:TILES, 0:2 * HEADS * P].rearrange("p (d h e) -> p d h e", d=2, h=HEADS)) \
                .then_inc(rT_ready, 1)
            v.sem_inc(reduced, 4)
            v.sem_inc(er_ready, 2)
            for d in range(2):
                top_dve(v, 4 + d, d)
                v.wait_ge(round_done, 5 + d)
                guard_dve(v, d)
                weighted_dve(v, d)
                weighted_out_dve(v, d)
            dve_link(v.tensor_copy(h[:, :, :], comb))
            norm_dve(v, 4, False)
            dve_link(v.tensor_tensor(h[:, :, :], h[:, :, :], row(brow[:, ROW["gamma"], :]), ALU.mult))
            dve_link(v.tensor_tensor(h[:, :, :], h[:, :, :], row(brow[:, ROW["beta"], :]), ALU.add))
            v.tensor_tensor(x[:, :, :], x[:, :, :], h[:, :, :], ALU.add).then_inc(x_final, 1)

        @block.tensor
        def _(t):
            t.wait_ge(loaded_consts, 16)
            t.wait_ge(zeros_ready, 1)
            t.wait_ge(loaded_w, 16)
            t.wait_ge(loaded_b, 48)
            t.matmul(PS[:, 7 * BANK:7 * BANK + SC], wt("L3_WT"), attn_sb[:, :], start=True, stop=True) \
                .then_inc(wx_summed, 1)

            def h_tile(k):
                return h[:, k, :]

            t.wait_ge(h_ready, 1)
            transposes_pe(t, h_tile, hT_summed)
            t.wait_ge(hT_ready, 1)
            t.wait_ge(wx_ready, 1)
            place_pe(t, 0)
            permute_pe(t)
            t.wait_ge(sorted_ready, 1)
            round_pe(t, 0, 0, True)
            rdeg_pe(t, 1)
            t.wait_ge(agg_ready, 1)
            node_major(t, [(hT, wt("L0_lin")), (aggT, wt("L0_agg"))], out0_summed)
            t.wait_ge(h_ready, 2)
            transposes_pe(t, h_tile, hT_summed)
            t.wait_ge(hT_ready, 2)
            round_pe(t, 1, 0, False)
            t.wait_ge(agg_ready, 2)
            sage1_pe(t)
            for k in range(2):
                t.wait_ge(act_done, 10)
                if k:
                    t.wait_ge(h1_ready, k)
                transposes_pe(t, lambda n: h1T[:, k, n * P:(n + 1) * P], h1_transposed)
            t.wait_ge(h1_ready, 2)
            wide_pe(t, 2, 0)
            t.wait_ge(agg_ready, 3)
            chain_pe(t)
            t.wait_ge(act_done, 10 + 6 * PAIRS)
            node_major(t, [(agg2T[:, 0, :], wt("fc3", 0)), (agg2T[:, 1, :], wt("fc3", D))], fc3_summed)
            t.wait_ge(h_ready, 3)
            transposes_pe(t, h_tile, hT_summed)
            t.wait_ge(hT_ready, 3)
            t.wait_ge(sorted_ready, 2)
            round_pe(t, 3, 1, True)
            rdeg_pe(t, 2)
            t.wait_ge(agg_ready, 4)
            node_major(t, [(hT, wt("L2_self")), (aggT, wt("L2_nei"))], out2_summed)
            t.wait_ge(h_ready, 4)
            transposes_pe(t, h_tile, hT_summed)
            t.wait_ge(hT_ready, 4)
            t.wait_ge(wx_ready, 1)
            for k in range(TILES):
                last = t.matmul(PS[:, 7 * BANK + k * SC:7 * BANK + (k + 1) * SC], hT[:, k * P:(k + 1) * P], Wx[:, :],
                                start=True, stop=True)
            last.then_inc(score_summed, 1)
            node_major(t, [(hT, wt("L3_W"))], proj_summed)
            t.wait_ge(proj_ready, 1)
            node_major(t, [(hT, wt("L3_self"))], self_summed)
            t.wait_ge(self_ready, 1)
            for d in range(2):
                for hd in range(HEADS):
                    at = (d * HEADS + hd) * P
                    last = t.transpose(PS[0:TILES, at:at + P], score[:, :, 8 * d + HEADS + hd], ident)
            last.then_inc(rT_summed, 1)
            t.wait_ge(rT_ready, 1)
            t.sem_inc(turned, LAP)
            t.sem_inc(er_summed, LAP)
            t.sem_inc(weighed, RING2)
            for d in range(2):
                top_pe(t, 4 + d, d)
                guard_pe(t, d)
                t.wait_ge(exb_ready, d + 1)
                weighted_pe(t, d)
                t.wait_ge(den_ready, d + 1)

        @block.scalar
        def _(a):
            def copy_hT(n):
                a.wait_ge(hT_summed, n)
                a.copy(hT[:, :], PS[:, 0:NP_]).then_inc(hT_ready, 1)

            a.wait_ge(wx_summed, 1)
            a.copy(Wx[:, :], PS[:, 7 * BANK:7 * BANK + SC]).then_inc(wx_ready, 1)
            norm_act(a, 0)
            copy_hT(1)
            a.wait_ge(sorted_ready, 1)
            round_act(a, 0, 0)
            a.wait_ge(out0_summed, 1)
            a.activation(h[:, :, :], PS[:, 0:NP_].rearrange("p (t f) -> p t f", t=TILES), ACT.Square) \
                .then_inc(square_ready, 1)
            a.wait_ge(sumsq_ready, 1)
            a.activation(st[:, 7, :], st[:, 6, :], ACT.Sqrt).then_inc(len_ready, 1)
            norm_act(a, 1)
            copy_hT(2)
            round_act(a, 1, 0)
            sage1_act(a)
            for k in range(2):
                a.wait_ge(h1_transposed, k + 1)
                a.copy(h[:, :, :] if k == 0 else h1N, PS[:, 0:NP_].rearrange("p (t f) -> p t f", t=TILES)) \
                    .then_inc(h1_ready, 1)
            round_act(a, 2, 0)
            chain_act(a)
            a.wait_ge(z_ready, 1)
            act_link(a.activation(scr, h[:, :, :], ACT.Abs))
            act_link(a.activation(scr, scr, ACT.Exp, scale=-1.0))
            a.activation(scr, scr, ACT.Ln, bias=1.0).then_inc(log_ready, 1)
            norm_act(a, 2)
            copy_hT(3)
            a.wait_ge(sorted_ready, 2)
            round_act(a, 3, 1)
            norm_act(a, 3)
            copy_hT(4)
            a.wait_ge(rT_ready, 1)
            a.sem_inc(ohT_ready, LAP)
            for d in range(2):
                (late_top_act if d else top_act)(a, 4 + d, d)
                guard_act(a, d)
                weighted_act(a, d)
            norm_act(a, 4)


def pack_consts():
    c = np.zeros((P, C_ALL), np.float32)
    c[:, C_ID:C_ID + P] = np.eye(P)
    c[:, C_TRI:C_TRI + P] = np.triu(np.ones((P, P)), 1)
    c[:, C_TRII:C_TRII + P] = np.triu(np.ones((P, P)), 0)
    c[:, C_IOTA:C_IOTA + CHUNKS] = np.arange(CHUNKS)
    c[:, C_ONE:C_ONE + P] = 1.0
    c[:TILES - 1, C_MASK] = -1.0
    for part in range(SPLIT):
        for hd in range(HEADS):
            c[part * HEADS + hd, C_PICK + hd * P:C_PICK + (hd + 1) * P] = 1.0
    return c


def pack_weights(g):
    def tr(w):
        wt = np.asarray(w).T
        return [wt[k:k + P] for k in range(0, wt.shape[0], P)]

    blocks = {"L0_lin": tr(g("L0_gnn_W_lin")), "L0_agg": tr(g("L0_gnn_W_agg")), "l1": tr(g("L1_gnn_W_l1")),
              "r1": tr(g("L1_gnn_W_r1")), "l2": tr(g("L1_gnn_W_l2")), "r2": tr(g("L1_gnn_W_r2")),
              "res1": tr(g("L1_gnn_res1_W")), "res2": tr(g("L1_gnn_res2_W")), "fc1": tr(g("L1_gnn_fc1_W")),
              "fc2": tr(g("L1_gnn_fc2_W")), "fc3": tr(g("L1_gnn_fc3_W")), "L2_self": tr(g("L2_gnn_W_self")),
              "L2_nei": tr(g("L2_gnn_W_nei")), "L3_W": [g("L3_gnn_W")], "L3_self": [g("L3_gnn_W_self")],
              "L3_WT": [g("L3_gnn_W").T]}
    return np.concatenate([b for n, _ in _W for b in blocks[n]], axis=1)


def pack_bias_cols(g):
    names = {"b_l1": "b_l1", "b_l2": "b_l2", "res1": "res1_b", "res2": "res2_b", "fc1": "fc1_b", "fc2": "fc2_b"}
    c = np.zeros((P, B_ALL), np.float32)
    for n, at in BCOL.items():
        c[:, at:at + 2] = g("L1_gnn_" + names[n]).reshape(2, P).T
    return c


def pack_attn(g):
    c = np.zeros((P, SC), np.float32)
    for d, name in enumerate(("L3_gnn_a_in", "L3_gnn_a_out")):
        for role in range(2):
            for hd in range(HEADS):
                c[hd * HD:(hd + 1) * HD, d * 8 + role * HEADS + hd] = g(name)[hd, role * HD:(role + 1) * HD]
    return c


def kernel(**inp):
    import concourse.bacc as bacc
    from concourse.bass_utils import run_bass_kernel_spmd

    def g(name):
        return np.asarray(inp[name])

    nc = bacc.Bacc("TRN2", target_bir_lowering=False, num_devices=1)
    rows = ["L1_gnn_fc3_b", "L2_gnn_b_self", "L2_gnn_b_nei", "L3_gnn_bias", "L3_gnn_ln_gamma", "L3_gnn_ln_beta"]
    arrays = {"edges": np.stack([g("src"), g("dst")]), "x_in": g("x"), "consts": pack_consts(),
              "weights": pack_weights(g), "bias_cols": pack_bias_cols(g), "bias_rows": np.stack([g(n) for n in rows]),
              "attn": pack_attn(g)}
    ap = {n: nc.dram_tensor(n, a.shape, mybir.dt.from_np(a.dtype), kind="ExternalInput").ap()
          for n, a in arrays.items()}
    out = nc.dram_tensor("out", [N_NODES, D], F32, kind="ExternalOutput").ap()
    gnn_kernel(nc, *ap.values(), out)
    r = run_bass_kernel_spmd(nc, [arrays], core_ids=[0])
    return r.results[0]["out"]
```

```python
from contextlib import ExitStack

import numpy as np
import concourse.bass as bass
from concourse import mybir

F32 = mybir.dt.float32
F16 = mybir.dt.float16
BF16 = mybir.dt.bfloat16
I32 = mybir.dt.int32
ALU = mybir.AluOpType
ACT = mybir.ActivationFunctionType
AX_X = mybir.AxisListType.X

P = 128
N_NODES, N_EDGES, D = 3125, 50000, 128
TILES = -(-N_NODES // P)
NP_ = TILES * P
TAIL = N_NODES - (TILES - 1) * P
EP = 125
EC = N_EDGES // EP
GROUP = 8
CHUNKS = -(-(N_EDGES // P + TILES) // (2 * GROUP)) * 2 * GROUP
STEPS = CHUNKS // (2 * GROUP)
SLOTS = 2 * GROUP
QUAD = 4
GROUPS = 2 * STEPS
LAP = 4
LAPS = GROUPS // LAP
AHEAD_OH, AHEAD_T = 3, 2
BLK = 400
NBLK = NP_ // BLK
HEADS, HD = 4, 32
H1 = 256
SC = 4 * HEADS
SPLIT = 3
ROW_ATT = D + SPLIT * HEADS
RING1 = 3
NEG_BIG = -float(2.0 ** 100)
BANK = 512
DEG_COL = NP_

C_ID, C_TRI, C_TRII, C_IOTA, C_ONE, C_MASK = 0, 128, 256, 384, 384 + CHUNKS, 384 + CHUNKS + 128
C_PICK = C_MASK + 1
C_ALL = C_PICK + HEADS * P

_W = [("L0_lin", D), ("L0_agg", D), ("l1", H1), ("r1", H1), ("l2", 2 * H1), ("r2", 2 * H1), ("res1", H1),
      ("res2", H1), ("fc1", 2 * H1), ("fc2", 2 * H1), ("fc3", 2 * D), ("L2_self", D), ("L2_nei", D),
      ("L3_W", D), ("L3_self", D), ("L3_WT", D)]
W_AT = {}
_at = 0
for _n, _c in _W:
    W_AT[_n] = _at
    _at += _c
W_ALL = _at
BCOL = {"b_l1": 0, "b_l2": 2, "res1": 4, "res2": 6, "fc1": 8, "fc2": 10}
B_ALL = 12
ROW = {"fc3": 0, "L2_self": 1, "L2_nei": 2, "L3_bias": 3, "gamma": 4, "beta": 5}
ROWS = 6


def linker(eng, sem):
    count = [0]

    def link(ins):
        count[0] += 1
        ins.then_inc(sem, 1)
        eng.wait_ge(sem, count[0])

    return link


def gnn_kernel(nc, edges, x_in, consts, weights, bias_cols, bias_rows, attn, out):
    with ExitStack() as ctx:
        def sb(name, shape, dt=F32):
            return ctx.enter_context(nc.sbuf_tensor(name, shape, dt))

        def sem(name):
            return ctx.enter_context(nc.semaphore(name))

        def dram(name, shape):
            return nc.dram_tensor(name, shape, F32, kind="Internal").ap()

        PS = ctx.enter_context(nc.psum_tensor("PS", [P, 8 * BANK], F32))

        cst = sb("cst", [P, C_ALL])
        ident, tri, tri_incl = cst[:, C_ID:C_ID + P], cst[:, C_TRI:C_TRI + P], cst[:, C_TRII:C_TRII + P]
        iota = cst[:, C_IOTA:C_IOTA + CHUNKS]
        ones = cst[:, C_ONE:C_ONE + P]
        neg_mask = cst[:, C_MASK:C_MASK + 1]
        iota_h = sb("iota_h", [P, CHUNKS], F16)
        ident_b = sb("ident_b", [P, P], BF16)
        big_id = sb("big_id", [P, P], BF16)
        pick = sb("pick", [P, HEADS, P], BF16)
        zeros = sb("zeros", [P, BANK], BF16)
        eps = sb("eps", [P, 2])
        W = sb("W", [P, W_ALL])
        bcol = sb("bcol", [P, B_ALL])
        bcol_m1 = sb("bcol_m1", [P, B_ALL])
        brow = sb("brow", [P, ROWS, D])
        rowsum = sb("rowsum", [P, D])
        attn_sb = sb("attn_sb", [P, SC])
        Wx = sb("Wx", [P, SC])

        x = sb("x", [P, TILES, D])
        h = sb("h", [P, TILES, D])
        hT = sb("hT", [P, NP_])
        rdeg = sb("rdeg", [P, NP_])
        st = sb("st", [P, 8, TILES])
        score = sb("score", [P, TILES, SC])
        parts = sb("parts", [P, 2, TILES, SPLIT * HEADS])
        part_h = sb("part_h", [P, TILES * HEADS], BF16)
        rT = sb("rT", [TILES, 2, HEADS, P])
        rden = sb("rden", [P, 2, TILES * HEADS])

        e_i = sb("e_i", [EP, 2, EC], I32)
        idx = sb("idx", [P, 2, CHUNKS], I32)
        key = sb("key", [P, 2, CHUNKS])
        tile_off = sb("tile_off", [1, 2, CHUNKS], I32)
        chunk_tile = sb("chunk_tile", [P, 2, CHUNKS])
        tile_sel = sb("tile_sel", [TILES, 2, CHUNKS])
        cnt = sb("cnt", [P, 6, TILES])
        cnt_i = sb("cnt_i", [P, 2, TILES], I32)
        col = sb("col", [TILES, 4])
        col_i = sb("col_i", [TILES, 2], I32)

        G = sb("G", [P, SLOTS, ROW_ATT])
        OH = sb("OH", [P, SLOTS, P])
        sT = sb("sT", [P, SLOTS, P], BF16)
        idxbuf = sb("idxbuf", [P, 2, GROUP], I32)
        idxbuf1 = sb("idxbuf1", [P, RING1, GROUP], I32)
        score_buf = sb("score_buf", [P, 2, GROUP, SPLIT * HEADS], BF16)
        exs = sb("exs", [P, 2, GROUP, SPLIT * HEADS], BF16)
        G_flat = G[:, :, :].rearrange("p s f -> p (s f)")
        OH_flat = OH[:, :, :].rearrange("p s e -> p (s e)")

        U = 5
        U0 = 4
        ACT_COLS = 3
        work = sb("work", [P, max(U * (CHUNKS + P), RING1 * GROUP * ROW_ATT)])
        big = sb("big", [P, 5 * NP_])
        masks = big[0:EP, 0:TILES * EC // 2].bitcast(BF16)
        scan = big[0:EP, TILES * EC // 2:TILES * EC // 2 * 3]
        scan_cmp = big[0:TILES, TILES * EC // 2 * 3:TILES * EC // 2 * 3 + 2 * CHUNKS].rearrange("p (a b) -> p a b", a=2)
        sort_v = big[0:EP, 0:4 * EC].rearrange("p (a b) -> p a b", a=4)
        lo_keep = big[:, 4 * EC:4 * EC + CHUNKS]
        cmp_i = big[:, 4 * EC + CHUNKS:4 * EC + 3 * CHUNKS].bitcast(I32).rearrange("p (a b) -> p a b", a=2)
        ev_i = work[0:EP, 0:3 * EC].bitcast(I32).rearrange("p (a b) -> p a b", a=3)
        tl = work[0:EP, 3 * EC:4 * EC]
        A0 = [m[0:EP, g * U0 * CHUNKS // 2:(g + 1) * U0 * CHUNKS // 2].bitcast(F16).rearrange("p (j c) -> p j c", j=U0)
              for m in (G_flat, OH_flat) for g in range(2)]
        B0 = work[0:EP, 0:4 * U0 * P].bitcast(F16).rearrange("p (g j k c) -> p g j k c", g=4, j=U0, k=2)
        eq0 = work[0:EP, 4 * U0 * P:6 * U0 * P].bitcast(F16).rearrange("p (g j c) -> p g j c", g=4, j=U0)
        A = work[0:EP, 0:U * CHUNKS].bitcast(F16).rearrange("p (g j c) -> p g j c", g=2, j=U)
        B = work[0:EP, U * CHUNKS:U * (CHUNKS + P)].bitcast(F16).rearrange("p (g j c) -> p g j c", g=2, j=U)
        h1T = big[:, 0:2 * NP_].rearrange("p (c n) -> p c n", c=2)
        agg2T = big[:, 2 * NP_:4 * NP_].rearrange("p (c n) -> p c n", c=2)
        h1N = agg2T[:, 0, :].rearrange("p (t f) -> p t f", t=TILES)
        aggT = big[:, 4 * NP_:5 * NP_]
        scr = aggT.rearrange("p (t f) -> p t f", t=TILES)
        narrow = [G[:, s, 0:D] for s in range(SLOTS)]
        wide = [(G_flat if s < GROUP else work)[:, s % GROUP * H1:(s % GROUP + 1) * H1] for s in range(SLOTS)]
        blk = work[:, 0:8 * BLK].rearrange("p (x o c n) -> p x o c n", x=2, o=2, c=2)
        EDGE = HEADS * CHUNKS
        RING2 = LAP
        ring1 = work[:, 0:RING1 * GROUP * ROW_ATT].rearrange("p (b j f) -> p b j f", b=RING1, j=GROUP)
        ring2 = big[:, 0:RING2 * GROUP * D].rearrange("p (b j f) -> p b j f", b=RING2, j=GROUP)
        mrb = big[:, 0:3 * EDGE].bitcast(BF16).rearrange("p (s q k) -> p s q k", s=SPLIT, q=2 * HEADS)
        cmax = big[:, 3 * EDGE:4 * EDGE].rearrange("p (h k) -> p h k", h=HEADS)
        mr = big[:, 4 * EDGE:6 * EDGE].rearrange("p (q k) -> p q k", q=2 * HEADS)
        ex_rest = big[:, 4 * EDGE:5 * EDGE].rearrange("p (h k) -> p h k", h=HEADS)
        er = big[:, 6 * EDGE:8 * EDGE].rearrange("p (q k) -> p q k", q=2 * HEADS)
        exb = big[:, 6 * EDGE:6 * EDGE + SPLIT * EDGE // 2].bitcast(BF16) \
            .rearrange("p (s h k) -> p s h k", s=SPLIT, h=HEADS)
        ex = big[:, 8 * EDGE:9 * EDGE].rearrange("p (h k) -> p h k", h=HEADS)
        sender = hT[:, 0:EDGE].rearrange("p (h k) -> p h k", h=HEADS)
        reset = hT[:, EDGE:EDGE + 2 * CHUNKS].rearrange("p (a k) -> p a k", a=2)
        comb = rdeg[:, :].rearrange("p (t f) -> p t f", t=TILES)
        sE = [a[:, 0:SPLIT * EDGE // 2].bitcast(BF16).rearrange("p (k c) -> p k c", c=SPLIT * HEADS)
              for a in (h[:, :, :].rearrange("p t f -> p (t f)"), W)]
        OHb = OH[:, :, :].bitcast(BF16)[:, :, 0:P]
        eq = OH_flat.bitcast(BF16).rearrange("p (g j e) -> p g j e", g=LAP, j=GROUP)
        OHw = G_flat[:, 0:GROUP * P].bitcast(BF16).rearrange("p (g j e) -> p g j e", g=2, j=GROUP)
        ohT = G_flat[:, 0:LAP * GROUP * P // 2].bitcast(BF16).rearrange("p (g j e) -> p g j e", g=LAP, j=GROUP)

        T = {n: dram(f"T_{n}", [NP_, w]) for n, w in (("h0", D), ("h1", D), ("g", H1), ("h2", D))}
        T_att = [dram(f"T_att{d}", [NP_, ROW_ATT]) for d in range(2)]
        spill = [dram(f"spill{d}", [P, CHUNKS * D]) for d in range(2)]

        dve_step, act_step, pool_step = sem("dve_step"), sem("act_step"), sem("pool_step")
        loaded_edges, loaded_consts, loaded_x = sem("loaded_edges"), sem("loaded_consts"), sem("loaded_x")
        loaded_w, loaded_b = sem("loaded_w"), sem("loaded_b")
        zeros_ready, x_cleared = sem("zeros_ready"), sem("x_cleared")
        counts_ready, counts_summed = sem("counts_ready"), sem("counts_summed")
        chunks_ready, chunks_summed = sem("chunks_ready"), sem("chunks_summed")
        bounds_ready, tiles_summed = sem("bounds_ready"), sem("tiles_summed")
        placed = sem("placed")
        eq_ready, payload_ready, perm0_used = sem("eq_ready"), sem("payload_ready"), sem("perm0_used")
        where_ready, perm_used = sem("where_ready"), sem("perm_used")
        sorted_ready = sem("sorted_ready")
        table = {n: sem(f"table_{n}") for n in ("h0", "h1", "g", "h2", "att0", "att1")}
        idx_ready = sem("idx_ready")
        landed = [sem(f"landed{i}") for i in range(SLOTS)]
        oh_ready = sem("oh_ready")
        used = [sem(f"used{i}") for i in range(2)]
        round_done = sem("round_done")
        gathers_begun = sem("gathers_begun")
        spills_begun = sem("spills_begun")
        chunks_here, added = sem("chunks_here"), sem("added")
        deg_read, sums_copied, rdeg_kept = sem("deg_read"), sem("sums_copied"), sem("rdeg_kept")
        diag_ready, rdeg_summed, agg_ready = sem("diag_ready"), sem("rdeg_summed"), sem("agg_ready")
        var_ready, std_ready, rstd_ready = sem("var_ready"), sem("std_ready"), sem("rstd_ready")
        h_ready, hT_summed, hT_ready = sem("h_ready"), sem("hT_summed"), sem("hT_ready")
        out0_summed, square_ready = sem("out0_summed"), sem("square_ready")
        sumsq_ready, len_ready = sem("sumsq_ready"), sem("len_ready")
        lin_ready, exp_ready, clipped = sem("lin_ready"), sem("exp_ready"), sem("clipped")
        elu_done, act_done = sem("elu_done"), sem("act_done")
        h1_transposed, h1_ready = sem("h1_transposed"), sem("h1_ready")
        fc3_summed, z_ready, log_ready = sem("fc3_summed"), sem("z_ready"), sem("log_ready")
        out2_summed = sem("out2_summed")
        wx_summed, wx_ready = sem("wx_summed"), sem("wx_ready")
        proj_summed, proj_ready = sem("proj_summed"), sem("proj_ready")
        score_summed, parts_ready = sem("score_summed"), sem("parts_ready")
        self_summed, self_ready = sem("self_summed"), sem("self_ready")
        rT_summed, rT_ready = sem("rT_summed"), sem("rT_ready")
        sT_summed, sT_ready = sem("sT_summed"), sem("sT_ready")
        masked_ready, reduced = sem("masked_ready"), sem("reduced")
        recv_summed, mr_ready, mrb_ready = sem("recv_summed"), sem("mr_ready"), sem("mrb_ready")
        idx_copied, scores_here, scores_brought = sem("idx_copied"), sem("scores_here"), sem("scores_brought")
        landed1 = [sem(f"landed1_{b}") for b in range(RING1)]
        spilled1 = [sem(f"spilled1_{b}") for b in range(RING1)]
        oh_again, turned, ohT_ready = sem("oh_again"), sem("turned"), sem("ohT_ready")
        er_summed, er_ready = sem("er_summed"), sem("er_ready")
        arg_ready, ex_ready, exb_ready = sem("arg_ready"), sem("ex_ready"), sem("exb_ready")
        spilled = [sem(f"spilled{i}") for i in range(2)]
        back = [sem(f"back{i}") for i in range(RING2)]
        oh_third, oh_cast, scaled_ready = sem("oh_third"), sem("oh_cast"), sem("scaled_ready")
        weighed, weighted_done, den_ready = sem("weighed"), sem("weighted_done"), sem("den_ready")
        x_final, stored = sem("x_final"), sem("stored")

        dve_link = linker(nc.vector, dve_step)
        pool_link = linker(nc.gpsimd, pool_step)
        act_link = linker(nc.scalar, act_step)
        block = ctx.enter_context(nc.Block())

        COUNT, EARLIER, TOTAL, UPTO, TILE_AT = 7 * BANK, 7 * BANK + TILES, 7 * BANK + 50, 7 * BANK + 51, 7 * BANK + 96
        PASS_GROUPS = EC // U

        def place_dve(v, d, pause):
            k_i, o_i = e_i[:, 1 - d, :], e_i[:, d, :]
            a, b, lo, hi = (sort_v[:, i, :] for i in range(4))
            dve_link(v.tensor_scalar(ev_i[:, 0, :], k_i, 7, None, ALU.arith_shift_right))
            dve_link(v.tensor_copy(tl, ev_i[:, 0, :]))
            m3 = masks.rearrange("p (t j) -> p t j", t=TILES)
            s3 = scan.rearrange("p (t j) -> p t j", t=TILES)
            dve_link(v.tensor_tensor(m3, iota[0:EP, 0:TILES].unsqueeze(2).to_broadcast([EP, TILES, EC]),
                                     tl.unsqueeze(1).to_broadcast([EP, TILES, EC]), ALU.is_equal))
            pause(1)
            dve_link(v.tensor_tensor_scan(scan, masks, masks, 0.0, ALU.add, ALU.max))
            pause(2)
            end, n, before, first = (cnt[0:EP, i, :] for i in range(4))
            dve_link(v.tensor_copy(end, s3[:, :, EC - 1]))
            v.tensor_copy(before[:, 1:TILES], end[:, 0:TILES - 1])
            dve_link(v.memset(before[:, 0:1], 0.0))
            v.tensor_tensor(n, end, before, ALU.subtract).then_inc(counts_ready, 1)
            v.wait_ge(counts_summed, d + 1)
            totb = cnt[:, 5, :]
            dve_link(v.tensor_scalar(cnt_i[:, 0, :], PS[:, COUNT:COUNT + TILES], float(P - 1), None, ALU.add))
            dve_link(v.tensor_scalar(cnt_i[:, 1, :], cnt_i[:, 0, :], 7, None, ALU.arith_shift_right))
            dve_link(v.tensor_copy(totb, cnt_i[:, 1, :]))
            dve_link(v.tensor_tensor(before, PS[0:EP, EARLIER:EARLIER + TILES], before, ALU.subtract))
            dve_link(v.tensor_scalar(col_i[:, 0:1], PS[0:TILES, TOTAL:TOTAL + 1], float(P - 1), None, ALU.add))
            dve_link(v.tensor_scalar(col_i[:, 1:2], col_i[:, 0:1], 7, None, ALU.arith_shift_right))
            v.tensor_copy(col[:, 0:1], col_i[:, 1:2]).then_inc(chunks_ready, 1)
            v.wait_ge(chunks_summed, d + 1)
            dve_link(v.tensor_copy(col[:, 1:2], PS[0:TILES, UPTO:UPTO + 1]))
            dve_link(v.tensor_tensor(col[:, 2:3], col[:, 1:2], col[:, 0:1], ALU.subtract))
            past, since = scan_cmp[:, 0, :], scan_cmp[:, 1, :]
            v.tensor_scalar(past, iota[0:TILES, :], col[:, 1:2], None, ALU.is_ge).then_inc(bounds_ready, 1)
            v.wait_ge(bounds_ready, d + 1)
            dve_link(v.tensor_scalar(since, iota[0:TILES, :], col[:, 2:3], None, ALU.is_ge))
            dve_link(v.scalar_tensor_tensor(tile_sel[:, d, :], past, neg_mask[0:TILES, :], since, ALU.mult, ALU.add))
            v.wait_ge(tiles_summed, d + 1)
            v.tensor_copy(chunk_tile[:, d, :], PS[:, TILE_AT:TILE_AT + CHUNKS])
            dve_link(v.tensor_copy(tile_off[0:1, d, :], PS[0:1, TILE_AT:TILE_AT + CHUNKS]))
            dve_link(v.tensor_tensor_scan(cnt[:, 4, :], totb, totb, 0.0, ALU.add, ALU.max))
            dve_link(v.tensor_tensor(cnt[:, 3, :], cnt[:, 4, :], totb, ALU.subtract))
            dve_link(v.tensor_scalar(first, first, float(P), -1.0, ALU.mult, ALU.add))
            dve_link(v.tensor_tensor(first, first, before, ALU.add))
            dve_link(v.tensor_tensor(s3, s3, first.unsqueeze(2).to_broadcast([EP, TILES, EC]), ALU.add))
            pause(3)
            dve_link(v.tensor_tensor(s3, s3, m3, ALU.mult))
            pause(4)
            dve_link(v.tensor_reduce(tl, scan.rearrange("p (t j) -> p j t", t=TILES), AX_X, ALU.add))
            pause(5)
            dve_link(v.tensor_copy(ev_i[:, 0, :], tl))
            dve_link(v.tensor_scalar(ev_i[:, 1, :], ev_i[:, 0, :], 7, None, ALU.arith_shift_right))
            dve_link(v.tensor_scalar(ev_i[:, 2, :], ev_i[:, 0, :], P - 1, None, ALU.bitwise_and))
            dve_link(v.tensor_copy(a, ev_i[:, 1, :]))
            dve_link(v.tensor_copy(b, ev_i[:, 2, :]))
            dve_link(v.tensor_scalar(ev_i[:, 1, :], k_i, P - 1, None, ALU.bitwise_and))
            dve_link(v.tensor_scalar(ev_i[:, 2, :], o_i, 256.0, 1.0, ALU.mult, ALU.add))
            dve_link(v.tensor_tensor(ev_i[:, 0, :], ev_i[:, 1, :], ev_i[:, 2, :], ALU.add))
            dve_link(v.tensor_scalar(ev_i[:, 1, :], ev_i[:, 0, :], 1023, None, ALU.bitwise_and))
            dve_link(v.tensor_scalar(ev_i[:, 2, :], ev_i[:, 0, :], 10, None, ALU.arith_shift_right))
            dve_link(v.tensor_copy(lo, ev_i[:, 1, :]))
            dve_link(v.tensor_copy(hi, ev_i[:, 2, :]))

        def where_group(v, n, g, at, k):
            v.wait_ge(perm_used, n + 1)
            for j in range(U):
                c = bass.ds(at + j, 1)
                v.tensor_scalar(A[:, g, j, :], iota_h[0:EP, :], sort_v[:, 0, c], None, ALU.is_equal)
                last = v.tensor_scalar(B[:, g, j, :], iota_h[0:EP, 0:P], sort_v[:, 1, c], sort_v[:, 2 + k, c],
                                       ALU.is_equal, ALU.mult)
            last.then_inc(where_ready, 1)

        def perm_group(t, n, g):
            t.wait_ge(where_ready, n + 1)
            for j in range(U):
                last = add_to(t, PS[:, 7 * BANK:7 * BANK + CHUNKS], B[:, g, j, :], A[:, g, j, :])
            last.then_inc(perm_used, 1)

        def clear_bank(t, k):
            t.matmul(PS[:, k * BANK:k * BANK + CHUNKS], zeros[:, 0:P], zeros[:, 0:CHUNKS], start=True, stop=False,
                     skip_group_check=True)

        def decode_dve(v, d, lo, hi):
            dve_link(v.scalar_tensor_tensor(cmp_i[:, 0, :], hi, 1024.0, lo, ALU.mult, ALU.add))
            dve_link(v.tensor_scalar(idx[:, d, :], cmp_i[:, 0, :], 8, None, ALU.arith_shift_right))
            dve_link(v.tensor_scalar(cmp_i[:, 1, :], cmp_i[:, 0, :], 255, None, ALU.bitwise_and))
            v.tensor_scalar(key[:, d, :], cmp_i[:, 1, :], -1.0, None, ALU.add).then_inc(sorted_ready, 1)

        LAPS0 = EC // (4 * U0)

        def permute_dve(v):
            def group(i, g, first=False):
                if not first:
                    v.wait_ge(perm0_used, 4 * i + g - 3)
                for j in range(U0):
                    c = bass.ds((4 * i + g) * U0 + j, 1)
                    v.tensor_scalar(A0[g][:, j, :], iota_h[0:EP, :], sort_v[:, 0, c], None, ALU.is_equal)
                    if j < ACT_COLS:
                        last = v.tensor_scalar(eq0[:, g, j, :], iota_h[0:EP, 0:P], sort_v[:, 1, c], None, ALU.is_equal)
                    else:
                        for k in range(2):
                            last = v.tensor_scalar(B0[:, g, j, k, :], iota_h[0:EP, 0:P], sort_v[:, 1, c],
                                                   sort_v[:, 2 + k, c], ALU.is_equal, ALU.mult)
                last.then_inc(eq_ready, 1)

            for g in range(4):
                group(0, g, True)
            with v.Fori(1, LAPS0) as i:
                for g in range(4):
                    group(i, g)
            v.wait_ge(perm0_used, 4 * LAPS0)
            dve_link(v.tensor_copy(lo_keep, PS[:, 4 * BANK:4 * BANK + CHUNKS]))
            decode_dve(v, 0, lo_keep, PS[:, 5 * BANK:5 * BANK + CHUNKS])

        def permute_act(a):
            with a.Fori(0, LAPS0) as i:
                for g in range(4):
                    a.wait_ge(eq_ready, 4 * i + g + 1)
                    for j in range(ACT_COLS):
                        for k in range(2):
                            c = bass.ds((4 * i + g) * U0 + j, 1)
                            last = a.activation(B0[:, g, j, k, :], eq0[:, g, j, :], ACT.Copy, scale=sort_v[:, 2 + k, c])
                    last.then_inc(payload_ready, 1)

        def permute_pe(t):
            for k in (4, 5):
                clear_bank(t, k)
            with t.Fori(0, LAPS0) as i:
                for g in range(4):
                    t.wait_ge(payload_ready, 4 * i + g + 1)
                    for j in range(U0):
                        for k in range(2):
                            at = (4 + k) * BANK
                            last = add_to(t, PS[:, at:at + CHUNKS], B0[:, g, j, k, :], A0[g][:, j, :])
                    last.then_inc(perm0_used, 1)

        def place_pe(t, d):
            t.wait_ge(counts_ready, d + 1)
            n = cnt[0:EP, 1, :]
            t.matmul(PS[:, COUNT:COUNT + TILES], ones[0:EP, :], n, start=True, stop=True)
            t.matmul(PS[0:EP, EARLIER:EARLIER + TILES], tri[0:EP, 0:EP], n, start=True, stop=True)
            t.matmul(PS[0:TILES, TOTAL:TOTAL + 1], n, ones[0:EP, 0:1], start=True, stop=True).then_inc(counts_summed, 1)
            t.wait_ge(chunks_ready, d + 1)
            t.matmul(PS[0:TILES, UPTO:UPTO + 1], tri_incl[0:TILES, 0:TILES], col[:, 0:1],
                     start=True, stop=True).then_inc(chunks_summed, 1)
            t.wait_ge(bounds_ready, d + 1)
            t.matmul(PS[:, TILE_AT:TILE_AT + CHUNKS], ones[0:TILES - 1, :], scan_cmp[0:TILES - 1, 0, :],
                     start=True, stop=True).then_inc(tiles_summed, 1)

        STEP_GROUPS = 4
        BEHIND = (STEPS - PASS_GROUPS // STEP_GROUPS, 1)

        def base(r):
            return r * STEPS

        def round_act(a, r, d, then=None):
            def step(i, half, first):
                if r or not first:
                    a.wait_ge(used[half], base(r) + i)
                c = bass.ds(i * SLOTS + half * GROUP, GROUP)
                a.copy(idxbuf[:, half, :], idx[:, d, c]).then_inc(idx_ready, 1)

            for half in range(2):
                step(0, half, True)
            if then is not None:
                then()
            with a.Fori(1, STEPS) as i:
                for half in range(2):
                    step(i, half, False)

        def round_pool(p, r, table, slots):
            def step(i):
                for half in range(2):
                    p.wait_ge(idx_ready, 2 * (base(r) + i) + half + 1)
                    p.sem_inc(gathers_begun)
                    for j in range(GROUP):
                        s = half * GROUP + j
                        p.indirect_dma_start(out=slots[s], out_offset=None, in_=table[:, :],
                                             in_offset=bass.IndirectOffsetOnAxis(ap=idxbuf[:, half, j:j + 1], axis=0)) \
                            .then_inc(landed[s], 16)

            with p.Fori(0, STEPS) as i:
                step(i)

        def one_hots(v, r, d, i, half, first=False):
            if r or not first:
                v.wait_ge(used[half], base(r) + i)
            c = bass.ds(i * SLOTS + half * GROUP, GROUP)
            v.tensor_tensor(OH[:, half * GROUP:(half + 1) * GROUP, :],
                            iota[:, 0:P].unsqueeze(1).to_broadcast([P, GROUP, P]),
                            key[:, d, c].unsqueeze(2).to_broadcast([P, GROUP, P]), ALU.is_equal).then_inc(oh_ready, 1)

        def round_dve(v, r, d, begin=1):
            if begin == 1:
                for half in range(2):
                    one_hots(v, r, d, 0, half, True)
            last = STEPS
            if r < 2:
                last = BEHIND[r] + PASS_GROUPS // STEP_GROUPS
                with v.Fori(BEHIND[r], last) as i:
                    for half in range(2):
                        one_hots(v, r, d, i, half)
                        for g in range(2):
                            n = (i - BEHIND[r]) * STEP_GROUPS + 2 * half + g
                            where_group(v, PASS_GROUPS * r + n, g, n * U, r)
                begin = last
            if begin < STEPS:
                with v.Fori(begin, STEPS) as i:
                    for half in range(2):
                        one_hots(v, r, d, i, half)
            if r < 2:
                v.wait_ge(perm_used, 2 + PASS_GROUPS * (r + 1))
                payload = PS[:, 7 * BANK:7 * BANK + CHUNKS]
                if r == 0:
                    dve_link(v.tensor_copy(lo_keep, payload))
                else:
                    decode_dve(v, 1, lo_keep, payload)

        def load_tiles(t, d, c):
            regs = [t.alloc_register(f"off{j}_{nc.next_id()}") for j in range(GROUP)]
            t.load(regs, tile_off[0:1, d, c])
            return [t.snap(g, min_val=0, max_val=TILES - 1) for g in regs]

        def clear_psum(t):
            for k in range(7):
                t.matmul(PS[:, k * BANK:(k + 1) * BANK], zeros[:, 0:P], zeros[:, 0:BANK], start=True, stop=False,
                         skip_group_check=True)

        def add_to(t, where, lhsT, rhs):
            return t.matmul(where, lhsT, rhs, start=False, stop=True, skip_group_check=True)

        def round_pe(t, r, d, degrees):
            clear_psum(t)

            def step(i, behind):
                for half in range(2):
                    tiles = load_tiles(t, d, bass.ds(i * SLOTS + half * GROUP, GROUP))
                    t.wait_ge(oh_ready, 2 * (base(r) + i) + half + 1)
                    for j in range(GROUP):
                        s = half * GROUP + j
                        t.wait_ge(landed[s], 16 * (base(r) + i + 1))
                        last = add_to(t, PS[:, bass.ds(tiles[j] * P, P)], G[:, s, 0:D], OH[:, s, :])
                        if degrees:
                            last = add_to(t, PS[:, bass.ds(tiles[j] + DEG_COL, 1)], OH[:, s, :], ones[:, 0:1])
                    last.then_inc(used[half], 1)
                    if behind:
                        for g in range(2):
                            n = (i - BEHIND[r]) * STEP_GROUPS + 2 * half + g
                            perm_group(t, PASS_GROUPS * r + n, g)

            begin = 0
            if r == 0:
                with t.Fori(0, 2) as i:
                    step(i, False)
                place_pe(t, 1)
                begin = 2
            if r < 2:
                with t.Fori(begin, BEHIND[r]) as i:
                    step(i, False)
                t.wait_ge(where_ready, PASS_GROUPS * r + 1)
                clear_bank(t, 7)
                begin = BEHIND[r] + PASS_GROUPS // STEP_GROUPS
                with t.Fori(BEHIND[r], begin) as i:
                    step(i, True)
            if begin < STEPS:
                with t.Fori(begin, STEPS) as i:
                    step(i, False)
            for half in range(2):
                t.wait_ge(used[half], base(r + 1))
            t.drain().then_inc(round_done, 1)

        def wide_pe(t, r, d):
            clear_psum(t)
            with t.Fori(0, STEPS) as i:
                for half in range(2):
                    tiles = load_tiles(t, d, bass.ds(i * SLOTS + half * GROUP, GROUP))
                    t.wait_ge(oh_ready, 2 * (base(r) + i) + half + 1)
                    for q in range(2):
                        t.wait_ge(added, i * SLOTS + half * GROUP + q * QUAD + 1)
                        for j in range(q * QUAD, (q + 1) * QUAD):
                            s = half * GROUP + j
                            t.wait_ge(landed[s], 16 * (base(r) + i + 1))
                            at = 7 * BANK + (j % QUAD) * P
                            last = t.matmul(PS[:, at:at + P], wide[s][:, D:], OH[:, s, :], start=True, stop=True)
                        last.then_inc(chunks_here, 1)
                        for j in range(q * QUAD, (q + 1) * QUAD):
                            s = half * GROUP + j
                            last = add_to(t, PS[:, bass.ds(tiles[j] * P, P)], wide[s][:, 0:D], OH[:, s, :])
                    last.then_inc(used[half], 1)
            for half in range(2):
                t.wait_ge(used[half], base(r + 1))
            t.drain().then_inc(round_done, 1)

        def wide_dve(v, r, d):
            acc = agg2T[:, 1, :]
            v.memset(acc, 0.0).then_inc(added, 1)

            def add(i, half):
                tiles = load_tiles(v, d, bass.ds(i * SLOTS + half * GROUP, GROUP))
                for q in range(2):
                    v.wait_ge(chunks_here, 4 * i + 2 * half + q + 1)
                    for j in range(q * QUAD, (q + 1) * QUAD):
                        v.wait_ge(added, i * SLOTS + half * GROUP + j + 1)
                        where = acc[:, bass.ds(tiles[j] * P, P)]
                        at = 7 * BANK + (j % QUAD) * P
                        v.tensor_tensor(where, where, PS[:, at:at + P], ALU.add).then_inc(added, 1)
        
            for half in range(2):
                one_hots(v, r, d, 0, half)
            with v.Fori(0, STEPS - 1) as i:
                for half in range(2):
                    add(i, half)
                    one_hots(v, r, d, i + 1, half)
            for half in range(2):
                add(STEPS - 1, half)
            v.wait_ge(added, CHUNKS + 1)
            dve_link(v.tensor_tensor(acc, acc, rdeg[:, :], ALU.mult))

        def bc(a, n):
            return a.unsqueeze(2).to_broadcast([P, a.shape[1], n])

        def norm_dve(v, n, relu):
            src = x if relu else h
            dve_link(v.tensor_reduce(st[:, 0, :], src[:, :, :], AX_X, ALU.add))
            dve_link(v.tensor_scalar(st[:, 0, :], st[:, 0, :], 1.0 / D, None, ALU.mult))
            dve_link(v.tensor_tensor(h[:, :, :], src[:, :, :], bc(st[:, 0, :], D), ALU.subtract))
            dve_link(v.tensor_tensor(scr, h[:, :, :], h[:, :, :], ALU.mult))
            v.tensor_reduce(st[:, 1, :], scr, AX_X, ALU.add).then_inc(var_ready, 1)
            v.wait_ge(std_ready, n + 1)
            dve_link(v.reciprocal(st[:, 3, :], st[:, 2, :]))
            if relu:
                v.scalar_tensor_tensor(h[:, :, :], h[:, :, :], 0.0, bc(st[:, 3, :], D), ALU.max, ALU.mult) \
                    .then_inc(h_ready, 1)
            else:
                dve_link(v.tensor_tensor(h[:, :, :], h[:, :, :], bc(st[:, 3, :], D), ALU.mult))

        def first_norm(p):
            halves = rdeg[:, :].rearrange("p (t f) -> p t f", t=TILES)

            def fold(src, out):
                w = D // 2
                while w > 1:
                    pool_link(p.tensor_tensor(halves[:, :, 0:w], src[:, :, 0:w], src[:, :, w:2 * w], ALU.add))
                    src, w = halves, w // 2
                return p.tensor_tensor(out, src[:, :, 0:1], src[:, :, 1:2], ALU.add)

            pool_link(fold(x, st[:, 0:1, :].rearrange("p a t -> p t a")))
            pool_link(p.tensor_scalar(st[:, 0, :], st[:, 0, :], 1.0 / D, None, ALU.mult))
            pool_link(p.tensor_tensor(h[:, :, :], x[:, :, :], bc(st[:, 0, :], D), ALU.subtract))
            pool_link(p.tensor_tensor(halves, h[:, :, :], h[:, :, :], ALU.mult))
            fold(halves, st[:, 1:2, :].rearrange("p a t -> p t a")).then_inc(var_ready, 1)
            p.wait_ge(rstd_ready, 1)
            pool_link(p.tensor_scalar(h[:, :, :], h[:, :, :], 0.0, None, ALU.max))
            p.tensor_tensor(h[:, :, :], h[:, :, :], bc(st[:, 3, :], D), ALU.mult).then_inc(h_ready, 1)

        def norm_act(a, n):
            a.wait_ge(var_ready, n + 1)
            a.activation(st[:, 2, :], st[:, 1, :], ACT.Sqrt, bias=eps[:, 0:1], scale=1.0 / D).then_inc(std_ready, 1)

        def transposes_pe(t, src_of, sem_):
            for k in range(TILES):
                last = t.transpose(PS[:, k * P:(k + 1) * P], src_of(k), ident)
            last.then_inc(sem_, 1)

        def node_major(t, pairs, sem_):
            for k in range(TILES):
                for n, (act_T, w) in enumerate(pairs):
                    last = t.matmul(PS[:, k * P:(k + 1) * P], act_T[:, k * P:(k + 1) * P], w,
                                    start=(n == 0), stop=(n == len(pairs) - 1))
            last.then_inc(sem_, 1)

        def wt(name, c=0, width=P):
            at = W_AT[name] + c
            return W[:, at:at + width]

        def agg_dve(v, r, dst, first, exact_one=True):
            v.wait_ge(round_done, r + 1)
            if not first:
                v.tensor_tensor(dst, PS[:, 0:NP_], rdeg[:, :], ALU.mult).then_inc(agg_ready, 1)
                return
            deg = PS[:, DEG_COL:DEG_COL + TILES]
            if exact_one:
                v.tensor_scalar(st[:, 4, :], deg, 1.0, None, ALU.max).then_inc(deg_read, 1)
            else:
                v.tensor_scalar(st[:, 4, :], deg, 1e-12, None, ALU.add).then_inc(deg_read, 1)
            v.wait_ge(deg_read, first)
            dve_link(v.reciprocal(st[:, 5, :], st[:, 4, :]))
            v.tensor_tensor(h[:, :, :], ident.unsqueeze(1).to_broadcast([P, TILES, P]), bc(st[:, 5, :], P),
                            ALU.mult).then_inc(diag_ready, 1)
            v.wait_ge(sums_copied, first)
            if first == 1:
                v.wait_ge(rdeg_kept, 1)
                v.tensor_tensor(dst, dst, rdeg[:, :], ALU.mult).then_inc(agg_ready, 1)
            else:
                v.wait_ge(rdeg_summed, first)
                v.tensor_tensor(dst, dst, PS[:, 0:NP_], ALU.mult).then_inc(agg_ready, 1)

        def sums_act(a, dst, first):
            a.wait_ge(deg_read, first)
            a.copy(dst, PS[:, 0:NP_]).then_inc(sums_copied, 1)
            if first == 1:
                a.wait_ge(rdeg_summed, 1)
                a.copy(rdeg[:, :], PS[:, 0:NP_]).then_inc(rdeg_kept, 1)

        def rdeg_pe(t, n):
            t.wait_ge(diag_ready, n)
            t.wait_ge(sums_copied, n)
            hf = h[:, :, :].rearrange("p t f -> p (t f)")
            for a0 in range(0, NP_, BANK):
                a1 = min(a0 + BANK, NP_)
                last = t.matmul(PS[:, a0:a1], ones, hf[:, a0:a1], start=True, stop=True)
            last.then_inc(rdeg_summed, 1)

        def lin_pe(t, bank, terms, sem_=None):
            for ob in range(2):
                o = PS[:, (bank + ob) * BANK:(bank + ob) * BANK + BLK]
                for n, (name, c, rhs) in enumerate(terms):
                    last = t.matmul(o, wt(name, c * H1 + ob * P), rhs, start=(n == 0), stop=(n == len(terms) - 1))
            if sem_ is not None:
                last.then_inc(sem_, 1)

        def elu_act(a, n, X, bname):
            a.wait_ge(lin_ready, n)
            for ob in range(2):
                last = a.activation(blk[:, X, 0, ob, :], PS[:, (2 * X + ob) * BANK:(2 * X + ob) * BANK + BLK], ACT.Exp,
                                    bias=bcol[:, BCOL[bname] + ob:BCOL[bname] + ob + 1])
            last.then_inc(exp_ready, 1)

        def elu_dve(v, n, X, bname, dest, res=None):
            v.wait_ge(exp_ready, n)
            e, o = blk[:, X, 0, :, :], blk[:, X, 1, :, :]
            for ob in range(2):
                last = v.tensor_scalar(o[:, ob, :], PS[:, (2 * X + ob) * BANK:(2 * X + ob) * BANK + BLK],
                                bcol_m1[:, BCOL[bname] + ob:BCOL[bname] + ob + 1], -1.0, ALU.add, ALU.max)
            last.then_inc(clipped, 1)
            v.wait_ge(clipped, n)
            if res is None:
                v.scalar_tensor_tensor(dest, e, 1.0, o, ALU.min, ALU.add).then_inc(act_done, 1)
                return
            v.scalar_tensor_tensor(e, e, 1.0, o, ALU.min, ALU.add).then_inc(elu_done, 1)
            v.wait_ge(elu_done, res[1])
            for ob in range(2):
                at = (4 + 2 * X + ob) * BANK
                c = BCOL[res[0]] + ob
                last = v.scalar_tensor_tensor(dest[:, ob, :], PS[:, at:at + BLK], bcol[:, c:c + 1], e[:, ob, :],
                                              ALU.add, ALU.add)
            last.then_inc(act_done, 1)

        PAIRS = NBLK // 2

        def cols(i, X):
            return bass.ds(i * (2 * BLK) + X * BLK, BLK)

        def sage1_pe(t):
            with t.Fori(0, PAIRS) as i:
                for X in range(2):
                    t.wait_ge(act_done, 2 * i + 1 + X)
                    lin_pe(t, 2 * X, [("l1", 0, aggT[:, cols(i, X)]), ("r1", 0, hT[:, cols(i, X)])], lin_ready)

        def chain_pe(t):
            with t.Fori(0, PAIRS) as i:
                for X in range(2):
                    c = cols(i, X)
                    t.wait_ge(act_done, 10 + 6 * i - 1 + X)
                    lin_pe(t, 4 + 2 * X, [("res1", 0, hT[:, c])])
                    lin_pe(t, 2 * X, [("l2", k, agg2T[:, k, c]) for k in range(2)]
                           + [("r2", k, h1T[:, k, c]) for k in range(2)], lin_ready)
                for X in range(2):
                    t.wait_ge(act_done, 10 + 6 * i + 1 + X)
                    lin_pe(t, 2 * X, [("fc1", k, blk[:, X, 1, k, :]) for k in range(2)], lin_ready)
                for X in range(2):
                    t.wait_ge(act_done, 10 + 6 * i + 3 + X)
                    lin_pe(t, 4 + 2 * X, [("res2", 0, hT[:, cols(i, X)])])
                    lin_pe(t, 2 * X, [("fc2", k, blk[:, X, 1, k, :]) for k in range(2)], lin_ready)

        def sage1_act(a):
            with a.Fori(0, PAIRS) as i:
                for X in range(2):
                    elu_act(a, 2 * i + 1 + X, X, "b_l1")

        def chain_act(a):
            with a.Fori(0, PAIRS) as i:
                for n, name in enumerate(("b_l2", "fc1", "fc2")):
                    for X in range(2):
                        elu_act(a, 8 + 6 * i + 2 * n + X + 1, X, name)

        def sage1_dve(v):
            with v.Fori(0, PAIRS) as i:
                for X in range(2):
                    elu_dve(v, 2 * i + 1 + X, X, "b_l1", h1T[:, :, cols(i, X)])

        def chain_dve(v):
            with v.Fori(0, PAIRS) as i:
                for X in range(2):
                    elu_dve(v, 8 + 6 * i + X + 1, X, "b_l2", blk[:, X, 1, :, :], ("res1", 4 * i + X + 1))
                for X in range(2):
                    elu_dve(v, 8 + 6 * i + 2 + X + 1, X, "fc1", blk[:, X, 1, :, :])
                for X in range(2):
                    elu_dve(v, 8 + 6 * i + 4 + X + 1, X, "fc2", agg2T[:, :, cols(i, X)], ("res2", 4 * i + 2 + X + 1))

        def top_act(a, r, d):
            def indices(i, half, spills=None):
                c = bass.ds(i * SLOTS + half * GROUP, GROUP)
                a.wait_ge(used[half], base(r) + i)
                if spills is not None:
                    a.wait_ge(spilled[half], spills)
                a.copy(idxbuf[:, half, :], idx[:, d, c]).then_inc(idx_ready, 1)

            def step(i, more):
                for half in range(2):
                    a.wait_ge(sT_summed, 2 * (STEPS * d + i) + half + 1)
                    c = bass.ds(i * SLOTS + half * GROUP, GROUP)
                    a.copy(sE[0][:, c, :], G[:, half * GROUP:(half + 1) * GROUP, D:])
                    at = (4 + 2 * half) * BANK
                    a.copy(sT[0:SPLIT * HEADS, half * GROUP:(half + 1) * GROUP, :],
                           PS[0:SPLIT * HEADS, at:at + GROUP * P].rearrange("p (j e) -> p j e", j=GROUP)) \
                        .then_inc(sT_ready, 1)
                    if more:
                        indices(i + 1, half, 16 * (STEPS * d + i + 1))

            for half in range(2):
                indices(0, half)
            a.wait_ge(table["att1"], 32)
            with a.Fori(0, STEPS - 1) as i:
                step(i, True)
            step(STEPS - 1, False)

        def late_top_act(a, r, d):
            def bring(i, half):
                n = 2 * i + half
                a.wait_ge(scores_here, n + 1)
                a.wait_ge(sT_summed, 2 * STEPS * d + n - 1)
                a.copy(score_buf[:, half, :, :], sE[d][:, bass.ds(i * SLOTS + half * GROUP, GROUP), :]) \
                    .then_inc(scores_brought, 1)

            def take(i, half):
                a.wait_ge(sT_summed, 2 * (STEPS * d + i) + half + 1)
                bank = PS[0:SPLIT * HEADS, (4 + 2 * half) * BANK:(5 + 2 * half) * BANK].bitcast(BF16)
                a.copy(sT[0:SPLIT * HEADS, half * GROUP:(half + 1) * GROUP, :],
                       bank.rearrange("p (j e) -> p j e", j=GROUP)).then_inc(sT_ready, 1)

            bring(0, 0)
            with a.Fori(0, STEPS - 1) as i:
                bring(i, 1)
                take(i, 0)
                bring(i + 1, 0)
                take(i, 1)
            bring(STEPS - 1, 1)
            take(STEPS - 1, 0)
            take(STEPS - 1, 1)

        def top_pe(t, r, d):
            def turn(i, half):
                at = (4 + 2 * half) * BANK
                if d == 1:
                    t.wait_ge(scores_brought, 2 * i + half + 1)
                    bank = PS[0:SPLIT * HEADS, at:at + BANK].bitcast(BF16)
                for j in range(GROUP):
                    s = half * GROUP + j
                    if d == 0:
                        t.wait_ge(landed[s], 16 * (base(r) + i + 1))
                        last = t.transpose(PS[0:SPLIT * HEADS, at + j * P:at + (j + 1) * P], G[:, s, D:], ident)
                    else:
                        last = t.transpose(bank[:, j * P:(j + 1) * P], score_buf[:, half, j, :], ident_b[:, :])
                last.then_inc(sT_summed, 1)

            def mask(i, half):
                n = 2 * (STEPS * d + i) + half
                t.wait_ge(oh_ready, 2 * (base(r) + i) + half + 1)
                t.wait_ge(sT_ready, n + 1)
                for j in range(GROUP):
                    s = half * GROUP + j
                    bank = (j % 4) * BANK
                    t.wait_ge(reduced, n * GROUP + j + 1)
                    t.matmul(PS[:, bank:bank + BANK], OHb[:, s, :],
                             big_id[:, :].unsqueeze(1).to_broadcast([P, HEADS, P]), start=True, stop=False,
                             skip_group_check=True)
                    for hd in range(HEADS):
                        last = t.matmul(PS[:, bank + hd * P:bank + (hd + 1) * P], pick[:, hd, :], sT[:, s, :],
                                        start=False, stop=True, skip_group_check=True)
                    last.then_inc(masked_ready, 1)
                t.nop().then_inc(used[half], 1)

            if d == 0:
                with t.Fori(0, STEPS) as i:
                    for half in range(2):
                        turn(i, half)
                        mask(i, half)
            else:
                turn(0, 0)
                with t.Fori(0, STEPS - 1) as i:
                    turn(i, 1)
                    mask(i, 0)
                    turn(i + 1, 0)
                    mask(i, 1)
                turn(STEPS - 1, 1)
                mask(STEPS - 1, 0)
                mask(STEPS - 1, 1)
            for half in range(2):
                t.wait_ge(used[half], base(r + 1))
            t.drain().then_inc(round_done, 1)

        def top_dve(v, r, d):
            def others(i, half):
                v.wait_ge(used[half], base(r) + i)
                c = bass.ds(i * SLOTS + half * GROUP, GROUP)
                v.tensor_tensor(OHb[:, half * GROUP:(half + 1) * GROUP, :],
                                iota[:, 0:P].unsqueeze(1).to_broadcast([P, GROUP, P]),
                                key[:, d, c].unsqueeze(2).to_broadcast([P, GROUP, P]), ALU.not_equal) \
                    .then_inc(oh_ready, 1)

            def reduce(i, half, chunks):
                for j in chunks:
                    v.wait_ge(masked_ready, (2 * (STEPS * d + i) + half) * GROUP + j + 1)
                    bank = (j % 4) * BANK
                    v.tensor_reduce(cmax[:, :, bass.ds(i * SLOTS + half * GROUP + j, 1)].rearrange("p h k -> p (h k)"),
                                    PS[:, bank:bank + BANK].rearrange("p (h e) -> p h e", h=HEADS), AX_X, ALU.max) \
                        .then_inc(reduced, 1)

            first, second = range(0, GROUP // 2), range(GROUP // 2, GROUP)
            others(0, 0)
            with v.Fori(0, STEPS - 1) as i:
                for half in range(2):
                    reduce(i, half, first)
                    others(i + half, 1 - half)
                    reduce(i, half, second)
            reduce(STEPS - 1, 0, first)
            others(STEPS - 1, 1)
            reduce(STEPS - 1, 0, second)
            reduce(STEPS - 1, 1, range(GROUP))

        def guard_dve(v, d):
            ct = chunk_tile[:, d, :]
            v.memset(reset[:, 0, 0:1], 0.0)
            v.memset(reset[:, 1, CHUNKS - 1:CHUNKS], 0.0)
            v.tensor_tensor(reset[:, 0, 1:CHUNKS], ct[:, 1:CHUNKS], ct[:, 0:CHUNKS - 1], ALU.not_equal)
            dve_link(v.tensor_tensor(reset[:, 1, 0:CHUNKS - 1], ct[:, 1:CHUNKS], ct[:, 0:CHUNKS - 1], ALU.not_equal))
            dve_link(v.tensor_scalar(reset, reset, NEG_BIG, None, ALU.mult))
            for hd in range(HEADS):
                v.tensor_tensor_scan(mr[:, hd, :], reset[:, 0, :], cmax[:, hd, :], NEG_BIG, ALU.add, ALU.max)
                last = v.tensor_tensor_scan(mr[:, HEADS + hd, ::-1], reset[:, 1, ::-1], cmax[:, hd, ::-1], NEG_BIG,
                                            ALU.add, ALU.max)
            dve_link(last)
            dve_link(v.tensor_tensor(cmax, mr[:, 0:HEADS, :], mr[:, HEADS:, :], ALU.max))
            v.wait_ge(recv_summed, d + 1)
            recv = PS[:, 0:4 * BANK].rearrange("p (h k) -> p h k", h=HEADS)[:, :, 0:CHUNKS]
            v.tensor_copy(mr[:, HEADS:, :], recv)
            dve_link(v.tensor_tensor(mr[:, 0:HEADS, :], recv, cmax, ALU.add))
            v.scalar_tensor_tensor(mr[:, 0:HEADS, :], mr[:, 0:HEADS, :], 0.2, mr[:, 0:HEADS, :], ALU.mult, ALU.max) \
                .then_inc(mr_ready, 1)
            v.tensor_tensor(sender, sE[d][:, :, 0:HEADS].rearrange("p k h -> p h k"),
                            sE[d][:, :, HEADS:2 * HEADS].rearrange("p k h -> p h k"), ALU.add).then_inc(mr_ready, 1)
            v.wait_ge(mr_ready, 2 * d + 2)
            dve_link(v.tensor_tensor(sender, sender, sE[d][:, :, 2 * HEADS:].rearrange("p k h -> p h k"), ALU.add))
            for k in range(SPLIT):
                dve_link(v.tensor_copy(mrb[:, k, :, :], mr))
                if k < SPLIT - 1:
                    dve_link(v.tensor_tensor(mr, mr, mrb[:, k, :, :], ALU.subtract))
            v.nop().then_inc(mrb_ready, 1)

            n0 = GROUPS * d

            def one_hot(i, b):
                n = n0 + LAP * i + b
                v.wait_ge(turned, n + 1)
                c = bass.ds((i * LAP + b) * GROUP, GROUP)
                v.tensor_tensor(eq[:, b % LAP, :, :], iota[:, 0:P].unsqueeze(1).to_broadcast([P, GROUP, P]),
                                key[:, d, c].unsqueeze(2).to_broadcast([P, GROUP, P]), ALU.is_equal) \
                    .then_inc(oh_again, 1)

            def take(i, b):
                n = n0 + LAP * i + b
                v.wait_ge(er_summed, LAP + n + 1)
                c = bass.ds((i * LAP + b) * GROUP, GROUP)
                at = (4 + b % 2) * BANK
                v.tensor_reduce(er[:, :, c].rearrange("p q k -> p k q"),
                                PS[:, at:at + 24 * GROUP].rearrange("p (k s q) -> p k q s", s=SPLIT, q=8), AX_X,
                                ALU.add).then_inc(er_ready, 1)

            for b in range(AHEAD_OH):
                one_hot(0, b)
            with v.Fori(0, LAPS - 1) as i:
                for b in range(LAP):
                    one_hot(i, b + AHEAD_OH)
                    take(i, b)
            for b in range(LAP):
                if b + AHEAD_OH < LAP:
                    one_hot(LAPS - 1, b + AHEAD_OH)
                take(LAPS - 1, b)
            v.wait_ge(er_ready, 2 + GROUPS * (d + 1))
            dve_link(v.tensor_tensor(ex, sender, er[:, HEADS:, :], ALU.add))
            dve_link(v.scalar_tensor_tensor(ex, ex, 0.2, ex, ALU.mult, ALU.max))
            dve_link(v.tensor_tensor(ex, ex, er[:, 0:HEADS, :], ALU.subtract))
            v.tensor_scalar(ex, ex, 0.0, None, ALU.min).then_inc(arg_ready, 1)

        def guard_pe(t, d):
            t.wait_ge(reduced, 4 + CHUNKS * (d + 1))
            for hd in range(HEADS):
                last = t.matmul(PS[:, hd * BANK:hd * BANK + CHUNKS], rT[:, d, hd, :], tile_sel[:, d, :],
                                start=True, stop=True)
            last.then_inc(recv_summed, 1)
            t.wait_ge(mrb_ready, d + 1)
            n0 = GROUPS * d

            def turn(i, b):
                n = n0 + LAP * i + b
                t.wait_ge(oh_again, n + 1)
                t.wait_ge(ohT_ready, n + 1)
                bank = PS[:, (b % LAP) * BANK:(b % LAP + 1) * BANK].bitcast(BF16)
                for j in range(GROUP):
                    last = t.transpose(bank[:, j * P:(j + 1) * P], eq[:, b % LAP, j, :], ident_b[:, :])
                last.then_inc(turned, 1)

            def take(i, b):
                n = n0 + LAP * i + b
                t.wait_ge(ohT_ready, LAP + n + 1)
                t.wait_ge(er_ready, n + 1)
                for j in range(GROUP):
                    at = (4 + b % 2) * BANK + 24 * j
                    k = bass.ds((i * LAP + b) * GROUP + j, 1)
                    last = t.matmul(PS[:, at:at + 24].rearrange("p (s q) -> p s q", s=SPLIT), ohT[:, b, j, :],
                                    mrb[:, :, :, k].rearrange("p s q k -> p s (q k)"), start=True, stop=True)
                last.then_inc(er_summed, 1)

            for b in range(AHEAD_T):
                turn(0, b)
            with t.Fori(0, LAPS - 1) as i:
                for b in range(LAP):
                    turn(i, b + AHEAD_T)
                    take(i, b)
            for b in range(LAP):
                if b + AHEAD_T < LAP:
                    turn(LAPS - 1, b + AHEAD_T)
                take(LAPS - 1, b)

        def guard_act(a, d):
            for half in range(2):
                a.wait_ge(spilled[half], 16 * STEPS)
            with a.Fori(0, LAPS) as i:
                for b in range(LAP):
                    n = GROUPS * d + LAP * i + b
                    a.wait_ge(turned, LAP + n + 1)
                    a.wait_ge(er_summed, n + 1)
                    bank = PS[:, b * BANK:(b + 1) * BANK].bitcast(BF16)
                    a.copy(ohT[:, b, :, :], bank.rearrange("p (j e) -> p j e", j=GROUP)).then_inc(ohT_ready, 1)
            a.wait_ge(arg_ready, d + 1)
            a.activation(ex, ex, ACT.Exp).then_inc(ex_ready, 1)


        def spill_sp(sp, r, d):
            with sp.Fori(0, STEPS) as i:
                for half in range(2):
                    for j in range(GROUP):
                        sp.wait_ge(landed[half * GROUP + j], 16 * (base(r) + i + 1))
                    c = bass.ds((i * SLOTS + half * GROUP) * D, GROUP * D)
                    sp.dma_start(spill[d][:, c].rearrange("p (j f) -> p j f", j=GROUP),
                                 G[:, half * GROUP:(half + 1) * GROUP, 0:D]).then_inc(spilled[half], 16)
            for half in range(2):
                sp.wait_ge(spilled[half], 16 * STEPS)

        def ahead_pool(p, r, d):
            p.wait_ge(self_summed, 1)

            def gather(i, b, first=False):
                if not first:
                    p.wait_ge(spilled1[b], 16 * i)
                c = bass.ds((i * RING1 + b) * GROUP, GROUP)
                p.tensor_copy(idxbuf1[:, b, :], idx[:, d, c]).then_inc(idx_copied, 1)
                p.wait_ge(idx_copied, i * RING1 + b + 1)
                p.sem_inc(gathers_begun)
                for j in range(GROUP):
                    p.indirect_dma_start(out=ring1[:, b, j, :], out_offset=None, in_=T_att[d][:, :],
                                         in_offset=bass.IndirectOffsetOnAxis(ap=idxbuf1[:, b, j:j + 1], axis=0)) \
                        .then_inc(landed1[b], 16)

            def send(i, b):
                p.wait_ge(landed1[b], 16 * GROUP * (i + 1))
                g = i * RING1 + b
                p.tensor_copy(sE[d][:, bass.ds(g * GROUP, GROUP), :], ring1[:, b, :, D:]).then_inc(scores_here, 1)
                p.wait_ge(scores_here, g + 1)
                p.sem_inc(spills_begun)
                p.dma_start(spill[d][:, bass.ds(g * (GROUP * D), GROUP * D)].rearrange("p (j f) -> p j f", j=GROUP),
                            ring1[:, b, :, 0:D]).then_inc(spilled1[b], 16)

            turns, odd = GROUPS // RING1, GROUPS % RING1
            assert odd == 1
            for b in range(RING1):
                gather(0, b, True)
                if b:
                    send(0, b - 1)
            with p.Fori(1, turns) as i:
                for b in range(RING1):
                    gather(i, b)
                    send(i if b else i - 1, (b - 1) % RING1)
            gather(turns, 0)
            send(turns - 1, RING1 - 1)
            send(turns, 0)
            for b in range(RING1):
                p.wait_ge(spilled1[b], 16 * (turns + (b < odd)))

        def back_sp(sp, d):
            if d == 1:
                for b in range(RING1):
                    sp.wait_ge(spilled1[b], 16 * (GROUPS // RING1 + (b < GROUPS % RING1)))
            sp.wait_ge(ex_ready, d + 1)
            with sp.Fori(0, LAPS) as i:
                for b in range(RING2):
                    sp.wait_ge(weighed, GROUPS * d + RING2 * i + b + 1)
                    c = bass.ds((i * RING2 + b) * (GROUP * D), GROUP * D)
                    sp.dma_start(ring2[:, b, :, :].rearrange("p j f -> p (j f)"), spill[d][:, c]) \
                        .then_inc(back[b], 16)

        def weighted_dve(v, d):
            v.wait_ge(ex_ready, d + 1)
            rest = ex
            for k in range(SPLIT):
                dve_link(v.tensor_copy(exb[:, k, :, :], rest))
                if k < SPLIT - 1:
                    dve_link(v.tensor_tensor(ex_rest, rest, exb[:, k, :, :], ALU.subtract))
                    rest = ex_rest
            v.nop().then_inc(exb_ready, 1)
            with v.Fori(0, LAPS) as i:
                for b in range(RING2):
                    half = b % 2
                    n = GROUPS * d + RING2 * i + b
                    v.wait_ge(weighed, n + RING2 - 1)
                    c = bass.ds((i * RING2 + b) * GROUP, GROUP)
                    v.tensor_tensor(OH[:, half * GROUP:(half + 1) * GROUP, :],
                                    iota[:, 0:P].unsqueeze(1).to_broadcast([P, GROUP, P]),
                                    key[:, d, c].unsqueeze(2).to_broadcast([P, GROUP, P]), ALU.is_equal) \
                        .then_inc(oh_third, 1)
                    v.wait_ge(back[b], 16 * (LAPS * d + i + 1))
                    g = ring2[:, b, :, :].rearrange("p j (h f) -> p j h f", h=HEADS)
                    v.tensor_tensor(g, g, ex[:, :, c].rearrange("p h k -> p k h").unsqueeze(3)
                                    .to_broadcast([P, GROUP, HEADS, HD]), ALU.mult).then_inc(scaled_ready, 1)

        def weighted_act(a, d):
            with a.Fori(0, LAPS) as i:
                for b in range(RING2):
                    a.wait_ge(oh_third, GROUPS * d + RING2 * i + b + 1)
                    half = b % 2
                    c = bass.ds((i * RING2 + b) * GROUP, GROUP)
                    a.copy(exs[:, half, :, :].rearrange("p j (s h) -> p s h j", s=SPLIT), exb[:, :, :, c])
                    a.copy(OHw[:, half, :, :], OH[:, half * GROUP:(half + 1) * GROUP, :]).then_inc(oh_cast, 1)

        def weighted_pe(t, d):
            clear_psum(t)
            with t.Fori(0, LAPS) as i:
                for b in range(RING2):
                    c = bass.ds((i * RING2 + b) * GROUP, GROUP)
                    tiles = load_tiles(t, d, c)
                    n = GROUPS * d + RING2 * i + b
                    t.wait_ge(scaled_ready, n + 1)
                    for j in range(GROUP):
                        s = (b % 2) * GROUP + j
                        add_to(t, PS[:, bass.ds(tiles[j] * P, P)], OH[:, s, :], ring2[:, b, j, :])
                    t.wait_ge(oh_cast, n + 1)
                    for j in range(GROUP):
                        at = bass.ds(tiles[j] * (SPLIT * HEADS) + DEG_COL, SPLIT * HEADS)
                        last = add_to(t, PS[:, at], OHw[:, b % 2, j, :], exs[:, b % 2, j, :])
                    last.then_inc(weighed, 1)
            t.wait_ge(weighed, RING2 + 2 * STEPS * (d + 1))
            t.drain().then_inc(weighted_done, 1)

        def weighted_out_dve(v, d):
            v.wait_ge(weighted_done, d + 1)
            n = TILES * HEADS
            den = rden[:, 0, :]
            dve_link(v.tensor_reduce(den.rearrange("p (t h) -> p t h", h=HEADS), PS[:, DEG_COL:DEG_COL + SPLIT * n]
                                     .rearrange("p (t s h) -> p t h s", s=SPLIT, h=HEADS), AX_X, ALU.add))
            dve_link(v.tensor_scalar(den, den, 1e-8, None, ALU.add))
            dve_link(v.reciprocal(rden[:, 1, :], den))
            hv = h[:, :, :].rearrange("p t (h f) -> p (t h) f", h=HEADS)
            dve_link(v.tensor_tensor(hv, PS[:, 0:NP_].rearrange("p (n f) -> p n f", f=HD),
                                     rden[:, 1, :].unsqueeze(2).to_broadcast([P, n, HD]), ALU.mult))
            dve_link(v.tensor_tensor(comb, comb, h[:, :, :], ALU.add))
            v.nop().then_inc(den_ready, 1)

        def table_rows(name):
            return T[name].rearrange("(t p) f -> p t f", p=P)

        @block.sync
        def _(sp):
            sp.dma_start(e_i[:, :, :], edges.rearrange("k (p j) -> p k j", p=EP)).then_inc(loaded_edges, 16)
            sp.dma_start(cst[:, :], consts).then_inc(loaded_consts, 16)
            sp.wait_ge(x_cleared, 1)
            with sp.Fori(0, TILES - 1) as i:
                sp.dma_start(x[:, bass.ds(i, 1), :].rearrange("p t f -> p (t f)"), x_in[bass.ds(i * P, P), :]) \
                    .then_inc(loaded_x, 16)
            sp.dma_start(x[0:TAIL, TILES - 1, :], x_in[(TILES - 1) * P:N_NODES, :]).then_inc(loaded_x, 16)
            sp.dma_start(W[:, :], weights).then_inc(loaded_w, 16)
            sp.dma_start(bcol[:, :], bias_cols).then_inc(loaded_b, 16)
            sp.dma_start(brow[:, :, :], bias_rows.unsqueeze(0).to_broadcast([P, ROWS, D])).then_inc(loaded_b, 16)
            sp.dma_start(attn_sb[:, :], attn).then_inc(loaded_b, 16)
            sp.wait_ge(h_ready, 1)
            sp.dma_start(table_rows("h0"), h[:, :, :]).then_inc(table["h0"], 16)
            sp.wait_ge(h_ready, 2)
            sp.dma_start(table_rows("h1"), h[:, :, :]).then_inc(table["h1"], 16)
            sp.wait_ge(h1_ready, 1)
            sp.dma_start(table_rows("g")[:, :, 0:D], h[:, :, :]).then_inc(table["g"], 16)
            sp.wait_ge(h1_ready, 2)
            sp.dma_start(table_rows("g")[:, :, D:], h1N).then_inc(table["g"], 16)
            sp.wait_ge(h_ready, 3)
            sp.dma_start(table_rows("h2"), h[:, :, :]).then_inc(table["h2"], 16)
            sp.wait_ge(proj_ready, 1)
            sp.wait_ge(parts_ready, 1)
            for d in range(2):
                rows = T_att[d].rearrange("(t p) f -> p t f", p=P)
                sp.dma_start(rows[:, :, 0:D], h[:, :, :]).then_inc(table[f"att{d}"], 16)
                sp.dma_start(rows[:, :, D:], parts[:, d, :, :]).then_inc(table[f"att{d}"], 16)
            spill_sp(sp, 4, 0)
            for d in range(2):
                back_sp(sp, d)
            sp.wait_ge(x_final, 1)
            sp.dma_start(out[0:(TILES - 1) * P, :].rearrange("(t p) f -> p t f", p=P), x[:, 0:TILES - 1, :]) \
                .then_inc(stored, 16)
            sp.dma_start(out[(TILES - 1) * P:N_NODES, :], x[0:TAIL, TILES - 1, :]).then_inc(stored, 16)
            sp.wait_ge(stored, 32)

        @block.gpsimd
        def _(p):
            p.memset(x[:, TILES - 1, :], 0.0).then_inc(x_cleared, 1)
            p.memset(zeros[:, :], 0.0)
            p.memset(sT[:, :, :], 0.0)
            p.memset(eps[:, :], 1e-5).then_inc(zeros_ready, 1)
            p.wait_ge(loaded_x, 16 * TILES)
            first_norm(p)
            for r, name in enumerate(("h0", "h1", "g", "h2")):
                p.wait_ge(table[name], 32 if name == "g" else 16)
                round_pool(p, r, T[name], wide if name == "g" else narrow)
            p.wait_ge(table["att0"], 32)
            round_pool(p, 4, T_att[0], [G[:, s, :] for s in range(SLOTS)])
            p.wait_ge(table["att1"], 32)
            ahead_pool(p, 5, 1)

        @block.vector
        def _(v):
            v.wait_ge(zeros_ready, 1)
            v.wait_ge(loaded_edges, 16)
            v.wait_ge(loaded_consts, 16)
            dve_link(v.tensor_copy(iota_h[:, :], iota))
            dve_link(v.tensor_copy(ident_b[:, :], ident))
            dve_link(v.tensor_scalar(big_id[:, :], ident, NEG_BIG, None, ALU.mult))
            dve_link(v.tensor_copy(pick[:, :, :], cst[:, C_PICK:C_ALL].rearrange("p (h m) -> p h m", h=HEADS)))

            def invert(k):
                if k == 5:
                    v.wait_ge(std_ready, 1)
                    v.reciprocal(st[:, 3, :], st[:, 2, :]).then_inc(rstd_ready, 1)

            place_dve(v, 0, invert)
            v.nop().then_inc(placed, 1)
            permute_dve(v)
            v.wait_ge(sorted_ready, 1)
            v.wait_ge(loaded_b, 48)
            dve_link(v.tensor_scalar(bcol_m1[:, :], bcol[:, :], -1.0, None, ALU.add))
            dve_link(v.tensor_tensor(rowsum[:, :], brow[:, ROW["L2_self"], :], brow[:, ROW["L2_nei"], :], ALU.add))

            def row(a):
                return a.unsqueeze(1).to_broadcast([P, TILES, D])

            ps3 = PS[:, 0:NP_].rearrange("p (t f) -> p t f", t=TILES)
            for half in range(2):
                one_hots(v, 0, 0, 0, half, True)

            def between(k):
                for half in range(2):
                    one_hots(v, 0, 0, k, half)

            place_dve(v, 1, between)
            round_dve(v, 0, 0, BEHIND[0])
            agg_dve(v, 0, aggT, 1, True)
            v.wait_ge(square_ready, 1)
            dve_link(v.tensor_reduce(st[:, 6, :], h[:, :, :], AX_X, ALU.add))
            v.nop().then_inc(sumsq_ready, 1)
            v.wait_ge(len_ready, 1)
            dve_link(v.tensor_scalar(st[:, 7, :], st[:, 7, :], 1e-12, None, ALU.max))
            dve_link(v.reciprocal(st[:, 6, :], st[:, 7, :]))
            dve_link(v.tensor_tensor(h[:, :, :], ps3, bc(st[:, 6, :], D), ALU.mult))
            dve_link(v.tensor_tensor(x[:, :, :], x[:, :, :], h[:, :, :], ALU.add))
            norm_dve(v, 1, True)
            v.wait_ge(hT_ready, 2)
            round_dve(v, 1, 0)
            agg_dve(v, 1, aggT, 0)
            v.sem_inc(act_done, 2)
            sage1_dve(v)
            v.wait_ge(h1_ready, 2)
            wide_dve(v, 2, 0)
            agg_dve(v, 2, agg2T[:, 0, :], 0)
            chain_dve(v)
            v.wait_ge(fc3_summed, 1)
            v.tensor_tensor(h[:, :, :], ps3, row(brow[:, ROW["fc3"], :]), ALU.add).then_inc(z_ready, 1)
            v.wait_ge(log_ready, 1)
            dve_link(v.scalar_tensor_tensor(h[:, :, :], h[:, :, :], 0.0, scr, ALU.max, ALU.add))
            dve_link(v.tensor_tensor(x[:, :, :], x[:, :, :], h[:, :, :], ALU.add))
            norm_dve(v, 2, True)
            v.wait_ge(hT_ready, 3)
            round_dve(v, 3, 1)
            agg_dve(v, 3, aggT, 2, False)
            v.wait_ge(out2_summed, 1)
            dve_link(v.tensor_tensor(h[:, :, :], ps3, row(rowsum[:, :]), ALU.add))
            dve_link(v.scalar_tensor_tensor(x[:, :, :], h[:, :, :], 0.0, x[:, :, :], ALU.max, ALU.add))
            norm_dve(v, 3, True)
            v.wait_ge(hT_ready, 4)
            v.wait_ge(score_summed, 1)
            dve_link(v.tensor_copy(score[:, :, :], PS[:, 7 * BANK:7 * BANK + TILES * SC]
                                   .rearrange("p (t c) -> p t c", t=TILES)))
            for d in range(2):
                rest = score[:, :, 8 * d:8 * d + HEADS]
                left = rden[:, 0, :].rearrange("p (t h) -> p t h", h=HEADS)
                ph = part_h[:, :].rearrange("p (t h) -> p t h", h=HEADS)
                for k in range(SPLIT):
                    part = parts[:, d, :, k * HEADS:(k + 1) * HEADS]
                    dve_link(v.tensor_copy(ph, rest))
                    dve_link(v.tensor_copy(part, ph))
                    if k < SPLIT - 1:
                        dve_link(v.tensor_tensor(left, rest, part, ALU.subtract))
                        rest = left
            v.nop().then_inc(parts_ready, 1)
            v.wait_ge(proj_summed, 1)
            v.tensor_copy(h[:, :, :], ps3).then_inc(proj_ready, 1)
            v.wait_ge(self_summed, 1)
            dve_link(v.tensor_tensor(comb, ps3, row(brow[:, ROW["L3_bias"], :]), ALU.add))
            v.nop().then_inc(self_ready, 1)
            v.wait_ge(rT_summed, 1)
            v.tensor_copy(rT[:, :, :, :],
                          PS[0:TILES, 0:2 * HEADS * P].rearrange("p (d h e) -> p d h e", d=2, h=HEADS)) \
                .then_inc(rT_ready, 1)
            v.sem_inc(reduced, 4)
            v.sem_inc(er_ready, 2)
            for d in range(2):
                top_dve(v, 4 + d, d)
                v.wait_ge(round_done, 5 + d)
                guard_dve(v, d)
                weighted_dve(v, d)
                weighted_out_dve(v, d)
            dve_link(v.tensor_copy(h[:, :, :], comb))
            norm_dve(v, 4, False)
            dve_link(v.tensor_tensor(h[:, :, :], h[:, :, :], row(brow[:, ROW["gamma"], :]), ALU.mult))
            dve_link(v.tensor_tensor(h[:, :, :], h[:, :, :], row(brow[:, ROW["beta"], :]), ALU.add))
            v.tensor_tensor(x[:, :, :], x[:, :, :], h[:, :, :], ALU.add).then_inc(x_final, 1)

        @block.tensor
        def _(t):
            t.wait_ge(loaded_consts, 16)
            t.wait_ge(zeros_ready, 1)
            t.wait_ge(loaded_w, 16)
            t.wait_ge(loaded_b, 48)
            t.matmul(PS[:, 7 * BANK:7 * BANK + SC], wt("L3_WT"), attn_sb[:, :], start=True, stop=True) \
                .then_inc(wx_summed, 1)

            def h_tile(k):
                return h[:, k, :]

            t.wait_ge(wx_ready, 1)
            place_pe(t, 0)
            permute_pe(t)
            t.sem_inc(perm_used, 2)
            t.wait_ge(sorted_ready, 1)
            t.wait_ge(h_ready, 1)
            transposes_pe(t, h_tile, hT_summed)
            t.wait_ge(hT_ready, 1)
            round_pe(t, 0, 0, True)
            rdeg_pe(t, 1)
            t.wait_ge(agg_ready, 1)
            node_major(t, [(hT, wt("L0_lin")), (aggT, wt("L0_agg"))], out0_summed)
            t.wait_ge(h_ready, 2)
            transposes_pe(t, h_tile, hT_summed)
            t.wait_ge(hT_ready, 2)
            round_pe(t, 1, 0, False)
            t.wait_ge(agg_ready, 2)
            sage1_pe(t)
            for k in range(2):
                t.wait_ge(act_done, 10)
                if k:
                    t.wait_ge(h1_ready, k)
                transposes_pe(t, lambda n: h1T[:, k, n * P:(n + 1) * P], h1_transposed)
            t.wait_ge(h1_ready, 2)
            wide_pe(t, 2, 0)
            t.wait_ge(agg_ready, 3)
            chain_pe(t)
            t.wait_ge(act_done, 10 + 6 * PAIRS)
            node_major(t, [(agg2T[:, 0, :], wt("fc3", 0)), (agg2T[:, 1, :], wt("fc3", D))], fc3_summed)
            t.wait_ge(h_ready, 3)
            transposes_pe(t, h_tile, hT_summed)
            t.wait_ge(hT_ready, 3)
            t.wait_ge(sorted_ready, 2)
            round_pe(t, 3, 1, True)
            rdeg_pe(t, 2)
            t.wait_ge(agg_ready, 4)
            node_major(t, [(hT, wt("L2_self")), (aggT, wt("L2_nei"))], out2_summed)
            t.wait_ge(h_ready, 4)
            transposes_pe(t, h_tile, hT_summed)
            t.wait_ge(hT_ready, 4)
            t.wait_ge(wx_ready, 1)
            for k in range(TILES):
                last = t.matmul(PS[:, 7 * BANK + k * SC:7 * BANK + (k + 1) * SC], hT[:, k * P:(k + 1) * P], Wx[:, :],
                                start=True, stop=True)
            last.then_inc(score_summed, 1)
            node_major(t, [(hT, wt("L3_W"))], proj_summed)
            t.wait_ge(proj_ready, 1)
            node_major(t, [(hT, wt("L3_self"))], self_summed)
            t.wait_ge(self_ready, 1)
            for d in range(2):
                for hd in range(HEADS):
                    at = (d * HEADS + hd) * P
                    last = t.transpose(PS[0:TILES, at:at + P], score[:, :, 8 * d + HEADS + hd], ident)
            last.then_inc(rT_summed, 1)
            t.wait_ge(rT_ready, 1)
            t.sem_inc(turned, LAP)
            t.sem_inc(er_summed, LAP)
            t.sem_inc(weighed, RING2)
            for d in range(2):
                top_pe(t, 4 + d, d)
                guard_pe(t, d)
                t.wait_ge(exb_ready, d + 1)
                weighted_pe(t, d)
                t.wait_ge(den_ready, d + 1)

        @block.scalar
        def _(a):
            def copy_hT(n):
                a.wait_ge(hT_summed, n)
                a.copy(hT[:, :], PS[:, 0:NP_]).then_inc(hT_ready, 1)

            a.wait_ge(wx_summed, 1)
            a.copy(Wx[:, :], PS[:, 7 * BANK:7 * BANK + SC]).then_inc(wx_ready, 1)
            norm_act(a, 0)
            a.wait_ge(placed, 1)
            permute_act(a)
            a.wait_ge(sorted_ready, 1)
            round_act(a, 0, 0, lambda: copy_hT(1))
            sums_act(a, aggT, 1)
            a.wait_ge(out0_summed, 1)
            a.activation(h[:, :, :], PS[:, 0:NP_].rearrange("p (t f) -> p t f", t=TILES), ACT.Square) \
                .then_inc(square_ready, 1)
            a.wait_ge(sumsq_ready, 1)
            a.activation(st[:, 7, :], st[:, 6, :], ACT.Sqrt).then_inc(len_ready, 1)
            norm_act(a, 1)
            copy_hT(2)
            round_act(a, 1, 0)
            sage1_act(a)
            for k in range(2):
                a.wait_ge(h1_transposed, k + 1)
                a.copy(h[:, :, :] if k == 0 else h1N, PS[:, 0:NP_].rearrange("p (t f) -> p t f", t=TILES)) \
                    .then_inc(h1_ready, 1)
            round_act(a, 2, 0)
            chain_act(a)
            a.wait_ge(z_ready, 1)
            act_link(a.activation(scr, h[:, :, :], ACT.Abs))
            act_link(a.activation(scr, scr, ACT.Exp, scale=-1.0))
            a.activation(scr, scr, ACT.Ln, bias=1.0).then_inc(log_ready, 1)
            norm_act(a, 2)
            copy_hT(3)
            a.wait_ge(sorted_ready, 2)
            round_act(a, 3, 1)
            sums_act(a, aggT, 2)
            norm_act(a, 3)
            copy_hT(4)
            a.wait_ge(rT_ready, 1)
            a.sem_inc(ohT_ready, LAP)
            for d in range(2):
                (late_top_act if d else top_act)(a, 4 + d, d)
                guard_act(a, d)
                weighted_act(a, d)
            norm_act(a, 4)


def pack_consts():
    c = np.zeros((P, C_ALL), np.float32)
    c[:, C_ID:C_ID + P] = np.eye(P)
    c[:, C_TRI:C_TRI + P] = np.triu(np.ones((P, P)), 1)
    c[:, C_TRII:C_TRII + P] = np.triu(np.ones((P, P)), 0)
    c[:, C_IOTA:C_IOTA + CHUNKS] = np.arange(CHUNKS)
    c[:, C_ONE:C_ONE + P] = 1.0
    c[:TILES - 1, C_MASK] = -1.0
    for part in range(SPLIT):
        for hd in range(HEADS):
            c[part * HEADS + hd, C_PICK + hd * P:C_PICK + (hd + 1) * P] = 1.0
    return c


def pack_weights(g):
    def tr(w):
        wt = np.asarray(w).T
        return [wt[k:k + P] for k in range(0, wt.shape[0], P)]

    blocks = {"L0_lin": tr(g("L0_gnn_W_lin")), "L0_agg": tr(g("L0_gnn_W_agg")), "l1": tr(g("L1_gnn_W_l1")),
              "r1": tr(g("L1_gnn_W_r1")), "l2": tr(g("L1_gnn_W_l2")), "r2": tr(g("L1_gnn_W_r2")),
              "res1": tr(g("L1_gnn_res1_W")), "res2": tr(g("L1_gnn_res2_W")), "fc1": tr(g("L1_gnn_fc1_W")),
              "fc2": tr(g("L1_gnn_fc2_W")), "fc3": tr(g("L1_gnn_fc3_W")), "L2_self": tr(g("L2_gnn_W_self")),
              "L2_nei": tr(g("L2_gnn_W_nei")), "L3_W": [g("L3_gnn_W")], "L3_self": [g("L3_gnn_W_self")],
              "L3_WT": [g("L3_gnn_W").T]}
    return np.concatenate([b for n, _ in _W for b in blocks[n]], axis=1)


def pack_bias_cols(g):
    names = {"b_l1": "b_l1", "b_l2": "b_l2", "res1": "res1_b", "res2": "res2_b", "fc1": "fc1_b", "fc2": "fc2_b"}
    c = np.zeros((P, B_ALL), np.float32)
    for n, at in BCOL.items():
        c[:, at:at + 2] = g("L1_gnn_" + names[n]).reshape(2, P).T
    return c


def pack_attn(g):
    c = np.zeros((P, SC), np.float32)
    for d, name in enumerate(("L3_gnn_a_in", "L3_gnn_a_out")):
        for role in range(2):
            for hd in range(HEADS):
                c[hd * HD:(hd + 1) * HD, d * 8 + role * HEADS + hd] = g(name)[hd, role * HD:(role + 1) * HD]
    return c


def kernel(**inp):
    import concourse.bacc as bacc
    from concourse.bass_utils import run_bass_kernel_spmd

    def g(name):
        return np.asarray(inp[name])

    nc = bacc.Bacc("TRN2", target_bir_lowering=False, num_devices=1)
    rows = ["L1_gnn_fc3_b", "L2_gnn_b_self", "L2_gnn_b_nei", "L3_gnn_bias", "L3_gnn_ln_gamma", "L3_gnn_ln_beta"]
    arrays = {"edges": np.stack([g("src"), g("dst")]), "x_in": g("x"), "consts": pack_consts(),
              "weights": pack_weights(g), "bias_cols": pack_bias_cols(g), "bias_rows": np.stack([g(n) for n in rows]),
              "attn": pack_attn(g)}
    ap = {n: nc.dram_tensor(n, a.shape, mybir.dt.from_np(a.dtype), kind="ExternalInput").ap()
          for n, a in arrays.items()}
    out = nc.dram_tensor("out", [N_NODES, D], F32, kind="ExternalOutput").ap()
    gnn_kernel(nc, *ap.values(), out)
    r = run_bass_kernel_spmd(nc, [arrays], core_ids=[0])
    return r.results[0]["out"]
```
